# Optimizing a Trainium2 kernel written in Bass

```python
import numpy as np
import jax
import jax.numpy as jnp

def _softmax(x, axis=-1):
    return jax.nn.softmax(x, axis=axis)

def _gelu(x):
    return jax.nn.gelu(x, approximate=True)

def _silu(x):
    return jax.nn.silu(x)

def _sigmoid(x):
    return jax.nn.sigmoid(x)

def _layernorm(x, axis=-1, eps=1e-05):
    m = jnp.mean(x, axis=axis, keepdims=True)
    v = jnp.var(x, axis=axis, keepdims=True)
    return (x - m) / jnp.sqrt(v + eps)

def _scatter_add(tgt, idx, src, axis=0):
    return tgt.at[idx].add(src)

def _segment_sum(src, seg, n):
    return jax.ops.segment_sum(src, seg, n)
kernel_name = 'mk_seq_preln_d2_jaxref_r8_a71fd4'

def setup_inputs(seed: int=0):
    np.random.seed(seed)
    _w = jnp.asarray

    def _L0_attn_setup():
        import jax, jax.numpy as jnp
        import numpy as np
        B, S, D = (16, 64, 256)
        NUM_HEADS, NUM_GROUPS = (16, 4)
        HEAD_DIM = D // NUM_HEADS
        MAX_SEQ_LEN, SHARED_SLOTS = (64, 32)
        EPS = 1e-06

        def _rope_tables(seq_positions):
            inv_freq = 1.0 / 10000.0 ** (jnp.arange(0, HEAD_DIM, 2, dtype=jnp.float32) / HEAD_DIM)
            freqs = jnp.outer(seq_positions.astype(jnp.float32), inv_freq)
            return (jnp.cos(freqs), jnp.sin(freqs))

        def _apply_rope(x, cos, sin):
            x1, x2 = jnp.split(x, 2, axis=-1)
            real = x1 * cos - x2 * sin
            imag = x1 * sin + x2 * cos
            return jnp.concatenate([real, imag], axis=-1).astype(x.dtype)

        def _rmsnorm(x, scale):
            x = x.astype(jnp.float32)
            ms = jnp.mean(jnp.square(x), axis=-1, keepdims=True)
            return x * jax.lax.rsqrt(ms + EPS) * scale
        key = jax.random.key(seed)
        ks = jax.random.split(key, 10)
        w = 0.02
        return {'x': jax.random.normal(ks[0], (B, S, D), dtype=jnp.float32), 'wq': jax.random.normal(ks[1], (D, D), dtype=jnp.float32) * w, 'bq': jnp.zeros((D,), dtype=jnp.float32), 'wk': jax.random.normal(ks[2], (D, NUM_GROUPS * HEAD_DIM), dtype=jnp.float32) * w, 'bk': jnp.zeros((NUM_GROUPS * HEAD_DIM,), dtype=jnp.float32), 'wv': jax.random.normal(ks[3], (D, NUM_GROUPS * HEAD_DIM), dtype=jnp.float32) * w, 'bv': jnp.zeros((NUM_GROUPS * HEAD_DIM,), dtype=jnp.float32), 'wo': jax.random.normal(ks[4], (D, D), dtype=jnp.float32) * w, 'bo': jnp.zeros((D,), dtype=jnp.float32), 'q_norm_scale': jnp.ones((HEAD_DIM,), dtype=jnp.float32), 'k_norm_scale': jnp.ones((HEAD_DIM,), dtype=jnp.float32)}
    _L0_attn_in = _L0_attn_setup()

    def _L0_ffn_setup():
        import jax, jax.numpy as jnp
        import numpy as np
        D = 256
        H = 176
        E = 8
        TOP_K = 2
        B, S = (4, 256)

        def _swiglu(x, Wg, Wu, Wd):
            return jax.nn.silu(x @ Wg) * (x @ Wu) @ Wd
        key = jax.random.key(seed)
        ks = jax.random.split(key, 10)
        sc = 0.02
        x = jax.random.normal(ks[0], (B, S, D), dtype=jnp.float32)
        Wg_s = jax.random.normal(ks[1], (D, H), dtype=jnp.float32) * sc
        Wu_s = jax.random.normal(ks[2], (D, H), dtype=jnp.float32) * sc
        Wd_s = jax.random.normal(ks[3], (H, D), dtype=jnp.float32) * sc
        Wg = jax.random.normal(ks[4], (E, D, H), dtype=jnp.float32) * sc
        Wu = jax.random.normal(ks[5], (E, D, H), dtype=jnp.float32) * sc
        Wd = jax.random.normal(ks[6], (E, H, D), dtype=jnp.float32) * sc
        Wr = jax.random.normal(ks[7], (D, E), dtype=jnp.float32) * sc
        br = jax.random.normal(ks[8], (E,), dtype=jnp.float32) * sc
        rb = jnp.zeros((E,), dtype=jnp.float32)
        return {'x': x, 'Wg_s': Wg_s, 'Wu_s': Wu_s, 'Wd_s': Wd_s, 'Wg': Wg, 'Wu': Wu, 'Wd': Wd, 'Wr': Wr, 'br': br, 'rb': rb}
    _L0_ffn_in = _L0_ffn_setup()

    def _L1_attn_setup():
        import jax, jax.numpy as jnp
        import numpy as np
        import math
        N_HEADS, D_MODEL, D_HEAD = (16, 256, 128)
        BATCH, SEQ = (4, 256)
        ROPE_THETA = 10000.0

        def _rope_cos_sin(seq_len, head_dim, dtype=jnp.float32):
            inv_freq = 1.0 / ROPE_THETA ** (jnp.arange(0, head_dim, 2, dtype=jnp.float32) / head_dim)
            m = jnp.arange(seq_len, dtype=jnp.float32)
            freqs = jnp.outer(m, inv_freq)
            return (jnp.cos(freqs).astype(dtype), jnp.sin(freqs).astype(dtype))

        def _apply_rope(x, cos, sin):
            x1 = x[..., 0::2]
            x2 = x[..., 1::2]
            cos = cos[None, :, None, :]
            sin = sin[None, :, None, :]
            r1 = x1 * cos - x2 * sin
            r2 = x1 * sin + x2 * cos
            out = jnp.stack([r1, r2], axis=-1)
            return out.reshape(x.shape)
        key = jax.random.key(seed)
        ks = jax.random.split(key, 9)
        std = 0.02
        return {'normalized_resid_pre': jax.random.normal(ks[0], (BATCH, SEQ, D_MODEL), jnp.float32), 'W_Q': jax.random.normal(ks[1], (N_HEADS, D_MODEL, D_HEAD), jnp.float32) * std, 'b_Q': jnp.zeros((N_HEADS, D_HEAD), jnp.float32), 'W_K': jax.random.normal(ks[2], (N_HEADS, D_MODEL, D_HEAD), jnp.float32) * std, 'b_K': jnp.zeros((N_HEADS, D_HEAD), jnp.float32), 'W_V': jax.random.normal(ks[3], (N_HEADS, D_MODEL, D_HEAD), jnp.float32) * std, 'b_V': jnp.zeros((N_HEADS, D_HEAD), jnp.float32), 'W_O': jax.random.normal(ks[4], (N_HEADS, D_HEAD, D_MODEL), jnp.float32) * std, 'b_O': jnp.zeros((D_MODEL,), jnp.float32)}
    _L1_attn_in = _L1_attn_setup()

    def _L1_ffn_setup():
        import jax, jax.numpy as jnp
        import numpy as np
        B, S, H = (4, 512, 256)
        E, I, TOP_K = (8, 128, 2)
        key = jax.random.key(seed)
        ks = jax.random.split(key, 6)
        sc = 0.02
        return {'x': jax.random.normal(ks[0], (B, S, H), dtype=jnp.float32), 'w_gate': jax.random.normal(ks[1], (H, E), dtype=jnp.float32) * sc, 'W1': jax.random.normal(ks[2], (E, H, I), dtype=jnp.float32) * sc, 'b1': jnp.zeros((E, I), dtype=jnp.float32), 'W2': jax.random.normal(ks[3], (E, I, H), dtype=jnp.float32) * sc, 'b2': jnp.zeros((E, H), dtype=jnp.float32)}
    _L1_ffn_in = _L1_ffn_setup()
    _d = {'L0_attn_x': _L0_attn_in['x'], 'L0_attn_wq': _L0_attn_in['wq'], 'L0_attn_bq': _L0_attn_in['bq'], 'L0_attn_wk': _L0_attn_in['wk'], 'L0_attn_bk': _L0_attn_in['bk'], 'L0_attn_wv': _L0_attn_in['wv'], 'L0_attn_bv': _L0_attn_in['bv'], 'L0_attn_wo': _L0_attn_in['wo'], 'L0_attn_bo': _L0_attn_in['bo'], 'L0_attn_q_norm_scale': _L0_attn_in['q_norm_scale'], 'L0_attn_k_norm_scale': _L0_attn_in['k_norm_scale'], 'L0_ffn_Wg_s': _L0_ffn_in['Wg_s'], 'L0_ffn_Wu_s': _L0_ffn_in['Wu_s'], 'L0_ffn_Wd_s': _L0_ffn_in['Wd_s'], 'L0_ffn_Wg': _L0_ffn_in['Wg'], 'L0_ffn_Wu': _L0_ffn_in['Wu'], 'L0_ffn_Wd': _L0_ffn_in['Wd'], 'L0_ffn_Wr': _L0_ffn_in['Wr'], 'L0_ffn_br': _L0_ffn_in['br'], 'L0_ffn_rb': _L0_ffn_in['rb'], 'L1_attn_W_Q': _L1_attn_in['W_Q'], 'L1_attn_b_Q': _L1_attn_in['b_Q'], 'L1_attn_W_K': _L1_attn_in['W_K'], 'L1_attn_b_K': _L1_attn_in['b_K'], 'L1_attn_W_V': _L1_attn_in['W_V'], 'L1_attn_b_V': _L1_attn_in['b_V'], 'L1_attn_W_O': _L1_attn_in['W_O'], 'L1_attn_b_O': _L1_attn_in['b_O'], 'L1_ffn_w_gate': _L1_ffn_in['w_gate'], 'L1_ffn_W1': _L1_ffn_in['W1'], 'L1_ffn_b1': _L1_ffn_in['b1'], 'L1_ffn_W2': _L1_ffn_in['W2'], 'L1_ffn_b2': _L1_ffn_in['b2']}
    _x0 = _d['L0_attn_x']
    _d['L0_attn_x'] = jax.random.normal(jax.random.fold_in(jax.random.key(seed), 1), (8, 512, 256), dtype=_x0.dtype)
    del _x0
    return _d

def reference(L0_attn_x, L0_attn_wq, L0_attn_bq, L0_attn_wk, L0_attn_bk, L0_attn_wv, L0_attn_bv, L0_attn_wo, L0_attn_bo, L0_attn_q_norm_scale, L0_attn_k_norm_scale, L0_ffn_Wg_s, L0_ffn_Wu_s, L0_ffn_Wd_s, L0_ffn_Wg, L0_ffn_Wu, L0_ffn_Wd, L0_ffn_Wr, L0_ffn_br, L0_ffn_rb, L1_attn_W_Q, L1_attn_b_Q, L1_attn_W_K, L1_attn_b_K, L1_attn_W_V, L1_attn_b_V, L1_attn_W_O, L1_attn_b_O, L1_ffn_w_gate, L1_ffn_W1, L1_ffn_b1, L1_ffn_W2, L1_ffn_b2):

    def _L0_attn_ref(x, wq, bq, wk, bk, wv, bv, wo, bo, q_norm_scale, k_norm_scale):
        import jax, jax.numpy as jnp
        import numpy as np
        B, S, D = (16, 64, 256)
        NUM_HEADS, NUM_GROUPS = (16, 4)
        HEAD_DIM = D // NUM_HEADS
        MAX_SEQ_LEN, SHARED_SLOTS = (64, 32)
        EPS = 1e-06

        def _rope_tables(seq_positions):
            inv_freq = 1.0 / 10000.0 ** (jnp.arange(0, HEAD_DIM, 2, dtype=jnp.float32) / HEAD_DIM)
            freqs = jnp.outer(seq_positions.astype(jnp.float32), inv_freq)
            return (jnp.cos(freqs), jnp.sin(freqs))

        def _apply_rope(x, cos, sin):
            x1, x2 = jnp.split(x, 2, axis=-1)
            real = x1 * cos - x2 * sin
            imag = x1 * sin + x2 * cos
            return jnp.concatenate([real, imag], axis=-1).astype(x.dtype)

        def _rmsnorm(x, scale):
            x = x.astype(jnp.float32)
            ms = jnp.mean(jnp.square(x), axis=-1, keepdims=True)
            return x * jax.lax.rsqrt(ms + EPS) * scale
        b, s, d = x.shape
        rep = NUM_HEADS // NUM_GROUPS
        head_scale = HEAD_DIM ** (-0.5)
        xh = x.astype(jnp.float16)
        q = (xh @ wq.astype(jnp.float16) + bq.astype(jnp.float16)).reshape(b, s, NUM_HEADS, HEAD_DIM)
        k = (xh @ wk.astype(jnp.float16) + bk.astype(jnp.float16)).reshape(b, s, NUM_GROUPS, HEAD_DIM)
        v = (xh @ wv.astype(jnp.float16) + bv.astype(jnp.float16)).reshape(b, s, NUM_GROUPS, HEAD_DIM)
        q = _rmsnorm(q, q_norm_scale)
        k = _rmsnorm(k, k_norm_scale)
        pos = jnp.arange(s)
        cos, sin = _rope_tables(pos)
        cos = cos[:, None, :]
        sin = sin[:, None, :]
        q = _apply_rope(q, cos, sin) * head_scale
        k = _apply_rope(k, cos, sin)
        q = q.astype(jnp.float16)
        k = k.astype(jnp.float16)
        v = v.astype(jnp.float16)
        qg = q.reshape(b, s, NUM_GROUPS, rep, HEAD_DIM)
        logits = jnp.einsum('btgrh,bsgh->bgrts', qg, k, preferred_element_type=jnp.float32) * head_scale
        causal = pos[:, None] >= pos[None, :]
        logits = jnp.where(causal[None, None, None, :, :], logits, jnp.finfo(jnp.float32).min)
        probs = jax.nn.softmax(logits, axis=-1).astype(jnp.float16)
        out = jnp.einsum('bgrts,bsgh->btgrh', probs, v)
        out = out.reshape(b, s, d)
        return out @ wo.astype(jnp.float16) + bo.astype(jnp.float16)

    def _L0_ffn_ref(x, Wg_s, Wu_s, Wd_s, Wg, Wu, Wd, Wr, br, rb):
        import jax, jax.numpy as jnp
        import numpy as np
        D = 256
        H = 176
        E = 8
        TOP_K = 2
        B, S = (4, 256)

        def _swiglu(x, Wg, Wu, Wd):
            return jax.nn.silu(x @ Wg) * (x @ Wu) @ Wd
        shared_out = _swiglu(x, Wg_s, Wu_s, Wd_s)
        logits = x @ Wr + br + rb
        probs = jax.nn.sigmoid(logits)
        top_v, top_i = jax.lax.top_k(probs, TOP_K)
        top_v = top_v / jnp.sum(top_v, axis=-1, keepdims=True)
        w = jnp.sum(top_v[..., None] * jax.nn.one_hot(top_i, E, dtype=x.dtype), axis=-2)
        routed_out = jnp.zeros_like(x)
        for e in range(E):
            routed_out = routed_out + _swiglu(x, Wg[e], Wu[e], Wd[e]) * w[..., e:e + 1]
        return shared_out + routed_out

    def _L1_attn_ref(normalized_resid_pre, W_Q, b_Q, W_K, b_K, W_V, b_V, W_O, b_O):
        import jax, jax.numpy as jnp
        import numpy as np
        import math
        N_HEADS, D_MODEL, D_HEAD = (16, 256, 128)
        BATCH, SEQ = (4, 256)
        ROPE_THETA = 10000.0

        def _rope_cos_sin(seq_len, head_dim, dtype=jnp.float32):
            inv_freq = 1.0 / ROPE_THETA ** (jnp.arange(0, head_dim, 2, dtype=jnp.float32) / head_dim)
            m = jnp.arange(seq_len, dtype=jnp.float32)
            freqs = jnp.outer(m, inv_freq)
            return (jnp.cos(freqs).astype(dtype), jnp.sin(freqs).astype(dtype))

        def _apply_rope(x, cos, sin):
            x1 = x[..., 0::2]
            x2 = x[..., 1::2]
            cos = cos[None, :, None, :]
            sin = sin[None, :, None, :]
            r1 = x1 * cos - x2 * sin
            r2 = x1 * sin + x2 * cos
            out = jnp.stack([r1, r2], axis=-1)
            return out.reshape(x.shape)
        x = normalized_resid_pre
        T = x.shape[1]
        d_head = W_Q.shape[-1]
        Q = jnp.einsum('btc,ncd->btnd', x, W_Q) + b_Q
        K = jnp.einsum('btc,ncd->btnd', x, W_K) + b_K
        V = jnp.einsum('btc,ncd->btnd', x, W_V) + b_V
        cos, sin = _rope_cos_sin(T, d_head, x.dtype)
        Q = _apply_rope(Q, cos, sin)
        K = _apply_rope(K, cos, sin)
        scores = jnp.einsum('bqnd,bknd->bnqk', Q, K) / math.sqrt(d_head)
        causal = jnp.tril(jnp.ones((T, T), dtype=bool))
        scores = jnp.where(causal[None, None], scores, -jnp.inf)
        probs = jax.nn.softmax(scores, axis=-1)
        z = jnp.einsum('bnqk,bknd->bqnd', probs, V)
        out = jnp.einsum('bqnd,ndm->bqm', z, W_O) + b_O
        return out

    def _L1_ffn_ref(x, w_gate, W1, b1, W2, b2):
        import jax, jax.numpy as jnp
        import numpy as np
        B, S, H = (4, 512, 256)
        E, I, TOP_K = (8, 128, 2)
        Bm, Sm, Hm = x.shape
        x_flat = x.reshape(-1, Hm)
        gate_logits = x_flat @ w_gate
        raw_weights = jax.nn.softmax(gate_logits, axis=-1)
        topk_w, topk_idx = jax.lax.top_k(raw_weights, TOP_K)
        topk_w = jax.nn.softmax(topk_w, axis=-1)
        combine = jnp.sum(jax.nn.one_hot(topk_idx, E, dtype=x.dtype) * topk_w[..., None], axis=1)
        out = jnp.zeros_like(x_flat)
        for e in range(E):
            h = jax.nn.gelu(x_flat @ W1[e] + b1[e], approximate=False)
            y = h @ W2[e] + b2[e]
            out = out + combine[:, e:e + 1] * y
        return out.reshape(Bm, Sm, Hm)
    x = L0_attn_x
    x = x + _L0_attn_ref(_layernorm(x, axis=-1), L0_attn_wq, L0_attn_bq, L0_attn_wk, L0_attn_bk, L0_attn_wv, L0_attn_bv, L0_attn_wo, L0_attn_bo, L0_attn_q_norm_scale, L0_attn_k_norm_scale)
    x = x + _L0_ffn_ref(_layernorm(x, axis=-1), L0_ffn_Wg_s, L0_ffn_Wu_s, L0_ffn_Wd_s, L0_ffn_Wg, L0_ffn_Wu, L0_ffn_Wd, L0_ffn_Wr, L0_ffn_br, L0_ffn_rb)
    x = x + _L1_attn_ref(_layernorm(x, axis=-1), L1_attn_W_Q, L1_attn_b_Q, L1_attn_W_K, L1_attn_b_K, L1_attn_W_V, L1_attn_b_V, L1_attn_W_O, L1_attn_b_O)
    x = x + _L1_ffn_ref(_layernorm(x, axis=-1), L1_ffn_w_gate, L1_ffn_W1, L1_ffn_b1, L1_ffn_W2, L1_ffn_b2)
    return x

_drawn_inputs = setup_inputs


def setup_inputs(seed=0):
    import zlib

    import numpy as np

    out = dict(_drawn_inputs(seed))
    spreads = {'L0_attn_bq': (0.0, 0.8),
     'L0_attn_bk': (0.0, 0.8),
     'L0_attn_bv': (0.0, 0.1),
     'L0_attn_bo': (0.0, 0.1),
     'L0_attn_q_norm_scale': (1.0, 0.6),
     'L0_attn_k_norm_scale': (1.0, 0.6),
     'L0_ffn_rb': (0.0, 0.8),
     'L1_attn_b_Q': (0.0, 0.8),
     'L1_attn_b_K': (0.0, 0.8),
     'L1_attn_b_V': (0.0, 0.1),
     'L1_attn_b_O': (0.0, 0.1),
     'L1_ffn_b1': (0.0, 0.8),
     'L1_ffn_b2': (0.0, 0.1)}
    factors = {'L0_attn_wq': 8.0,
     'L0_attn_wk': 8.0,
     'L0_attn_wv': 3.814,
     'L0_ffn_Wg_s': 3.49,
     'L0_ffn_Wu_s': 3.443,
     'L0_ffn_Wd_s': 3.465,
     'L0_ffn_Wg': 4.88,
     'L0_ffn_Wu': 4.606,
     'L0_ffn_Wd': 4.711,
     'L0_ffn_Wr': 5.574,
     'L0_ffn_br': 8.0,
     'L1_attn_W_Q': 8.0,
     'L1_attn_W_K': 8.0,
     'L1_ffn_W1': 3.144}
    for name, (base, spread) in spreads.items():
        noise = np.random.default_rng([zlib.crc32(name.encode()), seed]).standard_normal(out[name].shape)
        drawn = base * np.exp(spread * noise) if base else spread * noise
        out[name] = jnp.asarray(drawn.astype(out[name].dtype))
    for name, factor in factors.items():
        out[name] = (out[name] * factor).astype(out[name].dtype)
    return out
```

```python
from contextlib import ExitStack

import concourse.bass as bass
from concourse import mybir
from concourse.alu_op_type import AluOpType as ALU

F32 = mybir.dt.float32
F32R = mybir.dt.float32r
F16 = mybir.dt.float16
BF16 = mybir.dt.bfloat16
I32 = mybir.dt.int32
ACT = mybir.ActivationFunctionType
AX = mybir.AxisListType

P = 128
B, S, D = 8, 512, 256
NT = S // P
NC = D // P
LN_EPS = 1e-5
MASKED = -1e38
RSQRT_MAGIC = 1597463007.0


class Chain:

    def __init__(self, eng, sem):
        self.eng, self.sem, self.n = eng, sem, 0

    def step(self, ins):
        ins.then_inc(self.sem, 1)
        self.n += 1

    def done(self):
        self.eng.wait_ge(self.sem, self.n)

    def restart(self):
        self.done()
        self.eng.sem_clear(self.sem)
        self.n = 0


def rsqrt(dve, chain, y, x, half, sq):
    chain.step(dve.tensor_scalar(half, x, -0.5, None, ALU.mult))
    chain.step(dve.tensor_scalar(sq.bitcast(I32), x.bitcast(I32), 1, None, ALU.logical_shift_right))
    chain.done()
    chain.step(dve.tensor_scalar(y.bitcast(I32), sq.bitcast(I32), -1.0, RSQRT_MAGIC, ALU.mult, ALU.add))
    chain.done()
    for _ in range(4):
        chain.step(dve.tensor_tensor(sq, y, y, ALU.mult))
        chain.done()
        chain.step(dve.tensor_tensor(sq, sq, half, ALU.mult))
        chain.done()
        chain.step(dve.scalar_tensor_tensor(out=y, in0=sq, scalar=1.5, in1=y, op0=ALU.add, op1=ALU.mult))
        chain.done()


def layernorm_stats(dve, chain, x, ln):
    for t in range(NT):
        chain.step(dve.bn_stats(ln["stats"][:, t, :], x[:, t, :]))
    chain.done()
    for t in range(NT):
        chain.step(dve.bn_aggr(ln["mv"][:, t, :], ln["stats"][:, t, :]))
    chain.done()
    chain.step(dve.tensor_scalar(ln["var"][:, :], ln["mv"][:, :, 1], LN_EPS, None, ALU.add))
    chain.done()
    rsqrt(dve, chain, ln["rstd"][:, :], ln["var"][:, :], ln["half"][:, :], ln["sq"][:, :])


def layernorm_buffers(sb, tag):
    return {
        "stats": sb(f"{tag}_ln_stats", [P, NT, 6], F32),
        "mv": sb(f"{tag}_ln_mv", [P, NT, 2], F32),
        "var": sb(f"{tag}_ln_var", [P, NT], F32),
        "rstd": sb(f"{tag}_ln_rstd", [P, NT], F32),
        "half": sb(f"{tag}_ln_half", [P, NT], F32),
        "sq": sb(f"{tag}_ln_sq", [P, NT], F32),
    }


def token_tiles(x, b):
    return x[b, :, :].rearrange("(t p) d -> p t d", p=P)


def row_to_all(v):
    return v.rearrange("(o n) -> o n", o=1).partition_broadcast(P)


def make_identity(pool, chain, m):
    chain.step(pool.memset(m, 0.0))
    chain.done()
    chain.step(pool.affine_select(out=m, in_=m, compare_op=ALU.not_equal, fill=1.0, base=0,
                                  pattern=[[-1, P]], channel_multiplier=1))


def make_causal(pool, chain, m):
    chain.step(pool.memset(m, 0.0))
    chain.done()
    chain.step(pool.affine_select(out=m, in_=m, compare_op=ALU.is_ge, fill=MASKED, base=0,
                                  pattern=[[-1, P]], channel_multiplier=1))


HD0, H0, G0 = 16, 16, 4
REP0 = H0 // G0
QK0 = (H0 + G0) * HD0
QKV0 = (H0 + 2 * G0) * HD0
GW = 32
RMS_EPS = 1e-6
TRI = [P * (i + 1) for i in range(NT)]
P_AT = [sum(TRI[:i]) for i in range(NT + 1)]
T_AT = [sum(S - P * k for k in range(j)) for j in range(NT + 1)]


def attention0(nc, x, wq, bq, wk, bk, wv, bv, wo, bo, q_scale, k_scale, cos, sin, out):
    ctx = ExitStack()
    with ctx:
        def sb(name, shape, dt):
            return ctx.enter_context(nc.sbuf_tensor(f"a_{name}", shape, dt))

        def pb(name, shape, dt):
            return ctx.enter_context(nc.psum_tensor(f"a_{name}", shape, dt))

        def sem(name):
            return ctx.enter_context(nc.semaphore(f"a_{name}"))

        w_in = sb("w_in", [P, NC, QKV0], F32)
        wo_in = sb("wo_in", [P, NC, D], F32)
        w16 = sb("w16", [P, NC, QKV0], F16)
        wo16 = sb("wo16", [P, NC, D], F16)
        b_in = sb("b_in", [P, QKV0], F32)
        b16 = sb("b16", [P, QKV0], F16)
        bo_in = sb("bo_in", [P, D], F32)
        bo16 = sb("bo16", [P, D], F16)
        cs_in = sb("cs_in", [P, NT, HD0 // 2], F32)
        sn_in = sb("sn_in", [P, NT, HD0 // 2], F32)
        scales = sb("scales", [P, 2, HD0], F32)
        tab_c = sb("tab_c", [P, NT, 2, HD0], F32)
        tab_s = sb("tab_s", [P, NT, 2, HD0], F32)
        ident = sb("ident", [P, P], F16)
        ident_b = sb("ident_b", [P, P], BF16)
        causal = sb("causal", [P, P], BF16)
        x_in = sb("x_in", [P, NT, D], F32)
        x_res = sb("x_res", [P, NT, D], F32)
        x_out = sb("x_out", [P, NT, D], F32)
        xn = sb("xn", [P, NT, D], F16)
        ln = layernorm_buffers(sb, "x")
        xT = sb("xT", [P, NC, S], F16)
        qkv = sb("qkv", [P, NT, QKV0], F16)
        sq = sb("sq", [P, NT, QK0], F32)
        ra = sb("ra", [P, NT, QK0], F32)
        rb = sb("rb", [P, NT, QK0], F32)
        ms = sb("ms", [P, NT * (H0 + G0)], F32)
        rs = sb("rs", [P, NT * (H0 + G0)], F32)
        rs_half = sb("rs_half", [P, NT * (H0 + G0)], F32)
        rs_sq = sb("rs_sq", [P, NT * (H0 + G0)], F32)
        q_pad = sb("q_pad", [P, NT, REP0, G0, GW], F16)
        k_pad = sb("k_pad", [P, NT, G0, GW], F16)
        qT = sb("qT", [P, REP0, S], F16)
        kT = sb("kT", [P, G0, S], F16)
        nmax = sb("nmax", [P, 2, NT], F32)
        sums = sb("sums", [P, NT, H0], F32)
        rsum = sb("rsum", [P, NT, H0], F32)
        probs = sb("probs", [P, 2, P_AT[NT]], F16)
        pT = sb("pT", [P, 2, T_AT[NT]], F16)
        z16 = sb("z16", [P, NT, D], F16)
        zT = sb("zT", [P, NC, S], F16)

        ps_s = [pb(f"ps_s{i}", [P, S], F32) for i in range(4)]
        ps_t = [pb(f"ps_t{i}", [P, 2 * S], F16) for i in range(2)]
        ps_z = [pb(f"ps_z{i}", [P, 2, D], F32) for i in range(2)]
        ps_xT = ps_t
        ps_qkv = ps_s[0:2]
        ps_qT = ps_t
        ps_kT = ps_s[2][:, 0:S // 2].bitcast(F16)
        ps_zT = ps_t

        loaded = [sem(f"loaded{i}") for i in range(11)]
        setup_pool = sem("setup_pool")
        setup_dve = sem("setup_dve")
        consts_ready = sem("consts_ready")
        x_loaded = sem("x_loaded")
        x_taken = sem("x_taken")
        xn_ready = sem("xn_ready")
        xT_ps = sem("xT_ps")
        xT_ready = sem("xT_ready")
        qkv_ps = sem("qkv_ps")
        qkv_ready = sem("qkv_ready")
        sq_ready = sem("sq_ready")
        rot_ready = sem("rot_ready")
        qk_ready = sem("qk_ready")
        qkT_ps = sem("qkT_ps")
        qkT_ready = sem("qkT_ready")
        scores_ps = sem("scores_ps")
        max_ready = sem("max_ready")
        probs_ready = sem("probs_ready")
        pT_ps = sem("pT_ps")
        pT_ready = sem("pT_ready")
        z_ps = sem("z_ps")
        z_ready = sem("z_ready")
        zT_ps = sem("zT_ps")
        zT_ready = sem("zT_ready")
        y_ps = sem("y_ps")
        y_ready = sem("y_ready")
        stored = sem("stored")
        x_out_free = sem("x_out_free")
        dve_steps = sem("dve_steps")

        block = ctx.enter_context(nc.Block())

        @block.sync
        def _(sp):
            sp.dma_start(w_in[:, :, 0:D], wq.rearrange("(c p) n -> p c n", p=P)).then_inc(loaded[0], 16)
            sp.dma_start(w_in[:, :, D:QK0], wk.rearrange("(c p) n -> p c n", p=P)).then_inc(loaded[1], 16)
            sp.dma_start(w_in[:, :, QK0:QKV0], wv.rearrange("(c p) n -> p c n", p=P)).then_inc(loaded[2], 16)
            sp.dma_start(b_in[:, 0:D], row_to_all(bq)).then_inc(loaded[3], 16)
            sp.dma_start(b_in[:, D:QK0], row_to_all(bk)).then_inc(loaded[4], 16)
            sp.dma_start(b_in[:, QK0:QKV0], row_to_all(bv)).then_inc(loaded[5], 16)
            sp.dma_start(cs_in[:], cos.rearrange("(t p) n -> p t n", p=P)).then_inc(loaded[6], 16)
            sp.dma_start(sn_in[:], sin.rearrange("(t p) n -> p t n", p=P)).then_inc(loaded[7], 16)
            sp.dma_start(scales[:, 0, :], row_to_all(q_scale)).then_inc(loaded[8], 16)
            sp.dma_start(scales[:, 1, :], row_to_all(k_scale)).then_inc(loaded[8], 16)
            sp.dma_start(wo_in[:], wo.rearrange("(c p) n -> p c n", p=P)).then_inc(loaded[9], 16)
            sp.dma_start(bo_in[:], row_to_all(bo)).then_inc(loaded[10], 16)
            with sp.Fori(0, B) as b:
                sp.wait_ge(x_taken, b + 1)
                sp.dma_start(x_in[:], token_tiles(x, b)).then_inc(x_loaded, 16)

        @block.gpsimd
        def _(pool):
            chain = Chain(pool, setup_pool)
            make_identity(pool, chain, ident[:])
            make_identity(pool, chain, ident_b[:])
            make_causal(pool, chain, causal[:])
            pool.sem_inc(x_out_free, 1)
            with pool.Fori(0, B) as b:
                pool.wait_ge(y_ready, 2 * b + 2)
                pool.dma_start(token_tiles(out, b), x_out[:]).then_inc(stored, 16)
                pool.wait_ge(stored, 16 * (b + 1))
                pool.sem_inc(x_out_free, 1)

        @block.scalar
        def _(act):
            with act.Fori(0, B) as b:
                for c in range(NC):
                    act.wait_ge(xT_ps, NC * b + c + 1)
                    act.activation(xT[:, c, :], ps_xT[c][:, 0:S], ACT.Copy).then_inc(xT_ready, 1)
                for t in range(NT):
                    act.wait_ge(qkv_ready, NT * b + t + 1)
                    act.activation(sq[:, t, :], qkv[:, t, 0:QK0], ACT.Square).then_inc(sq_ready, 1)
                for r in range(REP0):
                    act.wait_ge(qkT_ps, 2 * b + 1)
                    act.activation(qT[:, r, :], ps_qT[r // 2][:, (r % 2) * S:(r % 2 + 1) * S],
                                   ACT.Copy).then_inc(qkT_ready, 1)
                act.wait_ge(qkT_ps, 2 * b + 2)
                for g in range(G0):
                    rows = slice(GW * g, GW * (g + 1))
                    act.activation(kT[rows, g, :], ps_kT[rows, :], ACT.Copy).then_inc(qkT_ready, 1)
                for h in range(H0):
                    for i in range(NT):
                        n = NT * h + i
                        act.wait_ge(max_ready, H0 * NT * b + n + 1)
                        if i == 0 and h >= 2:
                            act.wait_ge(pT_ps, 2 * H0 * b + 2 * (h - 1))
                        act.activation(probs[:, h % 2, P_AT[i]:P_AT[i + 1]], ps_s[i][:, 0:TRI[i]], ACT.Exp,
                                       bias=nmax[:, h % 2, i:i + 1],
                                       accum_out=sums[:, i, h:h + 1]).then_inc(probs_ready, 1)
                for c in range(NC):
                    act.wait_ge(zT_ps, NC * b + c + 1)
                    act.activation(zT[:, c, :], ps_zT[c][:, 0:S], ACT.Copy).then_inc(zT_ready, 1)

        @block.vector
        def _(dve):
            chain = Chain(dve, setup_dve)
            for i in (6, 7):
                dve.wait_ge(loaded[i], 16)
            dve.wait_ge(loaded[8], 32)
            half = HD0 // 2
            for j in range(2):
                by = float(HD0) ** -1 if j == 0 else 1.0
                lo = scales[:, j, 0:half].unsqueeze(1).to_broadcast([P, NT, half])
                hi = scales[:, j, half:HD0].unsqueeze(1).to_broadcast([P, NT, half])
                for dst, table, scale, sign in ((tab_c[:, :, j, 0:half], cs_in, lo, 1.0), (tab_c[:, :, j, half:HD0], cs_in, hi, 1.0),
                                                (tab_s[:, :, j, 0:half], sn_in, hi, -1.0), (tab_s[:, :, j, half:HD0], sn_in, lo, 1.0)):
                    chain.step(dve.scalar_tensor_tensor(out=dst, in0=table[:], scalar=sign * by, in1=scale,
                                                        op0=ALU.mult, op1=ALU.mult))
            for i in range(6):
                dve.wait_ge(loaded[i], 16)
            chain.step(dve.tensor_copy(w16[:], w_in[:]))
            chain.step(dve.tensor_copy(b16[:], b_in[:]))
            dve.wait_ge(loaded[9], 16)
            chain.step(dve.tensor_copy(wo16[:], wo_in[:]))
            dve.wait_ge(loaded[10], 16)
            chain.step(dve.tensor_copy(bo16[:], bo_in[:]))
            chain.step(dve.memset(q_pad[:].rearrange("p a b c d -> p (a b c d)"), 0.0))
            chain.step(dve.memset(k_pad[:].rearrange("p a b c -> p (a b c)"), 0.0))
            chain.step(dve.memset(kT[:].rearrange("p a b -> p (a b)"), 0.0))
            chain.done()
            dve.sem_inc(consts_ready, 1)
            dve.sem_inc(x_taken, 1)

            chain = Chain(dve, dve_steps)
            with dve.Fori(0, B) as b:
                dve.wait_ge(x_loaded, 16 * (b + 1))
                layernorm_stats(dve, chain, x_in, ln)
                for t in range(NT):
                    dve.tensor_scalar(xn[:, t, :], x_in[:, t, :], ln["mv"][:, t, 0:1], ln["rstd"][:, t:t + 1],
                                      ALU.subtract, ALU.mult).then_inc(xn_ready, 1)
                dve.tensor_tensor(x_res[:], x_in[:], bo16[:].unsqueeze(1).to_broadcast([P, NT, D]),
                                  ALU.add).then_inc(x_taken, 1)
                for t in range(NT):
                    dve.wait_ge(qkv_ps, NT * b + t + 1)
                    dve.tensor_tensor(qkv[:, t, :], ps_qkv[t % 2][:, 0:QKV0], b16[:], ALU.add).then_inc(qkv_ready, 1)
                dve.wait_ge(qkv_ready, NT * b + NT)
                for t in range(NT):
                    for j, (c0, nh) in enumerate(((0, H0), (D, G0))):
                        src = qkv[:, t, c0:c0 + nh * HD0].rearrange("p (h d) -> p h d", d=HD0)
                        a = ra[:, t, c0:c0 + nh * HD0].rearrange("p (h d) -> p h d", d=HD0)
                        r = rb[:, t, c0:c0 + nh * HD0].rearrange("p (h d) -> p h d", d=HD0)
                        chain.step(dve.tensor_tensor(a, src, tab_c[:, t, j, :].unsqueeze(1).to_broadcast([P, nh, HD0]), ALU.mult))
                        for to, frm in ((slice(0, half), slice(half, HD0)), (slice(half, HD0), slice(0, half))):
                            chain.step(dve.tensor_tensor(r[:, :, to], src[:, :, frm],
                                                         tab_s[:, t, j, to].unsqueeze(1).to_broadcast([P, nh, half]), ALU.mult))
                dve.wait_ge(sq_ready, NT * b + NT)
                chain.step(dve.tensor_reduce(ms[:], sq[:].rearrange("p t (h d) -> p (t h) d", d=HD0), AX.X, ALU.add))
                chain.done()
                chain.step(dve.tensor_tensor(ra[:], ra[:], rb[:], ALU.add))
                chain.step(dve.tensor_scalar(ms[:], ms[:], 1.0 / HD0, RMS_EPS, ALU.mult, ALU.add))
                chain.done()
                rsqrt(dve, chain, rs[:], ms[:], rs_half[:], rs_sq[:])
                for t in range(NT):
                    r4 = rs[:, t * (H0 + G0):(t + 1) * (H0 + G0)]
                    for g in range(G0):
                        h0 = g * REP0
                        dve.tensor_tensor(
                            q_pad[:, t, :, g, 0:HD0],
                            ra[:, t, h0 * HD0:(h0 + REP0) * HD0].rearrange("p (r d) -> p r d", d=HD0),
                            r4[:, h0:h0 + REP0].unsqueeze(2).to_broadcast([P, REP0, HD0]), ALU.mult).then_inc(qk_ready, 1)
                    dve.tensor_tensor(
                        k_pad[:, t, :, 0:HD0], ra[:, t, D:QK0].rearrange("p (g d) -> p g d", d=HD0),
                        r4[:, H0:H0 + G0].unsqueeze(2).to_broadcast([P, G0, HD0]), ALU.mult).then_inc(qk_ready, 1)

                def copy_pT(h):
                    for k, (j0, j1) in enumerate(((0, 2), (2, 4))):
                        dve.wait_ge(pT_ps, 2 * H0 * b + 2 * h + k + 1)
                        dve.tensor_copy(pT[:, h % 2, T_AT[j0]:T_AT[j1]],
                                        ps_t[k][:, 0:T_AT[j1] - T_AT[j0]]).then_inc(pT_ready, 1)

                for h in range(H0):
                    if h >= 1:
                        copy_pT(h - 1)
                    for i in range(NT):
                        dve.wait_ge(scores_ps, H0 * NT * b + NT * h + i + 1)
                        dve.tensor_reduce(nmax[:, h % 2, i:i + 1], ps_s[i][:, 0:TRI[i]], AX.X, ALU.max,
                                          negate=True).then_inc(max_ready, 1)
                copy_pT(H0 - 1)
                dve.wait_ge(probs_ready, H0 * NT * (b + 1))
                chain.step(dve.reciprocal(rsum[:], sums[:]))
                chain.done()
                dve.wait_ge(z_ps, b + 1)
                for t in range(NT):
                    dve.tensor_tensor(z16[:, t, :].rearrange("p (h d) -> p h d", d=HD0),
                                      ps_z[t // 2][:, t % 2, :].rearrange("p (h d) -> p h d", d=HD0),
                                      rsum[:, t, :].unsqueeze(2).to_broadcast([P, H0, HD0]), ALU.mult).then_inc(z_ready, 1)
                for u in range(2):
                    dve.wait_ge(y_ps, 2 * b + u + 1)
                    if u == 0:
                        dve.wait_ge(x_out_free, b + 1)
                    dve.tensor_tensor(x_out[:, 2 * u:2 * u + 2, :], ps_z[u][:], x_res[:, 2 * u:2 * u + 2, :],
                                      ALU.add).then_inc(y_ready, 1)
                chain.restart()

        @block.tensor
        def _(pe):
            pe.wait_ge(setup_pool, 6)
            pe.wait_ge(consts_ready, 1)
            with pe.Fori(0, B) as b:
                for c in range(NC):
                    for t in range(NT):
                        pe.wait_ge(xn_ready, NT * b + t + 1)
                        last = pe.transpose(ps_xT[c][:, t * P:(t + 1) * P],
                                            xn[:, t, c * P:(c + 1) * P], ident[:])
                    last.then_inc(xT_ps, 1)
                pe.wait_ge(xT_ready, NC * b + NC)
                for t in range(NT):
                    if t >= 2:
                        pe.wait_ge(qkv_ready, NT * b + t - 1)
                    for c in range(NC):
                        last = pe.matmul(ps_qkv[t % 2][:, 0:QKV0], xT[:, c, t * P:(t + 1) * P], w16[:, c, :],
                                         start=(c == 0), stop=(c == NC - 1))
                    last.then_inc(qkv_ps, 1)
                pe.wait_ge(qk_ready, NT * (G0 + 1) * (b + 1))
                for t in range(NT):
                    for r in range(REP0):
                        last = pe.transpose(ps_qT[r // 2][:, (r % 2) * S + t * P:(r % 2) * S + (t + 1) * P],
                                            q_pad[:, t, r, :, :].rearrange("p g d -> p (g d)"), ident[:])
                last.then_inc(qkT_ps, 1)
                for t in range(NT):
                    last = pe.transpose(ps_kT[:, t * P:(t + 1) * P],
                                        k_pad[:, t, :, :].rearrange("p g d -> p (g d)"), ident[:])
                last.then_inc(qkT_ps, 1)
                pe.wait_ge(qkT_ready, (REP0 + G0) * (b + 1))

                def scores(h):
                    g, r = h // REP0, h % REP0
                    for i in range(NT):
                        if h >= 1:
                            pe.wait_ge(probs_ready, H0 * NT * b + NT * (h - 1) + i + 1)
                        pe.matmul(ps_s[i][:, 0:TRI[i]], qT[:, r, i * P:(i + 1) * P], kT[:, g, 0:TRI[i]],
                                  start=True, stop=False)
                        pe.matmul(ps_s[i][:, i * P:TRI[i]], ident_b[:], causal[:],
                                  start=False, stop=True).then_inc(scores_ps, 1)

                def transposes(h):
                    pe.wait_ge(probs_ready, H0 * NT * b + NT * (h + 1))
                    if h >= 1:
                        pe.wait_ge(pT_ready, 2 * (H0 * b + h))
                    for k, (j0, j1) in enumerate(((0, 2), (2, 4))):
                        for j in range(j0, j1):
                            for i in range(j, NT):
                                at = T_AT[j] - T_AT[j0] + (i - j) * P
                                last = pe.transpose(ps_t[k][:, at:at + P],
                                                    probs[:, h % 2, P_AT[i] + j * P:P_AT[i] + (j + 1) * P], ident[:])
                        last.then_inc(pT_ps, 1)

                def values(h):
                    v0 = QK0 + (h // REP0) * HD0
                    pe.wait_ge(pT_ready, 2 * (H0 * b + h) + 2)
                    for i in range(NT):
                        for j in range(i + 1):
                            at = T_AT[j] + (i - j) * P
                            last = pe.matmul(ps_z[i // 2][:, i % 2, h * HD0:(h + 1) * HD0], pT[:, h % 2, at:at + P],
                                             qkv[:, j, v0:v0 + HD0], start=(j == 0), stop=(j == i))
                    if h == H0 - 1:
                        last.then_inc(z_ps, 1)

                scores(0)
                for h in range(H0):
                    transposes(h)
                    if h + 1 < H0:
                        scores(h + 1)
                    values(h)
                for c in range(NC):
                    for t in range(NT):
                        pe.wait_ge(z_ready, NT * b + t + 1)
                        last = pe.transpose(ps_zT[c][:, t * P:(t + 1) * P],
                                            z16[:, t, c * P:(c + 1) * P], ident[:])
                    last.then_inc(zT_ps, 1)
                pe.wait_ge(zT_ready, NC * b + NC)
                for t in range(NT):
                    for c in range(NC):
                        last = pe.matmul(ps_z[t // 2][:, t % 2, :], zT[:, c, t * P:(t + 1) * P], wo16[:, c, :],
                                         start=(c == 0), stop=(c == NC - 1))
                    if t % 2 == 1:
                        last.then_inc(y_ps, 1)

H1, HD1 = 16, 128
ROT = HD1 // 2
SCALE1 = float(HD1) ** -0.5
PASSES = ((0, 0), (0, 1), (1, 0))


def split_halves(parts, hi, lo):
    return (hi, lo)[parts]


def attention1(nc, x, wq, bq, wk, bk, wv, bv, wo, bo, cos, sin, out):
    ctx = ExitStack()
    with ctx:
        def sb(name, shape, dt, stack=ctx):
            return stack.enter_context(nc.sbuf_tensor(f"c_{name}", shape, dt))

        def pb(name, shape, dt):
            return ctx.enter_context(nc.psum_tensor(f"c_{name}", shape, dt))

        def sem(name):
            return ctx.enter_context(nc.semaphore(f"c_{name}"))

        DM = H1 * HD1
        w_hi = sb("w_hi", [P, 3, NC, DM], F32R)
        w_lo = sb("w_lo", [P, 3, NC, DM], F32R)
        w_parts = (w_hi, w_lo)
        wo_sb = sb("wo", [P, H1, D], F32)
        ident = sb("ident", [P, P], F32)
        ident_b = sb("ident_b", [P, P], BF16)
        causal = sb("causal", [P, P], BF16)
        cosT = sb("cosT", [P, S], F32)
        sinT = sb("sinT", [P, S], F32)
        bias = sb("bias", [P, 3, H1], F32)
        bo_sb = sb("bo", [P, D], F32)

        loaded = [sem(f"loaded{i}") for i in range(5)]
        setup_hi = sem("setup_hi")
        setup_lo = sem("setup_lo")
        setup_pool = sem("setup_pool")

        with ExitStack() as setup:
            w_in = sb("w_in", [P, 3, NC * DM], F32, setup)
            block = setup.enter_context(nc.Block())

            @block.sync
            def _(sp):
                for i, w in enumerate((wq, wk, wv)):
                    for c in range(NC):
                        sp.dma_start(w_in[:, i, c * DM:(c + 1) * DM], w[c * P:(c + 1) * P, :]).then_inc(loaded[i], 16)
                sp.dma_start(wo_sb[:], wo.rearrange("n d m -> d n m")).then_inc(loaded[3], 16)
                for i, v in enumerate((bq, bk, bv)):
                    sp.dma_start(bias[:, i, :], v).then_inc(loaded[4], 16)
                sp.dma_start(bo_sb[:], row_to_all(bo)).then_inc(loaded[4], 16)
                for k in range(2):
                    sp.dma_start(cosT[k * ROT:(k + 1) * ROT, :], cos).then_inc(loaded[4], 16)
                    sp.dma_start(sinT[k * ROT:(k + 1) * ROT, :], sin).then_inc(loaded[4], 16)
                sp.wait_ge(loaded[3], 16)

            @block.gpsimd
            def _(pool):
                chain = Chain(pool, setup_pool)
                make_identity(pool, chain, ident[:])
                make_identity(pool, chain, ident_b[:])
                make_causal(pool, chain, causal[:])
                chain.done()

            @block.scalar
            def _(act):
                for i in range(3):
                    act.wait_ge(loaded[i], 16 * NC)
                    act.activation(w_hi[:, i, :, :].rearrange("p c n -> p (c n)"), w_in[:, i, :],
                                   ACT.Copy).then_inc(setup_hi, 1)

            @block.vector
            def _(dve):
                for i in range(3):
                    dve.wait_ge(setup_hi, i + 1)
                    dve.tensor_tensor(w_lo[:, i, :, :].rearrange("p c n -> p (c n)"), w_in[:, i, :],
                                      w_hi[:, i, :, :].rearrange("p c n -> p (c n)").bitcast(F32),
                                      ALU.subtract).then_inc(setup_lo, 1)
                dve.wait_ge(loaded[4], 16 * 8)
                dve.tensor_scalar(bias[:, 0, :], bias[:, 0, :], SCALE1, None, ALU.mult).then_inc(setup_lo, 1)
                dve.tensor_scalar(sinT[0:ROT, :], sinT[0:ROT, :], 1.0, None, ALU.mult).then_inc(setup_lo, 1)
                dve.tensor_scalar(sinT[ROT:P, :], sinT[ROT:P, :], -1.0, None, ALU.mult).then_inc(setup_lo, 1)

        x_in = sb("x_in", [P, NT, D], F32)
        x_res = sb("x_res", [P, NT, D], F32)
        ln = layernorm_buffers(sb, "c")
        xT = [sb(f"xT{k}", [P, NC, S], F32R) for k in range(2)]
        raw = sb("raw", [P, 2, S], F32)
        turn = sb("turn", [P, 2, S], F32)
        cross = sb("cross", [P, 2, S], F32)
        qkT = [sb(f"qkT{k}", [P, 2, 2, S], F32R) for k in range(2)]
        v = [sb(f"v{k}", [P, 2, NT, 2 * HD1], F32R) for k in range(2)]
        probs = sb("probs", [P, 2, P_AT[NT]], F32)
        xn = probs[:, 0, 0:NT * D].rearrange("p (t d) -> p t d", d=D)
        pT = [sb(f"pT{k}", [P, T_AT[NT]], F32R) for k in range(2)]
        zT = [sb(f"zT{k}", [P, S], F32R) for k in range(2)]
        wo_parts = [sb(f"wo{k}", [P, 2, D], F32R) for k in range(2)]
        nmax = sb("nmax", [P, 2, NT], F32)
        sums = sb("sums", [P, 2, NT], F32)
        rsum = sb("rsum", [P, 2, NT], F32)

        ps_s = [pb(f"ps_s{i}", [P, S], F32) for i in range(2)]
        ps_t = [pb(f"ps_t{i}", [P, S], F32) for i in range(2)]
        ps_proj = pb("ps_proj", [P, S], F32)
        ps_z = pb("ps_z", [P, S], F32)
        ps_o = [pb(f"ps_o{i}", [P, 2, D], F32) for i in range(2)]
        ps_xT = ps_s

        x_loaded = sem("x_loaded")
        x_taken = sem("x_taken")
        xn_ready = sem("xn_ready")
        xT_ps = sem("xT_ps")
        xT_hi = sem("xT_hi")
        xT_lo = sem("xT_lo")
        qk_ps = sem("qk_ps")
        qk_raw = sem("qk_raw")
        qk_cos = sem("qk_cos")
        qk_turned = sem("qk_turned")
        qk_hi = sem("qk_hi")
        qk_lo = sem("qk_lo")
        v_ps = sem("v_ps")
        v_hi = sem("v_hi")
        v_lo = sem("v_lo")
        scores_ps = sem("scores_ps")
        max_ready = sem("max_ready")
        exp_ready = sem("exp_ready")
        probs_ready = sem("probs_ready")
        pT_ps = sem("pT_ps")
        pT_hi = sem("pT_hi")
        pT_lo = sem("pT_lo")
        z_ps = sem("z_ps")
        z_hi = sem("z_hi")
        z_lo = sem("z_lo")
        wo_hi = sem("wo_hi")
        wo_lo = sem("wo_lo")
        y_ps = sem("y_ps")
        y_ready = sem("y_ready")
        x_out_free = sem("x_out_free")
        stored = sem("stored")
        dve_steps = sem("dve_steps")

        block = ctx.enter_context(nc.Block())
        n_tiles = H1 * NT

        @block.sync
        def _(sp):
            with sp.Fori(0, B) as b:
                sp.wait_ge(x_taken, b + 1)
                sp.dma_start(x_in[:], token_tiles(x, b)).then_inc(x_loaded, 16)

        @block.gpsimd
        def _(pool):
            pool.sem_inc(x_out_free, 1)

            def rotate(b, h):
                for j in range(2):
                    n = 2 * H1 * b + 2 * h + j + 1
                    pool.wait_ge(qk_raw, n)
                    pool.tensor_tensor(turn[:, j, :], raw[:, j, :], cosT[:], ALU.mult).then_inc(qk_cos, 1)

            def low(b, h):
                for j in range(2):
                    n = 2 * H1 * b + 2 * h + j + 1
                    pool.wait_ge(qk_hi, n)
                    pool.tensor_tensor(qkT[1][:, h % 2, j, :], turn[:, j, :], qkT[0][:, h % 2, j, :].bitcast(F32),
                                       ALU.subtract).then_inc(qk_lo, 1)

            with pool.Fori(0, B) as b:
                rotate(b, 0)
                low(b, 0)
                for s in range(H1):
                    pool.wait_ge(wo_hi, H1 * b + s + 1)
                    pool.tensor_tensor(wo_parts[1][:, s % 2, :], wo_sb[:, s, :],
                                       wo_parts[0][:, s % 2, :].bitcast(F32), ALU.subtract).then_inc(wo_lo, 1)
                    if s + 1 < H1:
                        rotate(b, s + 1)
                        low(b, s + 1)
                pool.wait_ge(y_ready, 2 * b + 2)
                pool.dma_start(token_tiles(out, b), x_res[:]).then_inc(stored, 16)
                pool.wait_ge(stored, 16 * (b + 1))
                pool.sem_inc(x_out_free, 1)

        @block.scalar
        def _(act):
            def raw_head(b, h, j):
                act.wait_ge(qk_ps, 2 * H1 * b + 2 * h + j + 1)
                act.activation(raw[:, j, :], ps_proj[:], ACT.Identity, bias=bias[:, 1 - j, h:h + 1],
                               scale=SCALE1 if j == 1 else 1.0).then_inc(qk_raw, 1)

            def high_head(b, h, j):
                act.wait_ge(qk_turned, 2 * H1 * b + 2 * h + j + 1)
                act.activation(qkT[0][:, h % 2, j, :], turn[:, j, :], ACT.Copy).then_inc(qk_hi, 1)

            def high_v(b, part):
                act.wait_ge(v_ps, H1 * b + part + 1)
                t0 = 2 * (part % 2)
                act.activation(v[0][:, (part // 2) % 2, t0:t0 + 2, :], ps_proj[:].rearrange("p (t n) -> p t n", t=2),
                               ACT.Copy).then_inc(v_hi, 1)

            def exps(b, h, i):
                act.wait_ge(max_ready, n_tiles * b + NT * h + i + 1)
                act.activation(probs[:, h % 2, P_AT[i]:P_AT[i + 1]], ps_s[i % 2][:, 0:TRI[i]], ACT.Exp,
                               bias=nmax[:, h % 2, i:i + 1], accum_out=sums[:, h % 2, i:i + 1]).then_inc(exp_ready, 1)

            def high_pT(b, h, j):
                act.wait_ge(pT_ps, n_tiles * b + NT * h + j + 1)
                act.activation(pT[0][:, T_AT[j]:T_AT[j + 1]], ps_t[j % 2][:, 0:S - j * P], ACT.Copy).then_inc(pT_hi, 1)

            with act.Fori(0, B) as b:
                for c in range(NC):
                    act.wait_ge(xT_ps, NC * b + c + 1)
                    act.activation(xT[0][:, c, :], ps_xT[c][:], ACT.Copy).then_inc(xT_hi, 1)
                raw_head(b, 0, 0)
                high_head(b, 0, 0)
                raw_head(b, 0, 1)
                high_head(b, 0, 1)
                high_v(b, 0)
                for s in range(H1 + 1):
                    now, last, ahead = s < H1, s >= 1, s + 1 < H1
                    if last:
                        high_pT(b, s - 1, 0)
                    if now:
                        exps(b, s, 0)
                        act.activation(wo_parts[0][:, s % 2, :], wo_sb[:, s, :], ACT.Copy).then_inc(wo_hi, 1)
                    if last:
                        high_pT(b, s - 1, 1)
                    if now:
                        exps(b, s, 1)
                    if ahead:
                        raw_head(b, s + 1, 0)
                    if last:
                        high_pT(b, s - 1, 2)
                    if now:
                        exps(b, s, 2)
                    if ahead:
                        high_head(b, s + 1, 0)
                    if last:
                        high_pT(b, s - 1, 3)
                    if ahead:
                        raw_head(b, s + 1, 1)
                    if now:
                        exps(b, s, 3)
                    if last:
                        act.wait_ge(z_ps, H1 * b + s)
                        act.activation(zT[0][:], ps_z[:], ACT.Identity, bias=bias[:, 2, s - 1:s]).then_inc(z_hi, 1)
                    if ahead:
                        high_head(b, s + 1, 1)
                        high_v(b, s + 1)

        @block.vector
        def _(dve):
            chain = Chain(dve, dve_steps)
            dve.sem_inc(x_taken, 1)

            def cross_head(b, h, j):
                n = 2 * H1 * b + 2 * h + j + 1
                dve.wait_ge(qk_raw, n)
                for to, frm in ((slice(0, ROT), slice(ROT, P)), (slice(ROT, P), slice(0, ROT))):
                    chain.step(dve.tensor_tensor(cross[to, j, :], raw[frm, j, :], sinT[frm, :], ALU.mult))
                chain.done()
                dve.wait_ge(qk_cos, n)
                dve.tensor_tensor(turn[:, j, :], turn[:, j, :], cross[:, j, :], ALU.add).then_inc(qk_turned, 1)

            def low_v(b, part):
                dve.wait_ge(v_hi, H1 * b + part + 1)
                t0 = 2 * (part % 2)
                dve.tensor_tensor(v[1][:, (part // 2) % 2, t0:t0 + 2, :], ps_proj[:].rearrange("p (t n) -> p t n", t=2),
                                  v[0][:, (part // 2) % 2, t0:t0 + 2, :].bitcast(F32), ALU.subtract).then_inc(v_lo, 1)

            def maxima(b, h, i):
                dve.wait_ge(scores_ps, n_tiles * b + NT * h + i + 1)
                dve.tensor_reduce(nmax[:, h % 2, i:i + 1], ps_s[i % 2][:, 0:TRI[i]], AX.X, ALU.max,
                                  negate=True).then_inc(max_ready, 1)

            def normalize(b, h, i):
                dve.wait_ge(exp_ready, n_tiles * b + NT * h + i + 1)
                chain.step(dve.reciprocal(rsum[:, h % 2, i:i + 1], sums[:, h % 2, i:i + 1]))
                chain.done()
                pr = probs[:, h % 2, P_AT[i]:P_AT[i + 1]]
                dve.tensor_scalar(pr, pr, rsum[:, h % 2, i:i + 1], None, ALU.mult).then_inc(probs_ready, 1)

            def low_pT(b, h, j):
                dve.wait_ge(pT_hi, n_tiles * b + NT * h + j + 1)
                dve.tensor_tensor(pT[1][:, T_AT[j]:T_AT[j + 1]], ps_t[j % 2][:, 0:S - j * P],
                                  pT[0][:, T_AT[j]:T_AT[j + 1]].bitcast(F32), ALU.subtract).then_inc(pT_lo, 1)

            with dve.Fori(0, B) as b:
                dve.wait_ge(x_loaded, 16 * (b + 1))
                layernorm_stats(dve, chain, x_in, ln)
                for t in range(NT):
                    dve.tensor_scalar(xn[:, t, :], x_in[:, t, :], ln["mv"][:, t, 0:1], ln["rstd"][:, t:t + 1],
                                      ALU.subtract, ALU.mult).then_inc(xn_ready, 1)
                for c in range(NC):
                    dve.wait_ge(xT_hi, NC * b + c + 1)
                    dve.tensor_tensor(xT[1][:, c, :], ps_xT[c][:], xT[0][:, c, :].bitcast(F32),
                                      ALU.subtract).then_inc(xT_lo, 1)
                dve.wait_ge(x_out_free, b + 1)
                dve.tensor_tensor(x_res[:], x_in[:], bo_sb[:].unsqueeze(1).to_broadcast([P, NT, D]),
                                  ALU.add).then_inc(x_taken, 1)
                cross_head(b, 0, 0)
                cross_head(b, 0, 1)
                low_v(b, 0)
                for s in range(H1 + 1):
                    now, last, ahead = s < H1, s >= 1, s + 1 < H1
                    if last:
                        low_pT(b, s - 1, 0)
                    if now:
                        maxima(b, s, 0)
                    if last:
                        low_pT(b, s - 1, 1)
                    if now:
                        maxima(b, s, 1)
                        normalize(b, s, 0)
                        normalize(b, s, 1)
                    if ahead:
                        cross_head(b, s + 1, 0)
                    if last:
                        low_pT(b, s - 1, 2)
                    if now:
                        maxima(b, s, 2)
                    if last:
                        low_pT(b, s - 1, 3)
                    if now:
                        normalize(b, s, 2)
                    if ahead:
                        cross_head(b, s + 1, 1)
                    if now:
                        maxima(b, s, 3)
                    if last:
                        dve.wait_ge(z_hi, H1 * b + s)
                        dve.scalar_tensor_tensor(out=zT[1][:], in0=ps_z[:], scalar=bias[:, 2, s - 1:s],
                                                 in1=zT[0][:].bitcast(F32), op0=ALU.add,
                                                 op1=ALU.subtract).then_inc(z_lo, 1)
                    if now:
                        normalize(b, s, 3)
                    if ahead:
                        low_v(b, s + 1)
                for u in range(2):
                    dve.wait_ge(y_ps, b + 1)
                    dve.tensor_tensor(x_res[:, 2 * u:2 * u + 2, :], ps_o[u][:], x_res[:, 2 * u:2 * u + 2, :],
                                      ALU.add).then_inc(y_ready, 1)
                chain.restart()

        @block.tensor
        def _(pe):
            def project(b, h, j):
                n = 2 * h + j
                if n == 0:
                    pe.wait_ge(xT_lo, NC * (b + 1))
                elif j == 0:
                    pe.wait_ge(v_lo, H1 * b + h)
                else:
                    pe.wait_ge(qk_raw, 2 * H1 * b + n)
                k = 0
                for c in range(NC):
                    for a, m in PASSES:
                        last = pe.matmul(ps_proj[:], w_parts[a][:, 1 - j, c, h * HD1:(h + 1) * HD1], xT[m][:, c, :],
                                         start=(k == 0), stop=(k == 3 * NC - 1))
                        k += 1
                last.then_inc(qk_ps, 1)

            def project_v(b, part):
                pe.wait_ge(qk_raw, 2 * H1 * b + 2 * part + 2)
                n0 = (part // 2) * 2 * HD1
                for u in range(2):
                    t = 2 * (part % 2) + u
                    k = 0
                    for c in range(NC):
                        for a, m in PASSES:
                            last = pe.matmul(ps_proj[:, u * 2 * HD1:(u + 1) * 2 * HD1], xT[a][:, c, t * P:(t + 1) * P],
                                             w_parts[m][:, 2, c, n0:n0 + 2 * HD1], start=(k == 0), stop=(k == 3 * NC - 1))
                            k += 1
                last.then_inc(v_ps, 1)

            def scores(b, h, i):
                if i == 0:
                    pe.wait_ge(qk_lo, 2 * H1 * b + 2 * h + 2)
                if i >= 2 or h >= 1:
                    pe.wait_ge(exp_ready, n_tiles * b + NT * h + i - 1)
                for k, (a, m) in enumerate(PASSES):
                    pe.matmul(ps_s[i % 2][:, 0:TRI[i]], qkT[a][:, h % 2, 1, i * P:(i + 1) * P],
                              qkT[m][:, h % 2, 0, 0:TRI[i]], start=(k == 0), stop=False)
                pe.matmul(ps_s[i % 2][:, i * P:TRI[i]], ident_b[:], causal[:], start=False,
                          stop=True).then_inc(scores_ps, 1)

            def transposes(b, h, j):
                if j == 0:
                    pe.wait_ge(probs_ready, n_tiles * b + NT * (h + 1))
                if j >= 2 or h >= 1:
                    pe.wait_ge(pT_lo, n_tiles * b + NT * h + j - 1)
                for i in range(j, NT):
                    last = pe.transpose(ps_t[j % 2][:, (i - j) * P:(i - j + 1) * P],
                                        probs[:, h % 2, P_AT[i] + j * P:P_AT[i] + (j + 1) * P], ident[:])
                last.then_inc(pT_ps, 1)

            def values(b, h, j):
                pe.wait_ge(pT_lo, n_tiles * b + NT * h + j + 1)
                if j == 0:
                    pe.wait_ge(v_lo, H1 * b + 2 * (h // 2) + 2)
                    if h >= 1:
                        pe.wait_ge(z_lo, H1 * b + h)
                for k, (a, m) in enumerate(PASSES):
                    last = pe.matmul(ps_z[:, j * P:S], v[a][:, (h // 2) % 2, j, (h % 2) * HD1:(h % 2 + 1) * HD1],
                                     pT[m][:, T_AT[j]:T_AT[j + 1]], start=(j == 0 and k == 0),
                                     stop=(j == NT - 1 and k == 2), skip_group_check=True)
                if j == NT - 1:
                    last.then_inc(z_ps, 1)

            def outputs(b, h):
                pe.wait_ge(z_lo, H1 * b + h + 1)
                pe.wait_ge(wo_lo, H1 * b + h + 1)
                for t in range(NT):
                    for k, (a, m) in enumerate(PASSES):
                        last = pe.matmul(ps_o[t // 2][:, t % 2, :], zT[a][:, t * P:(t + 1) * P],
                                         wo_parts[m][:, h % 2, :], start=(h == 0 and k == 0 and t % 2 == 0),
                                         stop=(h == H1 - 1 and k == 2), skip_group_check=True)
                if h == H1 - 1:
                    last.then_inc(y_ps, 1)

            with pe.Fori(0, B) as b:
                for c in range(NC):
                    for t in range(NT):
                        pe.wait_ge(xn_ready, NT * b + t + 1)
                        last = pe.transpose(ps_xT[c][:, t * P:(t + 1) * P], xn[:, t, c * P:(c + 1) * P], ident[:])
                    last.then_inc(xT_ps, 1)
                project(b, 0, 0)
                project(b, 0, 1)
                project_v(b, 0)
                for s in range(H1 + 1):
                    now, last, ahead = s < H1, s >= 1, s + 1 < H1
                    if last:
                        transposes(b, s - 1, 0)
                    if now:
                        scores(b, s, 0)
                    if last:
                        transposes(b, s - 1, 1)
                    if now:
                        scores(b, s, 1)
                    if ahead:
                        project(b, s + 1, 0)
                    if last:
                        values(b, s - 1, 0)
                        transposes(b, s - 1, 2)
                        values(b, s - 1, 1)
                    if now:
                        scores(b, s, 2)
                    if last:
                        transposes(b, s - 1, 3)
                    if ahead:
                        project(b, s + 1, 1)
                    if last:
                        values(b, s - 1, 2)
                    if now:
                        scores(b, s, 3)
                    if last:
                        values(b, s - 1, 3)
                    if ahead:
                        project_v(b, s + 1)
                    if last:
                        outputs(b, s - 1)

E, TOP_K = 8, 2


def router_buffers(sb):
    names = {n: sb(f"r_{n}", [P, NT, E], F32) for n in ("logits", "e", "p", "rank", "mask", "w")}
    names.update({n: sb(f"r_{n}", [P, NT], F32) for n in ("max", "sum", "rsum")})
    names.update({n: sb(f"r_{n}", [P, NT, E, E], F32) for n in ("gt", "ge")})
    return names


def over_experts(v):
    return v.unsqueeze(2).to_broadcast([P, NT, E])


def top_k_mask(dve, chain, r, before):
    mine = r["p"][:].unsqueeze(3).to_broadcast([P, NT, E, E])
    other = r["p"][:].unsqueeze(2).to_broadcast([P, NT, E, E])
    chain.step(dve.tensor_tensor(r["gt"][:], other, mine, ALU.is_gt))
    chain.step(dve.tensor_tensor(r["ge"][:], other, mine, ALU.is_ge))
    chain.done()
    for t in range(NT):
        chain.step(dve.tensor_tensor(r["ge"][:, t, :, :], r["ge"][:, t, :, :], before[:], ALU.mult))
    chain.done()
    chain.step(dve.tensor_tensor(r["gt"][:], r["gt"][:], r["ge"][:], ALU.max))
    chain.done()
    chain.step(dve.tensor_reduce(r["rank"][:], r["gt"][:], AX.X, ALU.add))
    chain.done()
    chain.step(dve.tensor_scalar(r["mask"][:], r["rank"][:], TOP_K - 0.5, None, ALU.is_lt))
    chain.done()


def normalized(dve, chain, r, dst, v):
    chain.step(dve.tensor_reduce(r["sum"][:], v, AX.X, ALU.add))
    chain.done()
    chain.step(dve.reciprocal(r["rsum"][:], r["sum"][:]))
    chain.done()
    return dve.tensor_tensor(dst, v, over_experts(r["rsum"][:]), ALU.mult)


def make_before(pool, chain, m):
    chain.step(pool.memset(m, 1.0))
    chain.done()
    chain.step(pool.affine_select(out=m, in_=m, compare_op=ALU.is_gt, fill=0.0, base=0,
                                  pattern=[[1, E], [-1, E]], channel_multiplier=0))


HF = 176
NE0 = E + 1
FCH = -(-NE0 * HF // P)
FPAD = FCH * P
GROUP = S // P


def experts0(nc, x, wg, wu, wd, wgs, wus, wds, wr, br, rb, out):
    ctx = ExitStack()
    with ctx:
        def sb(name, shape, dt, stack=ctx):
            return stack.enter_context(nc.sbuf_tensor(f"b_{name}", shape, dt))

        def pb(name, shape, dt):
            return ctx.enter_context(nc.psum_tensor(f"b_{name}", shape, dt))

        def sem(name):
            return ctx.enter_context(nc.semaphore(f"b_{name}"))

        wgu = [sb(f"wgu{k}", [P, NC, NE0, 2 * HF], F32R) for k in range(2)]
        wdn = [sb(f"wdn{k}", [P, FCH, D], F32R) for k in range(2)]
        wrt = [sb(f"wrt{k}", [P, NC, E], F32R) for k in range(2)]
        ident = sb("ident", [P, P], F32)
        before = sb("before", [P, E, E], F32)
        rbias = sb("rbias", [P, 2, E], F32)

        loaded = [sem(f"loaded{i}") for i in range(4)]
        setup_hi = sem("setup_hi")
        setup_lo = sem("setup_lo")
        setup_pool = sem("setup_pool")
        cleared = sem("cleared")

        with ExitStack() as setup:
            wgu_in = sb("wgu_in", [P, NC, NE0, 2 * HF], F32, setup)
            wdn_in = sb("wdn_in", [P, FCH, D], F32, setup)
            wrt_in = sb("wrt_in", [P, NC, E], F32, setup)
            block = setup.enter_context(nc.Block())
            full = E * HF // P
            rest = NE0 * HF - full * P

            @block.sync
            def _(sp):
                for c in range(NC):
                    rows = slice(c * P, (c + 1) * P)
                    sp.dma_start(wgu_in[:, c, 0:E, 0:HF], wg[:, rows, :].rearrange("e p h -> p e h")).then_inc(loaded[0], 16)
                    sp.dma_start(wgu_in[:, c, 0:E, HF:2 * HF], wu[:, rows, :].rearrange("e p h -> p e h")).then_inc(loaded[0], 16)
                    sp.dma_start(wgu_in[:, c, E, 0:HF], wgs[rows, :]).then_inc(loaded[0], 16)
                    sp.dma_start(wgu_in[:, c, E, HF:2 * HF], wus[rows, :]).then_inc(loaded[0], 16)
                sp.wait_ge(cleared, 1)
                sp.dma_start(wdn_in[:, 0:full, :], wd.rearrange("e h d -> (e h) d").rearrange("(k p) d -> p k d", p=P)).then_inc(loaded[1], 16)
                sp.dma_start(wdn_in[:, full, :], wds[0:P, :]).then_inc(loaded[1], 16)
                sp.dma_start(wdn_in[0:rest - P, full + 1, :], wds[P:HF, :]).then_inc(loaded[1], 16)
                sp.dma_start(wrt_in[:], wr.rearrange("(c p) e -> p c e", p=P)).then_inc(loaded[2], 16)
                sp.dma_start(rbias[:, 0, :], row_to_all(br)).then_inc(loaded[3], 16)
                sp.dma_start(rbias[:, 1, :], row_to_all(rb)).then_inc(loaded[3], 16)

            @block.gpsimd
            def _(pool):
                chain = Chain(pool, setup_pool)
                make_identity(pool, chain, ident[:])
                make_before(pool, chain, before[:])
                chain.done()

            parts = ((wgu, wgu_in, 0, 16 * 4 * NC), (wdn, wdn_in, 1, 16 * 3), (wrt, wrt_in, 2, 16))

            @block.scalar
            def _(act):
                for w, w_in, k, n in parts:
                    act.wait_ge(loaded[k], n)
                    act.activation(w[0][:], w_in[:], ACT.Copy).then_inc(setup_hi, 1)

            @block.vector
            def _(dve):
                dve.memset(wdn_in[:, full + 1, :], 0.0).then_inc(cleared, 1)
                for i, (w, w_in, k, n) in enumerate(parts):
                    dve.wait_ge(setup_hi, i + 1)
                    dve.tensor_tensor(w[1][:], w_in[:], w[0][:].bitcast(F32), ALU.subtract).then_inc(setup_lo, 1)
                dve.wait_ge(loaded[3], 32)
                dve.tensor_tensor(rbias[:, 0, :], rbias[:, 0, :], rbias[:, 1, :], ALU.add).then_inc(setup_lo, 1)

        x_in = sb("x_in", [P, NT, D], F32)
        x_res = sb("x_res", [P, NT, D], F32)
        x_out = sb("x_out", [P, NT, D], F32)
        xn = sb("xn", [P, NT, D], F32)
        ln = layernorm_buffers(sb, "b")
        r = router_buffers(sb)
        xT = [sb(f"xT{k}", [P, NC, S], F32R) for k in range(2)]
        act_g = sb("act_g", [P, 2, HF], F32)
        hid = sb("hid", [P, 2, FPAD], F32)
        hT = [sb(f"hT{k}", [P, FCH, P], F32R) for k in range(2)]

        ps_gu = [pb(f"ps_gu{i}", [P, S], F32) for i in range(4)]
        ps_t = [pb(f"ps_t{i}", [P, GROUP, P], F32) for i in range(2)]
        ps_y = [pb(f"ps_y{i}", [P, S], F32) for i in range(2)]
        ps_xT = ps_gu[0:2]
        ps_r = ps_gu[2]

        x_loaded = sem("x_loaded")
        x_taken = sem("x_taken")
        xn_ready = sem("xn_ready")
        xT_ps = sem("xT_ps")
        xT_hi = sem("xT_hi")
        xT_lo = sem("xT_lo")
        router_ps = sem("router_ps")
        logits_ready = sem("logits_ready")
        odds_ready = sem("odds_ready")
        gu_ps = sem("gu_ps")
        silu_ready = sem("silu_ready")
        hid_ready = sem("hid_ready")
        hT_ps = sem("hT_ps")
        hT_hi = sem("hT_hi")
        hT_lo = sem("hT_lo")
        y_ps = sem("y_ps")
        y_ready = sem("y_ready")
        x_out_free = sem("x_out_free")
        stored = sem("stored")
        dve_steps = sem("dve_steps")

        order = [E] + list(range(E))
        n_groups = -(-FCH // GROUP)
        groups = [range(g * GROUP, min(FCH, (g + 1) * GROUP)) for g in range(n_groups)]
        block = ctx.enter_context(nc.Block())

        @block.sync
        def _(sp):
            with sp.Fori(0, B) as b:
                sp.wait_ge(x_taken, b + 1)
                sp.dma_start(x_in[:], token_tiles(x, b)).then_inc(x_loaded, 16)

        @block.gpsimd
        def _(pool):
            pool.sem_inc(x_out_free, 1)
            with pool.Fori(0, B) as b:
                pool.wait_ge(y_ready, NT * b + NT)
                pool.dma_start(token_tiles(out, b), x_out[:]).then_inc(stored, 16)
                pool.wait_ge(stored, 16 * (b + 1))
                pool.sem_inc(x_out_free, 1)

        @block.scalar
        def _(act):
            def high_hT(b, t, g):
                act.wait_ge(hT_ps, n_groups * (NT * b + t) + g + 1)
                k = groups[g]
                act.activation(hT[0][:, k.start:k.stop, :], ps_t[g % 2][:, 0:len(k), :], ACT.Copy).then_inc(hT_hi, 1)

            with act.Fori(0, B) as b:
                for c in range(NC):
                    act.wait_ge(xT_ps, NC * b + c + 1)
                    act.activation(xT[0][:, c, :], ps_xT[c][:], ACT.Copy).then_inc(xT_hi, 1)
                act.wait_ge(logits_ready, b + 1)
                act.activation(r["e"][:], r["logits"][:], ACT.Exp, scale=-1.0).then_inc(odds_ready, 1)
                for t in range(NT + 1):
                    for n in range(NE0):
                        if t < NT:
                            step = NE0 * t + n
                            act.wait_ge(gu_ps, NE0 * NT * b + step + 1)
                            if step >= 2:
                                act.wait_ge(hid_ready, NE0 * NT * b + step - 1)
                            act.activation(act_g[:, step % 2, :], ps_gu[step % 4][:, 0:HF], ACT.Silu).then_inc(silu_ready, 1)
                        if t >= 1 and n < n_groups:
                            high_hT(b, t - 1, n)

        @block.vector
        def _(dve):
            chain = Chain(dve, dve_steps)
            dve.sem_inc(x_taken, 1)
            chain.step(dve.memset(hid[:], 0.0))
            chain.restart()

            def low_hT(b, t, g):
                dve.wait_ge(hT_hi, n_groups * (NT * b + t) + g + 1)
                k = groups[g]
                dve.tensor_tensor(hT[1][:, k.start:k.stop, :], ps_t[g % 2][:, 0:len(k), :],
                                  hT[0][:, k.start:k.stop, :].bitcast(F32), ALU.subtract).then_inc(hT_lo, 1)

            with dve.Fori(0, B) as b:
                dve.wait_ge(x_loaded, 16 * (b + 1))
                layernorm_stats(dve, chain, x_in, ln)
                for t in range(NT):
                    dve.tensor_scalar(xn[:, t, :], x_in[:, t, :], ln["mv"][:, t, 0:1], ln["rstd"][:, t:t + 1],
                                      ALU.subtract, ALU.mult).then_inc(xn_ready, 1)
                for c in range(NC):
                    dve.wait_ge(xT_hi, NC * b + c + 1)
                    dve.tensor_tensor(xT[1][:, c, :], ps_xT[c][:], xT[0][:, c, :].bitcast(F32),
                                      ALU.subtract).then_inc(xT_lo, 1)
                dve.tensor_copy(x_res[:], x_in[:]).then_inc(x_taken, 1)
                dve.wait_ge(router_ps, b + 1)
                dve.tensor_tensor(r["logits"][:], ps_r[:, 0:NT * E].rearrange("p (t e) -> p t e", e=E),
                                  rbias[:, 0, :].unsqueeze(1).to_broadcast([P, NT, E]), ALU.add).then_inc(logits_ready, 1)
                dve.wait_ge(odds_ready, b + 1)
                chain.step(dve.tensor_scalar(r["e"][:], r["e"][:], 1.0, None, ALU.add))
                chain.done()
                chain.step(dve.reciprocal(r["p"][:], r["e"][:]))
                chain.done()
                top_k_mask(dve, chain, r, before)
                chain.step(dve.tensor_tensor(r["e"][:], r["p"][:], r["mask"][:], ALU.mult))
                chain.done()
                chain.step(normalized(dve, chain, r, r["w"][:], r["e"][:]))
                chain.done()
                for t in range(NT + 1):
                    for n, e in enumerate(order):
                        if t < NT:
                            step = NE0 * t + n
                            dve.wait_ge(silu_ready, NE0 * NT * b + step + 1)
                            dst = hid[:, t % 2, e * HF:(e + 1) * HF]
                            if n == 0 and t >= 2:
                                dve.wait_ge(hT_ps, n_groups * (NT * b + t - 1))
                            up = ps_gu[step % 4][:, HF:2 * HF]
                            if e == E:
                                dve.tensor_tensor(dst, act_g[:, step % 2, :], up, ALU.mult).then_inc(hid_ready, 1)
                            else:
                                dve.scalar_tensor_tensor(out=dst, in0=act_g[:, step % 2, :], scalar=r["w"][:, t, e:e + 1],
                                                         in1=up, op0=ALU.mult, op1=ALU.mult).then_inc(hid_ready, 1)
                        if t >= 1 and n < n_groups:
                            low_hT(b, t - 1, n)
                        if t >= 1 and n == n_groups + 1:
                            if t == 1:
                                dve.wait_ge(x_out_free, b + 1)
                            dve.wait_ge(y_ps, NT * b + t)
                            dve.tensor_tensor(x_out[:, t - 1, :], ps_y[(t - 1) % 2][:, 0:D], x_res[:, t - 1, :],
                                              ALU.add).then_inc(y_ready, 1)
                chain.restart()

        @block.tensor
        def _(pe):
            def gate_up(b, step):
                t, n = step // NE0, step % NE0
                if step >= 4:
                    pe.wait_ge(hid_ready, NE0 * NT * b + step - 3)
                elif step == 2:
                    pe.wait_ge(logits_ready, b + 1)
                k = 0
                for c in range(NC):
                    for a, m in PASSES:
                        last = pe.matmul(ps_gu[step % 4][:, 0:2 * HF], xT[a][:, c, t * P:(t + 1) * P],
                                         wgu[m][:, c, order[n], :], start=(k == 0), stop=(k == 3 * NC - 1))
                        k += 1
                last.then_inc(gu_ps, 1)

            def transposes(b, t, g):
                if g == 0:
                    pe.wait_ge(hid_ready, NE0 * (NT * b + t + 1))
                if g >= 2 or t >= 1:
                    pe.wait_ge(hT_lo, n_groups * (NT * b + t) + g - 1)
                for k in groups[g]:
                    last = pe.transpose(ps_t[g % 2][:, k - groups[g].start, :], hid[:, t % 2, k * P:(k + 1) * P], ident[:])
                last.then_inc(hT_ps, 1)

            def down(b, t, g):
                pe.wait_ge(hT_lo, n_groups * (NT * b + t) + g + 1)
                if g == 0 and t >= 2:
                    pe.wait_ge(y_ready, NT * b + t - 1)
                for k in groups[g]:
                    for j, (a, m) in enumerate(PASSES):
                        last = pe.matmul(ps_y[t % 2][:, 0:D], hT[a][:, k, :], wdn[m][:, k, :],
                                         start=(k == 0 and j == 0), stop=(k == FCH - 1 and j == 2))
                if g == n_groups - 1:
                    last.then_inc(y_ps, 1)

            with pe.Fori(0, B) as b:
                for c in range(NC):
                    for t in range(NT):
                        pe.wait_ge(xn_ready, NT * b + t + 1)
                        last = pe.transpose(ps_xT[c][:, t * P:(t + 1) * P], xn[:, t, c * P:(c + 1) * P], ident[:])
                    last.then_inc(xT_ps, 1)
                pe.wait_ge(xT_lo, NC * (b + 1))
                for t in range(NT):
                    k = 0
                    for c in range(NC):
                        for a, m in PASSES:
                            last = pe.matmul(ps_r[:, t * E:(t + 1) * E], xT[a][:, c, t * P:(t + 1) * P], wrt[m][:, c, :],
                                             start=(k == 0), stop=(k == 3 * NC - 1))
                            k += 1
                last.then_inc(router_ps, 1)
                for t in range(NT + 1):
                    for n in range(NE0):
                        if t < NT:
                            gate_up(b, NE0 * t + n)
                        if t >= 1 and n < n_groups:
                            transposes(b, t - 1, n)
                        if t >= 1 and 1 <= n <= n_groups:
                            down(b, t - 1, n - 1)


FW = 128


def experts1(nc, x, wr, w1, b1, w2, b2, out):
    ctx = ExitStack()
    with ctx:
        def sb(name, shape, dt, stack=ctx):
            return stack.enter_context(nc.sbuf_tensor(f"d_{name}", shape, dt))

        def pb(name, shape, dt):
            return ctx.enter_context(nc.psum_tensor(f"d_{name}", shape, dt))

        def sem(name):
            return ctx.enter_context(nc.semaphore(f"d_{name}"))

        wup = [sb(f"wup{k}", [P, NC, E, FW], F32R) for k in range(2)]
        wdn = [sb(f"wdn{k}", [P, E, D], F32R) for k in range(2)]
        wrt = [sb(f"wrt{k}", [P, NC, E], F32R) for k in range(2)]
        b2p = [sb(f"b2p{k}", [P, D], F32R) for k in range(2)]
        sel = sb("sel", [P, E, P], F32R)
        b1_sb = sb("b1", [P, E], F32)
        ident = sb("ident", [P, P], F32)
        before = sb("before", [P, E, E], F32)

        loaded = [sem(f"loaded{i}") for i in range(5)]
        setup_hi = sem("setup_hi")
        setup_lo = sem("setup_lo")
        setup_pool = sem("setup_pool")
        cleared = sem("cleared")

        with ExitStack() as setup:
            wup_in = sb("wup_in", [P, NC, E, FW], F32, setup)
            wdn_in = sb("wdn_in", [P, E, D], F32, setup)
            wrt_in = sb("wrt_in", [P, NC, E], F32, setup)
            b2_in = sb("b2_in", [P, D], F32, setup)
            sel_in = sb("sel_in", [P, E, P], F32, setup)
            block = setup.enter_context(nc.Block())

            @block.sync
            def _(sp):
                for c in range(NC):
                    sp.dma_start(wup_in[:, c, :, :], w1[:, c * P:(c + 1) * P, :].rearrange("e p f -> p e f")).then_inc(loaded[0], 16)
                sp.dma_start(wdn_in[:], w2.rearrange("e f d -> f e d")).then_inc(loaded[1], 16)
                sp.dma_start(wrt_in[:], wr.rearrange("(c p) e -> p c e", p=P)).then_inc(loaded[2], 16)
                sp.dma_start(b1_sb[:], b1).then_inc(loaded[4], 16)
                sp.wait_ge(cleared, 1)
                sp.dma_start(b2_in[0:E, :], b2).then_inc(loaded[3], 16)
                sp.wait_ge(loaded[4], 16)

            @block.gpsimd
            def _(pool):
                chain = Chain(pool, setup_pool)
                make_identity(pool, chain, ident[:])
                make_before(pool, chain, before[:])
                chain.step(pool.memset(sel_in[:], 0.0))
                chain.done()
                chain.step(pool.affine_select(out=sel_in[:], in_=sel_in[:], compare_op=ALU.not_equal, fill=1.0, base=0,
                                              pattern=[[-1, E], [0, P]], channel_multiplier=1))
                chain.done()

            parts = ((wup, wup_in, 0, 16 * NC), (wdn, wdn_in, 1, 16), (wrt, wrt_in, 2, 16), (b2p, b2_in, 3, 16))

            @block.scalar
            def _(act):
                for w, w_in, k, n in parts:
                    act.wait_ge(loaded[k], n)
                    act.activation(w[0][:], w_in[:], ACT.Copy).then_inc(setup_hi, 1)
                act.wait_ge(setup_pool, 6)
                act.activation(sel[:], sel_in[:], ACT.Copy).then_inc(setup_hi, 1)

            @block.vector
            def _(dve):
                dve.memset(b2_in[:], 0.0).then_inc(cleared, 1)
                for i, (w, w_in, k, n) in enumerate(parts):
                    dve.wait_ge(setup_hi, i + 1)
                    dve.tensor_tensor(w[1][:], w_in[:], w[0][:].bitcast(F32), ALU.subtract).then_inc(setup_lo, 1)

        x_in = sb("x_in", [P, NT, D], F32)
        x_res = sb("x_res", [P, NT, D], F32)
        x_out = sb("x_out", [P, NT, D], F32)
        xn = sb("xn", [P, NT, D], F32)
        ln = layernorm_buffers(sb, "d")
        r = router_buffers(sb)
        shares = sb("shares", [P, NT, P], F32)
        shT = [sb(f"shT{k}", [P, S], F32R) for k in range(2)]
        xT = [sb(f"xT{k}", [P, NC, S], F32R) for k in range(2)]
        gel = sb("gel", [P, 2, S], F32)
        hid = sb("hid", [P, 2, S], F32)
        hid_parts = [sb(f"hid{k}", [P, 2, S], F32R) for k in range(2)]

        ps_u = [pb(f"ps_u{i}", [P, S], F32) for i in range(2)]
        ps_c = [pb(f"ps_c{i}", [P, S], F32) for i in range(2)]
        ps_y = [pb(f"ps_y{i}", [P, 2, D], F32) for i in range(2)]
        ps_m = [pb(f"ps_m{i}", [P, S], F32) for i in range(2)]

        x_loaded = sem("x_loaded")
        x_taken = sem("x_taken")
        xn_ready = sem("xn_ready")
        xT_ps = sem("xT_ps")
        xT_hi = sem("xT_hi")
        xT_lo = sem("xT_lo")
        router_ps = sem("router_ps")
        shifted_ready = sem("shifted_ready")
        exp_ready = sem("exp_ready")
        shares_ready = sem("shares_ready")
        shT_ps = sem("shT_ps")
        shT_hi = sem("shT_hi")
        shT_lo = sem("shT_lo")
        u_ps = sem("u_ps")
        gelu_ready = sem("gelu_ready")
        c_ps = sem("c_ps")
        hid_ready = sem("hid_ready")
        hid_hi = sem("hid_hi")
        hid_lo = sem("hid_lo")
        down_done = sem("down_done")
        y_ready = sem("y_ready")
        x_out_free = sem("x_out_free")
        stored = sem("stored")
        dve_steps = sem("dve_steps")

        block = ctx.enter_context(nc.Block())

        @block.sync
        def _(sp):
            with sp.Fori(0, B) as b:
                sp.wait_ge(x_taken, b + 1)
                sp.dma_start(x_in[:], token_tiles(x, b)).then_inc(x_loaded, 16)

        @block.gpsimd
        def _(pool):
            pool.sem_inc(x_out_free, 1)
            with pool.Fori(0, B) as b:
                pool.wait_ge(y_ready, 2 * b + 2)
                pool.dma_start(token_tiles(out, b), x_out[:]).then_inc(stored, 16)
                pool.wait_ge(stored, 16 * (b + 1))
                pool.sem_inc(x_out_free, 1)

        @block.scalar
        def _(act):
            with act.Fori(0, B) as b:
                for c in range(NC):
                    act.wait_ge(xT_ps, NC * b + c + 1)
                    act.activation(xT[0][:, c, :], ps_m[c][:], ACT.Copy).then_inc(xT_hi, 1)
                for k in range(2):
                    act.wait_ge(shifted_ready, 2 * b + k + 1)
                    act.activation(r["e"][:], r["logits"][:], ACT.Exp).then_inc(exp_ready, 1)
                act.wait_ge(shT_ps, b + 1)
                act.activation(shT[0][:], ps_m[1][:], ACT.Copy).then_inc(shT_hi, 1)
                for e in range(E + 1):
                    if e < E:
                        act.wait_ge(u_ps, E * b + e + 1)
                        if e >= 2:
                            act.wait_ge(hid_ready, E * b + e - 1)
                        act.activation(gel[:, e % 2, :], ps_u[e % 2][:], ACT.Gelu, bias=b1_sb[:, e:e + 1]).then_inc(gelu_ready, 1)
                    if e >= 1:
                        act.wait_ge(hid_ready, E * b + e)
                        if e >= 3:
                            act.wait_ge(down_done, E * b + e - 2)
                        act.activation(hid_parts[0][:, (e - 1) % 2, :], hid[:, (e - 1) % 2, :], ACT.Copy).then_inc(hid_hi, 1)

        @block.vector
        def _(dve):
            chain = Chain(dve, dve_steps)
            dve.sem_inc(x_taken, 1)
            chain.step(dve.memset(shares[:], 0.0))
            chain.restart()

            with dve.Fori(0, B) as b:
                dve.wait_ge(x_loaded, 16 * (b + 1))
                layernorm_stats(dve, chain, x_in, ln)
                for t in range(NT):
                    dve.tensor_scalar(xn[:, t, :], x_in[:, t, :], ln["mv"][:, t, 0:1], ln["rstd"][:, t:t + 1],
                                      ALU.subtract, ALU.mult).then_inc(xn_ready, 1)
                for c in range(NC):
                    dve.wait_ge(xT_hi, NC * b + c + 1)
                    dve.tensor_tensor(xT[1][:, c, :], ps_m[c][:], xT[0][:, c, :].bitcast(F32),
                                      ALU.subtract).then_inc(xT_lo, 1)
                dve.tensor_copy(x_res[:], x_in[:]).then_inc(x_taken, 1)
                dve.wait_ge(router_ps, b + 1)
                lg = ps_m[0][:, 0:NT * E].rearrange("p (t e) -> p t e", e=E)
                chain.step(dve.tensor_reduce(r["max"][:], lg, AX.X, ALU.max))
                chain.done()
                dve.tensor_tensor(r["logits"][:], lg, over_experts(r["max"][:]), ALU.subtract).then_inc(shifted_ready, 1)
                dve.wait_ge(exp_ready, 2 * b + 1)
                chain.step(normalized(dve, chain, r, r["p"][:], r["e"][:]))
                chain.done()
                top_k_mask(dve, chain, r, before)
                chain.step(dve.tensor_reduce(r["max"][:], r["p"][:], AX.X, ALU.max))
                chain.done()
                dve.tensor_tensor(r["logits"][:], r["p"][:], over_experts(r["max"][:]), ALU.subtract).then_inc(shifted_ready, 1)
                dve.wait_ge(exp_ready, 2 * b + 2)
                chain.step(dve.tensor_tensor(r["w"][:], r["e"][:], r["mask"][:], ALU.mult))
                chain.done()
                normalized(dve, chain, r, shares[:, :, 0:E], r["w"][:]).then_inc(shares_ready, 1)
                dve.wait_ge(shT_hi, b + 1)
                dve.tensor_tensor(shT[1][:], ps_m[1][:], shT[0][:].bitcast(F32), ALU.subtract).then_inc(shT_lo, 1)
                for e in range(E + 1):
                    if e < E:
                        dve.wait_ge(gelu_ready, E * b + e + 1)
                        dve.wait_ge(c_ps, E * b + e + 1)
                        if e >= 2:
                            dve.wait_ge(hid_hi, E * b + e - 1)
                        dve.tensor_tensor(hid[:, e % 2, :], gel[:, e % 2, :], ps_c[e % 2][:], ALU.mult).then_inc(hid_ready, 1)
                    if e >= 1:
                        dve.wait_ge(hid_hi, E * b + e)
                        dve.tensor_tensor(hid_parts[1][:, (e - 1) % 2, :], hid[:, (e - 1) % 2, :],
                                          hid_parts[0][:, (e - 1) % 2, :].bitcast(F32), ALU.subtract).then_inc(hid_lo, 1)
                dve.wait_ge(x_out_free, b + 1)
                dve.wait_ge(down_done, E * (b + 1))
                for u in range(2):
                    dve.tensor_tensor(x_out[:, 2 * u:2 * u + 2, :], ps_y[u][:], x_res[:, 2 * u:2 * u + 2, :],
                                      ALU.add).then_inc(y_ready, 1)
                chain.restart()

        @block.tensor
        def _(pe):
            def up(b, e):
                if e >= 2:
                    pe.wait_ge(gelu_ready, E * b + e - 1)
                k = 0
                for c in range(NC):
                    for a, m in PASSES:
                        last = pe.matmul(ps_u[e % 2][:], wup[a][:, c, e, :], xT[m][:, c, :], start=(k == 0), stop=(k == 3 * NC - 1))
                        k += 1
                last.then_inc(u_ps, 1)

            def spread(b, e):
                if e >= 2:
                    pe.wait_ge(hid_ready, E * b + e - 1)
                for m in range(2):
                    last = pe.matmul(ps_c[e % 2][:], sel[:, e, :], shT[m][:], start=(m == 0), stop=(m == 1))
                last.then_inc(c_ps, 1)

            def down(b, e):
                pe.wait_ge(hid_lo, E * b + e + 1)
                for t in range(NT):
                    for k, (a, m) in enumerate(PASSES):
                        last = pe.matmul(ps_y[t // 2][:, t % 2, :], hid_parts[a][:, e % 2, t * P:(t + 1) * P], wdn[m][:, e, :],
                                         start=False, stop=(e == E - 1 and k == 2), skip_group_check=True)
                last.then_inc(down_done, 1)

            with pe.Fori(0, B) as b:
                for c in range(NC):
                    for t in range(NT):
                        pe.wait_ge(xn_ready, NT * b + t + 1)
                        last = pe.transpose(ps_m[c][:, t * P:(t + 1) * P], xn[:, t, c * P:(c + 1) * P], ident[:])
                    last.then_inc(xT_ps, 1)
                pe.wait_ge(xT_lo, NC * (b + 1))
                for t in range(NT):
                    k = 0
                    for c in range(NC):
                        for a, m in PASSES:
                            last = pe.matmul(ps_m[0][:, t * E:(t + 1) * E], xT[a][:, c, t * P:(t + 1) * P], wrt[m][:, c, :],
                                             start=(k == 0), stop=(k == 3 * NC - 1))
                            k += 1
                last.then_inc(router_ps, 1)
                up(b, 0)
                up(b, 1)
                pe.wait_ge(shares_ready, b + 1)
                for t in range(NT):
                    last = pe.transpose(ps_m[1][:, t * P:(t + 1) * P], shares[:, t, :], ident[:])
                last.then_inc(shT_ps, 1)
                pe.wait_ge(shT_lo, b + 1)
                for t in range(NT):
                    for k, (a, m) in enumerate(PASSES):
                        pe.matmul(ps_y[t // 2][:, t % 2, :], shT[a][:, t * P:(t + 1) * P], b2p[m][:],
                                  start=(k == 0 and t % 2 == 0), stop=False, skip_group_check=True)
                for e in range(E):
                    spread(b, e)
                    if e + 2 < E:
                        up(b, e + 2)
                    if e >= 1:
                        down(b, e - 1)
                down(b, E - 1)


def preln_stack(nc, x, out, a, f, g, e, cs0, sn0, cs1, sn1):
    mid = [nc.dram_tensor(f"x_after_{n}", (B, S, D), F32, kind="Internal").ap() for n in ("attention0", "experts0", "attention1")]
    attention0(nc, x, *a, cs0, sn0, mid[0])
    experts0(nc, mid[0], *f, mid[1])
    attention1(nc, mid[1], *g, cs1, sn1, mid[2])
    experts1(nc, mid[2], *e, out)


def rope_tables(n, width):
    import numpy as np

    inv = (1.0 / 10000.0 ** (np.arange(0, width, 2, dtype=np.float32) / width)).astype(np.float32)
    freqs = np.outer(np.arange(n, dtype=np.float32), inv)
    return np.cos(freqs).astype(np.float32), np.sin(freqs).astype(np.float32)


def kernel(**inputs):
    import numpy as np
    import concourse.bacc as bacc
    from concourse.bass_utils import run_bass_kernel_spmd

    i = {k: np.asarray(v) for k, v in inputs.items()}
    cs0, sn0 = rope_tables(S, HD0)
    cs1, sn1 = rope_tables(S, HD1)

    def heads(w):
        return w.reshape(H1, D, ROT, 2).transpose(1, 0, 3, 2).reshape(D, H1 * HD1)

    def head_bias(v):
        return v.reshape(H1, ROT, 2).transpose(2, 1, 0).reshape(HD1, H1)

    groups = {
        "x": [i["L0_attn_x"]],
        "a": [i["L0_attn_" + n] for n in ("wq", "bq", "wk", "bk", "wv", "bv", "wo", "bo", "q_norm_scale", "k_norm_scale")],
        "f": [i["L0_ffn_" + n] for n in ("Wg", "Wu", "Wd", "Wg_s", "Wu_s", "Wd_s", "Wr", "br", "rb")],
        "g": [heads(i["L1_attn_W_Q"]), head_bias(i["L1_attn_b_Q"]), heads(i["L1_attn_W_K"]), head_bias(i["L1_attn_b_K"]),
              i["L1_attn_W_V"].transpose(1, 0, 2).reshape(D, H1 * HD1), i["L1_attn_b_V"].T, i["L1_attn_W_O"], i["L1_attn_b_O"]],
        "e": [i["L1_ffn_w_gate"], i["L1_ffn_W1"], i["L1_ffn_b1"].T, i["L1_ffn_W2"], i["L1_ffn_b2"]],
        "t": [cs0, sn0, cs1.T, sn1.T],
    }
    nc = bacc.Bacc("TRN2", target_bir_lowering=False, num_devices=1)
    arrays, args = {}, {}
    for name, group in groups.items():
        args[name] = []
        for n, v in enumerate(group):
            v = np.ascontiguousarray(v)
            arrays[f"in_{name}{n}"] = v
            args[name].append(nc.dram_tensor(f"in_{name}{n}", v.shape, mybir.dt.from_np(v.dtype), kind="ExternalInput").ap())
    out = nc.dram_tensor("out", (B, S, D), F32, kind="ExternalOutput").ap()
    preln_stack(nc, args["x"][0], out, args["a"], args["f"], args["g"], args["e"], *args["t"])
    r = run_bass_kernel_spmd(nc, [arrays], core_ids=[0])
    return r.results[0]["out"]
```

```python
from contextlib import ExitStack

import concourse.bass as bass
from concourse import mybir
from concourse.alu_op_type import AluOpType as ALU

F32 = mybir.dt.float32
F32R = mybir.dt.float32r
F16 = mybir.dt.float16
BF16 = mybir.dt.bfloat16
I32 = mybir.dt.int32
ACT = mybir.ActivationFunctionType
AX = mybir.AxisListType

P = 128
B, S, D = 8, 512, 256
NT = S // P
NC = D // P
LN_EPS = 1e-5
MASKED = -1e38
RSQRT_MAGIC = 1597463007.0


class Chain:

    def __init__(self, eng, sem):
        self.eng, self.sem, self.n = eng, sem, 0

    def step(self, ins):
        ins.then_inc(self.sem, 1)
        self.n += 1
        return self.n

    def done(self, n=None):
        self.eng.wait_ge(self.sem, self.n if n is None else n)

    def restart(self):
        self.done()
        self.eng.sem_clear(self.sem)
        self.n = 0


def rsqrt(dve, chain, y, x, half, sq):
    chain.step(dve.tensor_scalar(half, x, -0.5, None, ALU.mult))
    chain.step(dve.tensor_scalar(sq.bitcast(I32), x.bitcast(I32), 1, None, ALU.logical_shift_right))
    chain.done()
    chain.step(dve.tensor_scalar(y.bitcast(I32), sq.bitcast(I32), -1.0, RSQRT_MAGIC, ALU.mult, ALU.add))
    chain.done()
    for _ in range(4):
        chain.step(dve.tensor_tensor(sq, y, y, ALU.mult))
        chain.done()
        chain.step(dve.tensor_tensor(sq, sq, half, ALU.mult))
        chain.done()
        chain.step(dve.scalar_tensor_tensor(out=y, in0=sq, scalar=1.5, in1=y, op0=ALU.add, op1=ALU.mult))
        chain.done()


def layernorm_stats(dve, chain, x, ln):
    for t in range(NT):
        chain.step(dve.bn_stats(ln["stats"][:, t, :], x[:, t, :]))
    chain.done()
    for t in range(NT):
        chain.step(dve.bn_aggr(ln["mv"][:, t, :], ln["stats"][:, t, :]))
    chain.done()
    chain.step(dve.tensor_scalar(ln["var"][:, :], ln["mv"][:, :, 1], LN_EPS, None, ALU.add))
    chain.done()
    rsqrt(dve, chain, ln["rstd"][:, :], ln["var"][:, :], ln["half"][:, :], ln["sq"][:, :])


def layernorm_buffers(sb, tag):
    return {
        "stats": sb(f"{tag}_ln_stats", [P, NT, 6], F32),
        "mv": sb(f"{tag}_ln_mv", [P, NT, 2], F32),
        "var": sb(f"{tag}_ln_var", [P, NT], F32),
        "rstd": sb(f"{tag}_ln_rstd", [P, NT], F32),
        "half": sb(f"{tag}_ln_half", [P, NT], F32),
        "sq": sb(f"{tag}_ln_sq", [P, NT], F32),
    }


def token_tiles(x, b):
    return x[b, :, :].rearrange("(t p) d -> p t d", p=P)


def row_to_all(v):
    return v.rearrange("(o n) -> o n", o=1).partition_broadcast(P)


def make_identity(pool, chain, m):
    chain.step(pool.memset(m, 0.0))
    chain.done()
    chain.step(pool.affine_select(out=m, in_=m, compare_op=ALU.not_equal, fill=1.0, base=0,
                                  pattern=[[-1, P]], channel_multiplier=1))


def make_causal(pool, chain, m):
    chain.step(pool.memset(m, 0.0))
    chain.done()
    chain.step(pool.affine_select(out=m, in_=m, compare_op=ALU.is_ge, fill=MASKED, base=0,
                                  pattern=[[-1, P]], channel_multiplier=1))


HD0, H0, G0 = 16, 16, 4
REP0 = H0 // G0
QK0 = (H0 + G0) * HD0
QKV0 = (H0 + 2 * G0) * HD0
GW = 32
RMS_EPS = 1e-6
TRI = [P * (i + 1) for i in range(NT)]
P_AT = [sum(TRI[:i]) for i in range(NT + 1)]
T_AT = [sum(S - P * k for k in range(j)) for j in range(NT + 1)]


def attention0(nc, x, wq, bq, wk, bk, wv, bv, wo, bo, q_scale, k_scale, cos, sin, out):
    ctx = ExitStack()
    with ctx:
        def sb(name, shape, dt):
            return ctx.enter_context(nc.sbuf_tensor(f"a_{name}", shape, dt))

        def pb(name, shape, dt):
            return ctx.enter_context(nc.psum_tensor(f"a_{name}", shape, dt))

        def sem(name):
            return ctx.enter_context(nc.semaphore(f"a_{name}"))

        w_in = sb("w_in", [P, NC, QKV0], F32)
        wo_in = sb("wo_in", [P, NC, D], F32)
        w16 = sb("w16", [P, NC, QKV0], F16)
        wo16 = sb("wo16", [P, NC, D], F16)
        b_in = sb("b_in", [P, QKV0], F32)
        b16 = sb("b16", [P, QKV0], F16)
        bo_in = sb("bo_in", [P, D], F32)
        bo16 = sb("bo16", [P, D], F16)
        cs_in = sb("cs_in", [P, NT, HD0 // 2], F32)
        sn_in = sb("sn_in", [P, NT, HD0 // 2], F32)
        scales = sb("scales", [P, 2, HD0], F32)
        tab_c = sb("tab_c", [P, NT, 2, HD0], F32)
        tab_s = sb("tab_s", [P, NT, 2, HD0], F32)
        ident = sb("ident", [P, P], F16)
        ident_b = sb("ident_b", [P, P], BF16)
        causal = sb("causal", [P, P], BF16)
        x_in = sb("x_in", [P, NT, D], F32)
        x_res = sb("x_res", [P, NT, D], F32)
        x_out = sb("x_out", [P, NT, D], F32)
        xn = sb("xn", [P, NT, D], F16)
        ln = layernorm_buffers(sb, "x")
        xT = sb("xT", [P, NC, S], F16)
        qkv = sb("qkv", [P, NT, QKV0], F16)
        sq = sb("sq", [P, NT, QK0], F32)
        ra = sb("ra", [P, NT, QK0], F32)
        rb = sb("rb", [P, NT, QK0], F32)
        ms = sb("ms", [P, NT * (H0 + G0)], F32)
        rs = sb("rs", [P, NT * (H0 + G0)], F32)
        rs_half = sb("rs_half", [P, NT * (H0 + G0)], F32)
        rs_sq = sb("rs_sq", [P, NT * (H0 + G0)], F32)
        q_pad = sb("q_pad", [P, NT, REP0, G0, GW], F16)
        k_pad = sb("k_pad", [P, NT, G0, GW], F16)
        qT = sb("qT", [P, REP0, S], F16)
        kT = sb("kT", [P, G0, S], F16)
        nmax = sb("nmax", [P, 2, NT], F32)
        sums = sb("sums", [P, NT, H0], F32)
        rsum = sb("rsum", [P, NT, H0], F32)
        probs = sb("probs", [P, 2, P_AT[NT]], F16)
        pT = sb("pT", [P, 2, T_AT[NT]], F16)
        z16 = sb("z16", [P, NT, D], F16)
        zT = sb("zT", [P, NC, S], F16)

        ps_s = [pb(f"ps_s{i}", [P, S], F32) for i in range(4)]
        ps_t = [pb(f"ps_t{i}", [P, 2 * S], F16) for i in range(2)]
        ps_z = [pb(f"ps_z{i}", [P, 2, D], F32) for i in range(2)]
        ps_xT = ps_t
        ps_qkv = ps_s[0:2]
        ps_qT = ps_t
        ps_kT = ps_s[2][:, 0:S // 2].bitcast(F16)
        ps_zT = ps_t

        loaded = [sem(f"loaded{i}") for i in range(3)]
        setup_pool = sem("setup_pool")
        setup_dve = sem("setup_dve")
        consts_ready = sem("consts_ready")
        x_loaded = sem("x_loaded")
        x_taken = sem("x_taken")
        xn_ready = sem("xn_ready")
        xT_ps = sem("xT_ps")
        xT_ready = sem("xT_ready")
        qkv_ps = sem("qkv_ps")
        qkv_ready = sem("qkv_ready")
        sq_ready = sem("sq_ready")
        rot_ready = sem("rot_ready")
        qk_ready = sem("qk_ready")
        qkT_ps = sem("qkT_ps")
        qkT_ready = sem("qkT_ready")
        scores_ps = sem("scores_ps")
        max_ready = sem("max_ready")
        probs_ready = sem("probs_ready")
        pT_ps = sem("pT_ps")
        pT_ready = sem("pT_ready")
        z_ps = sem("z_ps")
        z_ready = sem("z_ready")
        zT_ps = sem("zT_ps")
        zT_ready = sem("zT_ready")
        y_ps = sem("y_ps")
        y_ready = sem("y_ready")
        stored = sem("stored")
        x_out_free = sem("x_out_free")
        dve_steps = sem("dve_steps")

        block = ctx.enter_context(nc.Block())

        @block.sync
        def _(sp):
            sp.dma_start(w_in[:, :, 0:D], wq.rearrange("(c p) n -> p c n", p=P)).then_inc(loaded[1], 16)
            sp.dma_start(w_in[:, :, D:QK0], wk.rearrange("(c p) n -> p c n", p=P)).then_inc(loaded[1], 16)
            sp.dma_start(w_in[:, :, QK0:QKV0], wv.rearrange("(c p) n -> p c n", p=P)).then_inc(loaded[1], 16)
            sp.dma_start(b_in[:, 0:D], row_to_all(bq)).then_inc(loaded[1], 16)
            sp.dma_start(b_in[:, D:QK0], row_to_all(bk)).then_inc(loaded[1], 16)
            sp.dma_start(b_in[:, QK0:QKV0], row_to_all(bv)).then_inc(loaded[1], 16)
            sp.dma_start(cs_in[:], cos.rearrange("(t p) n -> p t n", p=P)).then_inc(loaded[0], 16)
            sp.dma_start(sn_in[:], sin.rearrange("(t p) n -> p t n", p=P)).then_inc(loaded[0], 16)
            sp.dma_start(scales[:, 0, :], row_to_all(q_scale)).then_inc(loaded[0], 16)
            sp.dma_start(scales[:, 1, :], row_to_all(k_scale)).then_inc(loaded[0], 16)
            sp.dma_start(wo_in[:], wo.rearrange("(c p) n -> p c n", p=P)).then_inc(loaded[2], 16)
            sp.dma_start(bo_in[:], row_to_all(bo)).then_inc(loaded[2], 16)
            with sp.Fori(0, B) as b:
                sp.wait_ge(x_taken, b + 1)
                sp.dma_start(x_in[:], token_tiles(x, b)).then_inc(x_loaded, 16)

        @block.gpsimd
        def _(pool):
            chain = Chain(pool, setup_pool)
            make_identity(pool, chain, ident[:])
            make_identity(pool, chain, ident_b[:])
            make_causal(pool, chain, causal[:])
            pool.sem_inc(x_out_free, 1)
            with pool.Fori(0, B) as b:
                pool.wait_ge(y_ready, 2 * b + 2)
                pool.dma_start(token_tiles(out, b), x_out[:]).then_inc(stored, 16)
                pool.wait_ge(stored, 16 * (b + 1))
                pool.sem_inc(x_out_free, 1)

        @block.scalar
        def _(act):
            with act.Fori(0, B) as b:
                for c in range(NC):
                    act.wait_ge(xT_ps, NC * b + c + 1)
                    act.activation(xT[:, c, :], ps_xT[c][:, 0:S], ACT.Copy).then_inc(xT_ready, 1)
                for t in range(NT):
                    act.wait_ge(qkv_ready, NT * b + t + 1)
                    act.activation(sq[:, t, :], qkv[:, t, 0:QK0], ACT.Square).then_inc(sq_ready, 1)
                for r in range(REP0):
                    act.wait_ge(qkT_ps, 2 * b + 1)
                    act.activation(qT[:, r, :], ps_qT[r // 2][:, (r % 2) * S:(r % 2 + 1) * S],
                                   ACT.Copy).then_inc(qkT_ready, 1)
                act.wait_ge(qkT_ps, 2 * b + 2)
                for g in range(G0):
                    rows = slice(GW * g, GW * (g + 1))
                    act.activation(kT[rows, g, :], ps_kT[rows, :], ACT.Copy).then_inc(qkT_ready, 1)
                for h in range(H0):
                    for i in range(NT):
                        n = NT * h + i
                        act.wait_ge(max_ready, H0 * NT * b + n + 1)
                        if i == 0 and h >= 2:
                            act.wait_ge(pT_ps, 2 * H0 * b + 2 * (h - 1))
                        act.activation(probs[:, h % 2, P_AT[i]:P_AT[i + 1]], ps_s[i][:, 0:TRI[i]], ACT.Exp,
                                       bias=nmax[:, h % 2, i:i + 1],
                                       accum_out=sums[:, i, h:h + 1]).then_inc(probs_ready, 1)
                for c in range(NC):
                    act.wait_ge(zT_ps, NC * b + c + 1)
                    act.activation(zT[:, c, :], ps_zT[c][:, 0:S], ACT.Copy).then_inc(zT_ready, 1)

        @block.vector
        def _(dve):
            chain = Chain(dve, setup_dve)
            dve.wait_ge(loaded[0], 16 * 4)
            half = HD0 // 2
            for j in range(2):
                by = float(HD0) ** -1 if j == 0 else 1.0
                lo = scales[:, j, 0:half].unsqueeze(1).to_broadcast([P, NT, half])
                hi = scales[:, j, half:HD0].unsqueeze(1).to_broadcast([P, NT, half])
                for dst, table, scale, sign in ((tab_c[:, :, j, 0:half], cs_in, lo, 1.0), (tab_c[:, :, j, half:HD0], cs_in, hi, 1.0),
                                                (tab_s[:, :, j, 0:half], sn_in, hi, -1.0), (tab_s[:, :, j, half:HD0], sn_in, lo, 1.0)):
                    chain.step(dve.scalar_tensor_tensor(out=dst, in0=table[:], scalar=sign * by, in1=scale,
                                                        op0=ALU.mult, op1=ALU.mult))
            dve.wait_ge(loaded[1], 16 * 6)
            chain.step(dve.tensor_copy(w16[:], w_in[:]))
            chain.step(dve.tensor_copy(b16[:], b_in[:]))
            dve.wait_ge(loaded[2], 16 * 2)
            chain.step(dve.tensor_copy(wo16[:], wo_in[:]))
            chain.step(dve.tensor_copy(bo16[:], bo_in[:]))
            chain.step(dve.memset(q_pad[:].rearrange("p a b c d -> p (a b c d)"), 0.0))
            chain.step(dve.memset(k_pad[:].rearrange("p a b c -> p (a b c)"), 0.0))
            chain.step(dve.memset(kT[:].rearrange("p a b -> p (a b)"), 0.0))
            chain.done()
            dve.sem_inc(consts_ready, 1)
            dve.sem_inc(x_taken, 1)

            chain = Chain(dve, dve_steps)
            with dve.Fori(0, B) as b:
                dve.wait_ge(x_loaded, 16 * (b + 1))
                layernorm_stats(dve, chain, x_in, ln)
                for t in range(NT):
                    dve.tensor_scalar(xn[:, t, :], x_in[:, t, :], ln["mv"][:, t, 0:1], ln["rstd"][:, t:t + 1],
                                      ALU.subtract, ALU.mult).then_inc(xn_ready, 1)
                dve.tensor_tensor(x_res[:], x_in[:], bo16[:].unsqueeze(1).to_broadcast([P, NT, D]),
                                  ALU.add).then_inc(x_taken, 1)
                for t in range(NT):
                    dve.wait_ge(qkv_ps, NT * b + t + 1)
                    dve.tensor_tensor(qkv[:, t, :], ps_qkv[t % 2][:, 0:QKV0], b16[:], ALU.add).then_inc(qkv_ready, 1)
                dve.wait_ge(qkv_ready, NT * b + NT)
                for t in range(NT):
                    for j, (c0, nh) in enumerate(((0, H0), (D, G0))):
                        src = qkv[:, t, c0:c0 + nh * HD0].rearrange("p (h d) -> p h d", d=HD0)
                        a = ra[:, t, c0:c0 + nh * HD0].rearrange("p (h d) -> p h d", d=HD0)
                        r = rb[:, t, c0:c0 + nh * HD0].rearrange("p (h d) -> p h d", d=HD0)
                        chain.step(dve.tensor_tensor(a, src, tab_c[:, t, j, :].unsqueeze(1).to_broadcast([P, nh, HD0]), ALU.mult))
                        for to, frm in ((slice(0, half), slice(half, HD0)), (slice(half, HD0), slice(0, half))):
                            chain.step(dve.tensor_tensor(r[:, :, to], src[:, :, frm],
                                                         tab_s[:, t, j, to].unsqueeze(1).to_broadcast([P, nh, half]), ALU.mult))
                dve.wait_ge(sq_ready, NT * b + NT)
                chain.step(dve.tensor_reduce(ms[:], sq[:].rearrange("p t (h d) -> p (t h) d", d=HD0), AX.X, ALU.add))
                chain.done()
                chain.step(dve.tensor_tensor(ra[:], ra[:], rb[:], ALU.add))
                chain.step(dve.tensor_scalar(ms[:], ms[:], 1.0 / HD0, RMS_EPS, ALU.mult, ALU.add))
                chain.done()
                rsqrt(dve, chain, rs[:], ms[:], rs_half[:], rs_sq[:])
                for t in range(NT):
                    r4 = rs[:, t * (H0 + G0):(t + 1) * (H0 + G0)]
                    for g in range(G0):
                        h0 = g * REP0
                        dve.tensor_tensor(
                            q_pad[:, t, :, g, 0:HD0],
                            ra[:, t, h0 * HD0:(h0 + REP0) * HD0].rearrange("p (r d) -> p r d", d=HD0),
                            r4[:, h0:h0 + REP0].unsqueeze(2).to_broadcast([P, REP0, HD0]), ALU.mult).then_inc(qk_ready, 1)
                    dve.tensor_tensor(
                        k_pad[:, t, :, 0:HD0], ra[:, t, D:QK0].rearrange("p (g d) -> p g d", d=HD0),
                        r4[:, H0:H0 + G0].unsqueeze(2).to_broadcast([P, G0, HD0]), ALU.mult).then_inc(qk_ready, 1)

                def copy_pT(h):
                    for k, (j0, j1) in enumerate(((0, 2), (2, 4))):
                        dve.wait_ge(pT_ps, 2 * H0 * b + 2 * h + k + 1)
                        dve.tensor_copy(pT[:, h % 2, T_AT[j0]:T_AT[j1]],
                                        ps_t[k][:, 0:T_AT[j1] - T_AT[j0]]).then_inc(pT_ready, 1)

                for h in range(H0):
                    if h >= 1:
                        copy_pT(h - 1)
                    for i in range(NT):
                        dve.wait_ge(scores_ps, H0 * NT * b + NT * h + i + 1)
                        dve.tensor_reduce(nmax[:, h % 2, i:i + 1], ps_s[i][:, 0:TRI[i]], AX.X, ALU.max,
                                          negate=True).then_inc(max_ready, 1)
                copy_pT(H0 - 1)
                dve.wait_ge(probs_ready, H0 * NT * (b + 1))
                chain.step(dve.reciprocal(rsum[:], sums[:]))
                chain.done()
                dve.wait_ge(z_ps, b + 1)
                for t in range(NT):
                    dve.tensor_tensor(z16[:, t, :].rearrange("p (h d) -> p h d", d=HD0),
                                      ps_z[t // 2][:, t % 2, :].rearrange("p (h d) -> p h d", d=HD0),
                                      rsum[:, t, :].unsqueeze(2).to_broadcast([P, H0, HD0]), ALU.mult).then_inc(z_ready, 1)
                for u in range(2):
                    dve.wait_ge(y_ps, 2 * b + u + 1)
                    if u == 0:
                        dve.wait_ge(x_out_free, b + 1)
                    dve.tensor_tensor(x_out[:, 2 * u:2 * u + 2, :], ps_z[u][:], x_res[:, 2 * u:2 * u + 2, :],
                                      ALU.add).then_inc(y_ready, 1)
                chain.restart()

        @block.tensor
        def _(pe):
            pe.wait_ge(setup_pool, 6)
            pe.wait_ge(consts_ready, 1)
            with pe.Fori(0, B) as b:
                for c in range(NC):
                    for t in range(NT):
                        pe.wait_ge(xn_ready, NT * b + t + 1)
                        last = pe.transpose(ps_xT[c][:, t * P:(t + 1) * P],
                                            xn[:, t, c * P:(c + 1) * P], ident[:])
                    last.then_inc(xT_ps, 1)
                pe.wait_ge(xT_ready, NC * b + NC)
                for t in range(NT):
                    if t >= 2:
                        pe.wait_ge(qkv_ready, NT * b + t - 1)
                    for c in range(NC):
                        last = pe.matmul(ps_qkv[t % 2][:, 0:QKV0], xT[:, c, t * P:(t + 1) * P], w16[:, c, :],
                                         start=(c == 0), stop=(c == NC - 1))
                    last.then_inc(qkv_ps, 1)
                pe.wait_ge(qk_ready, NT * (G0 + 1) * (b + 1))
                for t in range(NT):
                    for r in range(REP0):
                        last = pe.transpose(ps_qT[r // 2][:, (r % 2) * S + t * P:(r % 2) * S + (t + 1) * P],
                                            q_pad[:, t, r, :, :].rearrange("p g d -> p (g d)"), ident[:])
                last.then_inc(qkT_ps, 1)
                for t in range(NT):
                    last = pe.transpose(ps_kT[:, t * P:(t + 1) * P],
                                        k_pad[:, t, :, :].rearrange("p g d -> p (g d)"), ident[:])
                last.then_inc(qkT_ps, 1)
                pe.wait_ge(qkT_ready, (REP0 + G0) * (b + 1))

                def scores(h):
                    g, r = h // REP0, h % REP0
                    for i in range(NT):
                        if h >= 1:
                            pe.wait_ge(probs_ready, H0 * NT * b + NT * (h - 1) + i + 1)
                        pe.matmul(ps_s[i][:, 0:TRI[i]], qT[:, r, i * P:(i + 1) * P], kT[:, g, 0:TRI[i]],
                                  start=True, stop=False)
                        pe.matmul(ps_s[i][:, i * P:TRI[i]], ident_b[:], causal[:],
                                  start=False, stop=True).then_inc(scores_ps, 1)

                def transposes(h):
                    pe.wait_ge(probs_ready, H0 * NT * b + NT * (h + 1))
                    if h >= 1:
                        pe.wait_ge(pT_ready, 2 * (H0 * b + h))
                    for k, (j0, j1) in enumerate(((0, 2), (2, 4))):
                        for j in range(j0, j1):
                            for i in range(j, NT):
                                at = T_AT[j] - T_AT[j0] + (i - j) * P
                                last = pe.transpose(ps_t[k][:, at:at + P],
                                                    probs[:, h % 2, P_AT[i] + j * P:P_AT[i] + (j + 1) * P], ident[:])
                        last.then_inc(pT_ps, 1)

                def values(h):
                    v0 = QK0 + (h // REP0) * HD0
                    pe.wait_ge(pT_ready, 2 * (H0 * b + h) + 2)
                    for i in range(NT):
                        for j in range(i + 1):
                            at = T_AT[j] + (i - j) * P
                            last = pe.matmul(ps_z[i // 2][:, i % 2, h * HD0:(h + 1) * HD0], pT[:, h % 2, at:at + P],
                                             qkv[:, j, v0:v0 + HD0], start=(j == 0), stop=(j == i))
                    if h == H0 - 1:
                        last.then_inc(z_ps, 1)

                scores(0)
                for h in range(H0):
                    transposes(h)
                    if h + 1 < H0:
                        scores(h + 1)
                    values(h)
                for c in range(NC):
                    for t in range(NT):
                        pe.wait_ge(z_ready, NT * b + t + 1)
                        last = pe.transpose(ps_zT[c][:, t * P:(t + 1) * P],
                                            z16[:, t, c * P:(c + 1) * P], ident[:])
                    last.then_inc(zT_ps, 1)
                pe.wait_ge(zT_ready, NC * b + NC)
                for t in range(NT):
                    for c in range(NC):
                        last = pe.matmul(ps_z[t // 2][:, t % 2, :], zT[:, c, t * P:(t + 1) * P], wo16[:, c, :],
                                         start=(c == 0), stop=(c == NC - 1))
                    if t % 2 == 1:
                        last.then_inc(y_ps, 1)

H1, HD1 = 16, 128
ROT = HD1 // 2
SCALE1 = float(HD1) ** -0.5
PASSES = ((0, 0), (0, 1), (1, 0))


def split_halves(parts, hi, lo):
    return (hi, lo)[parts]


def attention1(nc, x, wq, bq, wk, bk, wv, bv, wo, bo, cos, sin, out):
    ctx = ExitStack()
    with ctx:
        def sb(name, shape, dt, stack=ctx):
            return stack.enter_context(nc.sbuf_tensor(f"c_{name}", shape, dt))

        def pb(name, shape, dt):
            return ctx.enter_context(nc.psum_tensor(f"c_{name}", shape, dt))

        def sem(name):
            return ctx.enter_context(nc.semaphore(f"c_{name}"))

        DM = H1 * HD1
        w_hi = sb("w_hi", [P, 3, NC, DM], F32R)
        w_lo = sb("w_lo", [P, 3, NC, DM], F32R)
        w_parts = (w_hi, w_lo)
        wo_sb = sb("wo", [P, H1, D], F32)
        ident = sb("ident", [P, P], F32)
        ident_b = sb("ident_b", [P, P], BF16)
        causal = sb("causal", [P, P], BF16)
        cosT = sb("cosT", [P, S], F32)
        sinT = sb("sinT", [P, S], F32)
        bias = sb("bias", [P, 3, H1], F32)
        bo_sb = sb("bo", [P, D], F32)

        loaded = [sem(f"loaded{i}") for i in range(5)]
        setup_hi = sem("setup_hi")
        setup_lo = sem("setup_lo")
        setup_pool = sem("setup_pool")

        with ExitStack() as setup:
            w_in = sb("w_in", [P, 3, NC * DM], F32, setup)
            block = setup.enter_context(nc.Block())

            @block.sync
            def _(sp):
                for i, w in enumerate((wq, wk, wv)):
                    for c in range(NC):
                        sp.dma_start(w_in[:, i, c * DM:(c + 1) * DM], w[c * P:(c + 1) * P, :]).then_inc(loaded[i], 16)
                sp.dma_start(wo_sb[:], wo.rearrange("n d m -> d n m")).then_inc(loaded[3], 16)
                for i, v in enumerate((bq, bk, bv)):
                    sp.dma_start(bias[:, i, :], v).then_inc(loaded[4], 16)
                sp.dma_start(bo_sb[:], row_to_all(bo)).then_inc(loaded[4], 16)
                for k in range(2):
                    sp.dma_start(cosT[k * ROT:(k + 1) * ROT, :], cos).then_inc(loaded[4], 16)
                    sp.dma_start(sinT[k * ROT:(k + 1) * ROT, :], sin).then_inc(loaded[4], 16)
                sp.wait_ge(loaded[3], 16)

            @block.gpsimd
            def _(pool):
                chain = Chain(pool, setup_pool)
                make_identity(pool, chain, ident[:])
                make_identity(pool, chain, ident_b[:])
                make_causal(pool, chain, causal[:])
                chain.done()

            @block.scalar
            def _(act):
                for i in range(3):
                    act.wait_ge(loaded[i], 16 * NC)
                    act.activation(w_hi[:, i, :, :].rearrange("p c n -> p (c n)"), w_in[:, i, :],
                                   ACT.Copy).then_inc(setup_hi, 1)

            @block.vector
            def _(dve):
                for i in range(3):
                    dve.wait_ge(setup_hi, i + 1)
                    dve.tensor_tensor(w_lo[:, i, :, :].rearrange("p c n -> p (c n)"), w_in[:, i, :],
                                      w_hi[:, i, :, :].rearrange("p c n -> p (c n)").bitcast(F32),
                                      ALU.subtract).then_inc(setup_lo, 1)
                dve.wait_ge(loaded[4], 16 * 8)
                dve.tensor_scalar(bias[:, 0, :], bias[:, 0, :], SCALE1, None, ALU.mult).then_inc(setup_lo, 1)
                dve.tensor_scalar(sinT[0:ROT, :], sinT[0:ROT, :], 1.0, None, ALU.mult).then_inc(setup_lo, 1)
                dve.tensor_scalar(sinT[ROT:P, :], sinT[ROT:P, :], -1.0, None, ALU.mult).then_inc(setup_lo, 1)

        x_in = sb("x_in", [P, NT, D], F32)
        x_res = sb("x_res", [P, NT, D], F32)
        ln = layernorm_buffers(sb, "c")
        xT = [sb(f"xT{k}", [P, NC, S], F32R) for k in range(2)]
        raw = sb("raw", [P, 2, S], F32)
        turn = sb("turn", [P, 2, S], F32)
        cross = sb("cross", [P, 2, S], F32)
        qkT = [sb(f"qkT{k}", [P, 2, 2, S], F32R) for k in range(2)]
        v = [sb(f"v{k}", [P, 2, NT, 2 * HD1], F32R) for k in range(2)]
        probs = sb("probs", [P, 2, P_AT[NT]], F32)
        xn = probs[:, 0, 0:NT * D].rearrange("p (t d) -> p t d", d=D)
        pT = [sb(f"pT{k}", [P, T_AT[NT]], F32R) for k in range(2)]
        zT = [sb(f"zT{k}", [P, S], F32R) for k in range(2)]
        wo_parts = [sb(f"wo{k}", [P, 2, D], F32R) for k in range(2)]
        nmax = sb("nmax", [P, 2, NT], F32)
        sums = sb("sums", [P, 2, NT], F32)
        rsum = sb("rsum", [P, 2, NT], F32)

        ps_s = [pb(f"ps_s{i}", [P, S], F32) for i in range(2)]
        ps_t = [pb(f"ps_t{i}", [P, S], F32) for i in range(2)]
        ps_proj = pb("ps_proj", [P, S], F32)
        ps_z = pb("ps_z", [P, S], F32)
        ps_o = [pb(f"ps_o{i}", [P, 2, D], F32) for i in range(2)]
        ps_xT = ps_s

        x_loaded = sem("x_loaded")
        x_taken = sem("x_taken")
        xn_ready = sem("xn_ready")
        xT_ps = sem("xT_ps")
        xT_hi = sem("xT_hi")
        xT_lo = sem("xT_lo")
        qk_ps = [sem(f"qk_ps{j}") for j in range(2)]
        qk_raw = [sem(f"qk_raw{j}") for j in range(2)]
        qk_cos = [sem(f"qk_cos{j}") for j in range(2)]
        qk_turned = [sem(f"qk_turned{j}") for j in range(2)]
        qk_hi = [sem(f"qk_hi{j}") for j in range(2)]
        qk_lo = [sem(f"qk_lo{j}") for j in range(2)]
        v_ps = sem("v_ps")
        v_hi = sem("v_hi")
        v_lo = sem("v_lo")
        scores_ps = [sem(f"scores_ps{i}") for i in range(NT)]
        max_ready = [sem(f"max_ready{i}") for i in range(NT)]
        exp_ready = [sem(f"exp_ready{i}") for i in range(NT)]
        probs_ready = [sem(f"probs_ready{i}") for i in range(NT)]
        pT_ps = sem("pT_ps")
        pT_hi = sem("pT_hi")
        pT_lo = sem("pT_lo")
        pv_done = sem("pv_done")
        o_done = sem("o_done")
        z_hi = sem("z_hi")
        z_lo = sem("z_lo")
        wo_hi = sem("wo_hi")
        wo_lo = sem("wo_lo")
        y_ready = sem("y_ready")
        x_out_free = sem("x_out_free")
        stored = sem("stored")
        dve_steps = sem("dve_steps")

        block = ctx.enter_context(nc.Block())

        @block.sync
        def _(sp):
            with sp.Fori(0, B) as b:
                sp.wait_ge(x_taken, b + 1)
                sp.dma_start(x_in[:], token_tiles(x, b)).then_inc(x_loaded, 16)

        def at(b, h):
            return H1 * b + h + 1

        def row_at(b, h, j):
            return NT * (H1 * b + h) + j + 1

        def real(h):
            return 0 <= h < H1

        @block.gpsimd
        def _(pool):
            pool.sem_inc(x_out_free, 1)

            def cos_part(b, h, j):
                if real(h):
                    pool.wait_ge(qk_raw[j], at(b, h))
                    if h >= 1:
                        pool.wait_ge(qk_lo[j], at(b, h - 1))
                    pool.tensor_tensor(turn[:, j, :], raw[:, j, :], cosT[:], ALU.mult).then_inc(qk_cos[j], 1)

            def low_head(b, h, j):
                if real(h):
                    pool.wait_ge(qk_hi[j], at(b, h))
                    pool.tensor_tensor(qkT[1][:, h % 2, j, :], turn[:, j, :], qkT[0][:, h % 2, j, :].bitcast(F32),
                                       ALU.subtract).then_inc(qk_lo[j], 1)

            def low_wo(b, h):
                if real(h):
                    pool.wait_ge(wo_hi, at(b, h))
                    pool.tensor_tensor(wo_parts[1][:, h % 2, :], wo_sb[:, h, :],
                                       wo_parts[0][:, h % 2, :].bitcast(F32), ALU.subtract).then_inc(wo_lo, 1)

            with pool.Fori(0, B) as b:
                for s in range(-2, H1 + 2):
                    low_head(b, s + 1, 1)
                    cos_part(b, s + 2, 0)
                    cos_part(b, s + 2, 1)
                    low_head(b, s + 2, 0)
                    low_wo(b, s)
                pool.wait_ge(y_ready, 2 * b + 2)
                pool.dma_start(token_tiles(out, b), x_res[:]).then_inc(stored, 16)
                pool.wait_ge(stored, 16 * (b + 1))
                pool.sem_inc(x_out_free, 1)

        @block.scalar
        def _(act):
            def raw_head(b, h, j):
                if real(h):
                    act.wait_ge(qk_ps[j], at(b, h))
                    act.activation(raw[:, j, :], ps_proj[:], ACT.Identity, bias=bias[:, 1 - j, h:h + 1],
                                   scale=SCALE1 if j == 1 else 1.0).then_inc(qk_raw[j], 1)

            def high_head(b, h, j):
                if real(h):
                    act.wait_ge(qk_turned[j], at(b, h))
                    if h >= 2:
                        act.wait_ge(scores_ps[NT - 1], at(b, h - 2))
                    act.activation(qkT[0][:, h % 2, j, :], turn[:, j, :], ACT.Copy).then_inc(qk_hi[j], 1)

            def high_v(b, part):
                if real(part):
                    act.wait_ge(v_ps, at(b, part))
                    if part >= 4:
                        act.wait_ge(pv_done, row_at(b, 2 * (part // 2) - 3, NT - 1))
                    t0 = 2 * (part % 2)
                    act.activation(v[0][:, (part // 2) % 2, t0:t0 + 2, :], ps_proj[:].rearrange("p (t n) -> p t n", t=2),
                                   ACT.Copy).then_inc(v_hi, 1)

            def exps(b, h, i):
                if real(h):
                    act.wait_ge(max_ready[i], at(b, h))
                    if h >= 2:
                        act.wait_ge(pT_ps, row_at(b, h - 2, i))
                    act.activation(probs[:, h % 2, P_AT[i]:P_AT[i + 1]], ps_s[i % 2][:, 0:TRI[i]], ACT.Exp,
                                   bias=nmax[:, h % 2, i:i + 1], accum_out=sums[:, h % 2, i:i + 1]).then_inc(exp_ready[i], 1)

            def high_pT(b, h, j):
                if real(h):
                    act.wait_ge(pT_ps, row_at(b, h, j))
                    if h >= 1:
                        act.wait_ge(pv_done, row_at(b, h - 1, j))
                    act.activation(pT[0][:, T_AT[j]:T_AT[j + 1]], ps_t[j % 2][:, 0:S - j * P], ACT.Copy).then_inc(pT_hi, 1)

            def high_z(b, h):
                if real(h):
                    act.wait_ge(pv_done, row_at(b, h, NT - 1))
                    if h >= 1:
                        act.wait_ge(o_done, at(b, h - 1))
                    act.activation(zT[0][:], ps_z[:], ACT.Identity, bias=bias[:, 2, h:h + 1]).then_inc(z_hi, 1)

            def high_wo(b, h):
                if real(h):
                    if h >= 2:
                        act.wait_ge(o_done, at(b, h - 2))
                    act.activation(wo_parts[0][:, h % 2, :], wo_sb[:, h, :], ACT.Copy).then_inc(wo_hi, 1)

            with act.Fori(0, B) as b:
                for c in range(NC):
                    act.wait_ge(xT_ps, NC * b + c + 1)
                    act.activation(xT[0][:, c, :], ps_xT[c][:], ACT.Copy).then_inc(xT_hi, 1)
                for s in range(-2, H1 + 2):
                    high_head(b, s, 1)
                    exps(b, s - 1, 2)
                    high_pT(b, s - 2, 2)
                    high_pT(b, s - 2, 3)
                    exps(b, s - 1, 3)
                    high_wo(b, s - 1)
                    raw_head(b, s + 1, 0)
                    high_z(b, s - 2)
                    raw_head(b, s + 1, 1)
                    exps(b, s, 0)
                    high_pT(b, s - 1, 0)
                    high_head(b, s + 1, 0)
                    high_pT(b, s - 1, 1)
                    exps(b, s, 1)
                    high_v(b, s + 1)

        @block.vector
        def _(dve):
            chain = Chain(dve, dve_steps)
            crossed, inverted = {}, {}
            dve.sem_inc(x_taken, 1)

            def cross_part(b, h, j):
                if real(h):
                    dve.wait_ge(qk_raw[j], at(b, h))
                    for to, frm in ((slice(0, ROT), slice(ROT, P)), (slice(ROT, P), slice(0, ROT))):
                        crossed[j] = chain.step(dve.tensor_tensor(cross[to, j, :], raw[frm, j, :], sinT[frm, :], ALU.mult))

            def turn_head(b, h, j):
                if real(h):
                    chain.done(crossed[j])
                    dve.wait_ge(qk_cos[j], at(b, h))
                    dve.tensor_tensor(turn[:, j, :], turn[:, j, :], cross[:, j, :], ALU.add).then_inc(qk_turned[j], 1)

            def low_v(b, part):
                if real(part):
                    dve.wait_ge(v_hi, at(b, part))
                    t0 = 2 * (part % 2)
                    dve.tensor_tensor(v[1][:, (part // 2) % 2, t0:t0 + 2, :], ps_proj[:].rearrange("p (t n) -> p t n", t=2),
                                      v[0][:, (part // 2) % 2, t0:t0 + 2, :].bitcast(F32), ALU.subtract).then_inc(v_lo, 1)

            def maxima(b, h, i):
                if real(h):
                    dve.wait_ge(scores_ps[i], at(b, h))
                    dve.tensor_reduce(nmax[:, h % 2, i:i + 1], ps_s[i % 2][:, 0:TRI[i]], AX.X, ALU.max,
                                      negate=True).then_inc(max_ready[i], 1)

            def invert(b, h, i):
                if real(h):
                    dve.wait_ge(exp_ready[i], at(b, h))
                    inverted[i] = chain.step(dve.reciprocal(rsum[:, h % 2, i:i + 1], sums[:, h % 2, i:i + 1]))

            def normalize(b, h, i):
                if real(h):
                    chain.done(inverted[i])
                    pr = probs[:, h % 2, P_AT[i]:P_AT[i + 1]]
                    dve.tensor_scalar(pr, pr, rsum[:, h % 2, i:i + 1], None, ALU.mult).then_inc(probs_ready[i], 1)

            def low_pT(b, h, j):
                if real(h):
                    dve.wait_ge(pT_hi, row_at(b, h, j))
                    dve.tensor_tensor(pT[1][:, T_AT[j]:T_AT[j + 1]], ps_t[j % 2][:, 0:S - j * P],
                                      pT[0][:, T_AT[j]:T_AT[j + 1]].bitcast(F32), ALU.subtract).then_inc(pT_lo, 1)

            def low_z(b, h):
                if real(h):
                    dve.wait_ge(z_hi, at(b, h))
                    dve.scalar_tensor_tensor(out=zT[1][:], in0=ps_z[:], scalar=bias[:, 2, h:h + 1],
                                             in1=zT[0][:].bitcast(F32), op0=ALU.add, op1=ALU.subtract).then_inc(z_lo, 1)

            with dve.Fori(0, B) as b:
                dve.wait_ge(x_loaded, 16 * (b + 1))
                layernorm_stats(dve, chain, x_in, ln)
                for t in range(NT):
                    dve.tensor_scalar(xn[:, t, :], x_in[:, t, :], ln["mv"][:, t, 0:1], ln["rstd"][:, t:t + 1],
                                      ALU.subtract, ALU.mult).then_inc(xn_ready, 1)
                for c in range(NC):
                    dve.wait_ge(xT_hi, NC * b + c + 1)
                    dve.tensor_tensor(xT[1][:, c, :], ps_xT[c][:], xT[0][:, c, :].bitcast(F32),
                                      ALU.subtract).then_inc(xT_lo, 1)
                dve.wait_ge(x_out_free, b + 1)
                dve.tensor_tensor(x_res[:], x_in[:], bo_sb[:].unsqueeze(1).to_broadcast([P, NT, D]),
                                  ALU.add).then_inc(x_taken, 1)
                for s in range(-2, H1 + 2):
                    low_v(b, s)
                    maxima(b, s - 1, 3)
                    invert(b, s - 1, 1)
                    normalize(b, s - 1, 0)
                    invert(b, s - 1, 2)
                    low_pT(b, s - 2, 2)
                    low_pT(b, s - 2, 3)
                    normalize(b, s - 1, 2)
                    normalize(b, s - 1, 1)
                    invert(b, s - 1, 3)
                    normalize(b, s - 1, 3)
                    maxima(b, s, 0)
                    cross_part(b, s + 1, 0)
                    maxima(b, s, 1)
                    low_z(b, s - 2)
                    turn_head(b, s + 1, 0)
                    cross_part(b, s + 1, 1)
                    invert(b, s, 0)
                    low_pT(b, s - 1, 0)
                    turn_head(b, s + 1, 1)
                    low_pT(b, s - 1, 1)
                    maxima(b, s, 2)
                for u in range(2):
                    dve.wait_ge(o_done, at(b, H1 - 1))
                    dve.tensor_tensor(x_res[:, 2 * u:2 * u + 2, :], ps_o[u][:], x_res[:, 2 * u:2 * u + 2, :],
                                      ALU.add).then_inc(y_ready, 1)
                chain.restart()

        @block.tensor
        def _(pe):
            def project(b, h, j):
                if not real(h):
                    return
                if j == 1:
                    pe.wait_ge(qk_raw[0], at(b, h))
                elif h >= 1:
                    pe.wait_ge(v_lo, at(b, h - 1))
                k = 0
                for c in range(NC):
                    for a, m in PASSES:
                        last = pe.matmul(ps_proj[:], w_parts[a][:, 1 - j, c, h * HD1:(h + 1) * HD1], xT[m][:, c, :],
                                         start=(k == 0), stop=(k == 3 * NC - 1))
                        k += 1
                last.then_inc(qk_ps[j], 1)

            def project_v(b, part):
                if not real(part):
                    return
                pe.wait_ge(qk_raw[1], at(b, part))
                n0 = (part // 2) * 2 * HD1
                for u in range(2):
                    t = 2 * (part % 2) + u
                    k = 0
                    for c in range(NC):
                        for a, m in PASSES:
                            last = pe.matmul(ps_proj[:, u * 2 * HD1:(u + 1) * 2 * HD1], xT[a][:, c, t * P:(t + 1) * P],
                                             w_parts[m][:, 2, c, n0:n0 + 2 * HD1], start=(k == 0), stop=(k == 3 * NC - 1))
                            k += 1
                last.then_inc(v_ps, 1)

            def scores(b, h, i):
                if not real(h):
                    return
                for j in range(2):
                    pe.wait_ge(qk_lo[j], at(b, h))
                if i >= 2:
                    pe.wait_ge(exp_ready[i - 2], at(b, h))
                elif h >= 1:
                    pe.wait_ge(exp_ready[i + 2], at(b, h - 1))
                for k, (a, m) in enumerate(PASSES):
                    pe.matmul(ps_s[i % 2][:, 0:TRI[i]], qkT[a][:, h % 2, 1, i * P:(i + 1) * P],
                              qkT[m][:, h % 2, 0, 0:TRI[i]], start=(k == 0), stop=False)
                pe.matmul(ps_s[i % 2][:, i * P:TRI[i]], ident_b[:], causal[:], start=False,
                          stop=True).then_inc(scores_ps[i], 1)

            def transposes(b, h, j):
                if not real(h):
                    return
                for i in range(j, NT):
                    pe.wait_ge(probs_ready[i], at(b, h))
                if j >= 2:
                    pe.wait_ge(pT_lo, row_at(b, h, j - 2))
                elif h >= 1:
                    pe.wait_ge(pT_lo, row_at(b, h - 1, j + 2))
                for i in range(j, NT):
                    last = pe.transpose(ps_t[j % 2][:, (i - j) * P:(i - j + 1) * P],
                                        probs[:, h % 2, P_AT[i] + j * P:P_AT[i] + (j + 1) * P], ident[:])
                last.then_inc(pT_ps, 1)

            def values(b, h, j):
                if not real(h):
                    return
                pe.wait_ge(pT_lo, row_at(b, h, j))
                if j == 0:
                    pe.wait_ge(v_lo, at(b, 2 * (h // 2) + 1))
                    if h >= 1:
                        pe.wait_ge(z_lo, at(b, h - 1))
                for k, (a, m) in enumerate(PASSES):
                    last = pe.matmul(ps_z[:, j * P:S], v[a][:, (h // 2) % 2, j, (h % 2) * HD1:(h % 2 + 1) * HD1],
                                     pT[m][:, T_AT[j]:T_AT[j + 1]], start=(j == 0 and k == 0),
                                     stop=(j == NT - 1 and k == 2), skip_group_check=True)
                last.then_inc(pv_done, 1)

            def outputs(b, h):
                if not real(h):
                    return
                pe.wait_ge(z_lo, at(b, h))
                pe.wait_ge(wo_lo, at(b, h))
                for t in range(NT):
                    for k, (a, m) in enumerate(PASSES):
                        last = pe.matmul(ps_o[t // 2][:, t % 2, :], zT[a][:, t * P:(t + 1) * P],
                                         wo_parts[m][:, h % 2, :], start=(h == 0 and k == 0 and t % 2 == 0),
                                         stop=(h == H1 - 1 and k == 2), skip_group_check=True)
                last.then_inc(o_done, 1)

            with pe.Fori(0, B) as b:
                for c in range(NC):
                    for t in range(NT):
                        pe.wait_ge(xn_ready, NT * b + t + 1)
                        last = pe.transpose(ps_xT[c][:, t * P:(t + 1) * P], xn[:, t, c * P:(c + 1) * P], ident[:])
                    last.then_inc(xT_ps, 1)
                pe.wait_ge(xT_lo, NC * (b + 1))
                for s in range(-2, H1 + 2):
                    scores(b, s, 0)
                    values(b, s - 2, 2)
                    values(b, s - 2, 3)
                    project(b, s + 1, 1)
                    transposes(b, s - 1, 0)
                    transposes(b, s - 1, 1)
                    project_v(b, s + 1)
                    scores(b, s, 2)
                    outputs(b, s - 2)
                    scores(b, s, 3)
                    transposes(b, s - 1, 2)
                    transposes(b, s - 1, 3)
                    values(b, s - 1, 0)
                    values(b, s - 1, 1)
                    project(b, s + 2, 0)
                    scores(b, s + 1, 1)

E, TOP_K = 8, 2


def router_buffers(sb):
    names = {n: sb(f"r_{n}", [P, NT, E], F32) for n in ("logits", "e", "p", "rank", "mask", "w")}
    names.update({n: sb(f"r_{n}", [P, NT], F32) for n in ("max", "sum", "rsum")})
    names.update({n: sb(f"r_{n}", [P, NT, E, E], F32) for n in ("gt", "ge")})
    return names


def over_experts(v):
    return v.unsqueeze(2).to_broadcast([P, NT, E])


def top_k_mask(dve, chain, r, before):
    mine = r["p"][:].unsqueeze(3).to_broadcast([P, NT, E, E])
    other = r["p"][:].unsqueeze(2).to_broadcast([P, NT, E, E])
    chain.step(dve.tensor_tensor(r["gt"][:], other, mine, ALU.is_gt))
    chain.step(dve.tensor_tensor(r["ge"][:], other, mine, ALU.is_ge))
    chain.done()
    for t in range(NT):
        chain.step(dve.tensor_tensor(r["ge"][:, t, :, :], r["ge"][:, t, :, :], before[:], ALU.mult))
    chain.done()
    chain.step(dve.tensor_tensor(r["gt"][:], r["gt"][:], r["ge"][:], ALU.max))
    chain.done()
    chain.step(dve.tensor_reduce(r["rank"][:], r["gt"][:], AX.X, ALU.add))
    chain.done()
    chain.step(dve.tensor_scalar(r["mask"][:], r["rank"][:], TOP_K - 0.5, None, ALU.is_lt))
    chain.done()


def normalized(dve, chain, r, dst, v):
    chain.step(dve.tensor_reduce(r["sum"][:], v, AX.X, ALU.add))
    chain.done()
    chain.step(dve.reciprocal(r["rsum"][:], r["sum"][:]))
    chain.done()
    return dve.tensor_tensor(dst, v, over_experts(r["rsum"][:]), ALU.mult)


def make_before(pool, chain, m):
    chain.step(pool.memset(m, 1.0))
    chain.done()
    chain.step(pool.affine_select(out=m, in_=m, compare_op=ALU.is_gt, fill=0.0, base=0,
                                  pattern=[[1, E], [-1, E]], channel_multiplier=0))


HF = 176
NE0 = E + 1
FCH = -(-NE0 * HF // P)
FPAD = FCH * P
GROUP = S // P


def experts0(nc, x, wg, wu, wd, wgs, wus, wds, wr, br, rb, out):
    ctx = ExitStack()
    with ctx:
        def sb(name, shape, dt, stack=ctx):
            return stack.enter_context(nc.sbuf_tensor(f"b_{name}", shape, dt))

        def pb(name, shape, dt):
            return ctx.enter_context(nc.psum_tensor(f"b_{name}", shape, dt))

        def sem(name):
            return ctx.enter_context(nc.semaphore(f"b_{name}"))

        wgu = [sb(f"wgu{k}", [P, NC, NE0, 2 * HF], F32R) for k in range(2)]
        wdn = [sb(f"wdn{k}", [P, FCH, D], F32R) for k in range(2)]
        wrt = [sb(f"wrt{k}", [P, NC, E], F32R) for k in range(2)]
        ident = sb("ident", [P, P], F32)
        before = sb("before", [P, E, E], F32)
        rbias = sb("rbias", [P, 2, E], F32)

        loaded = [sem(f"loaded{i}") for i in range(4)]
        setup_hi = sem("setup_hi")
        setup_lo = sem("setup_lo")
        setup_pool = sem("setup_pool")
        cleared = sem("cleared")

        with ExitStack() as setup:
            wgu_in = sb("wgu_in", [P, NC, NE0, 2 * HF], F32, setup)
            wdn_in = sb("wdn_in", [P, FCH, D], F32, setup)
            wrt_in = sb("wrt_in", [P, NC, E], F32, setup)
            block = setup.enter_context(nc.Block())
            full = E * HF // P
            rest = NE0 * HF - full * P

            @block.sync
            def _(sp):
                for c in range(NC):
                    rows = slice(c * P, (c + 1) * P)
                    sp.dma_start(wgu_in[:, c, 0:E, 0:HF], wg[:, rows, :].rearrange("e p h -> p e h")).then_inc(loaded[0], 16)
                    sp.dma_start(wgu_in[:, c, 0:E, HF:2 * HF], wu[:, rows, :].rearrange("e p h -> p e h")).then_inc(loaded[0], 16)
                    sp.dma_start(wgu_in[:, c, E, 0:HF], wgs[rows, :]).then_inc(loaded[0], 16)
                    sp.dma_start(wgu_in[:, c, E, HF:2 * HF], wus[rows, :]).then_inc(loaded[0], 16)
                sp.wait_ge(cleared, 1)
                sp.dma_start(wdn_in[:, 0:full, :], wd.rearrange("e h d -> (e h) d").rearrange("(k p) d -> p k d", p=P)).then_inc(loaded[1], 16)
                sp.dma_start(wdn_in[:, full, :], wds[0:P, :]).then_inc(loaded[1], 16)
                sp.dma_start(wdn_in[0:rest - P, full + 1, :], wds[P:HF, :]).then_inc(loaded[1], 16)
                sp.dma_start(wrt_in[:], wr.rearrange("(c p) e -> p c e", p=P)).then_inc(loaded[2], 16)
                sp.dma_start(rbias[:, 0, :], row_to_all(br)).then_inc(loaded[3], 16)
                sp.dma_start(rbias[:, 1, :], row_to_all(rb)).then_inc(loaded[3], 16)

            @block.gpsimd
            def _(pool):
                chain = Chain(pool, setup_pool)
                make_identity(pool, chain, ident[:])
                make_before(pool, chain, before[:])
                chain.done()

            parts = ((wgu, wgu_in, 0, 16 * 4 * NC), (wdn, wdn_in, 1, 16 * 3), (wrt, wrt_in, 2, 16))

            @block.scalar
            def _(act):
                for w, w_in, k, n in parts:
                    act.wait_ge(loaded[k], n)
                    act.activation(w[0][:], w_in[:], ACT.Copy).then_inc(setup_hi, 1)

            @block.vector
            def _(dve):
                dve.memset(wdn_in[:, full + 1, :], 0.0).then_inc(cleared, 1)
                for i, (w, w_in, k, n) in enumerate(parts):
                    dve.wait_ge(setup_hi, i + 1)
                    dve.tensor_tensor(w[1][:], w_in[:], w[0][:].bitcast(F32), ALU.subtract).then_inc(setup_lo, 1)
                dve.wait_ge(loaded[3], 32)
                dve.tensor_tensor(rbias[:, 0, :], rbias[:, 0, :], rbias[:, 1, :], ALU.add).then_inc(setup_lo, 1)

        x_in = sb("x_in", [P, NT, D], F32)
        x_res = sb("x_res", [P, NT, D], F32)
        x_out = sb("x_out", [P, NT, D], F32)
        xn = sb("xn", [P, NT, D], F32)
        ln = layernorm_buffers(sb, "b")
        r = router_buffers(sb)
        xT = [sb(f"xT{k}", [P, NC, S], F32R) for k in range(2)]
        act_g = sb("act_g", [P, 2, HF], F32)
        hid = sb("hid", [P, 2, FPAD], F32)
        hT = [sb(f"hT{k}", [P, FCH, P], F32R) for k in range(2)]

        ps_gu = [pb(f"ps_gu{i}", [P, S], F32) for i in range(4)]
        ps_t = [pb(f"ps_t{i}", [P, GROUP, P], F32) for i in range(2)]
        ps_y = [pb(f"ps_y{i}", [P, S], F32) for i in range(2)]
        ps_xT = ps_gu[0:2]
        ps_r = ps_gu[2]

        x_loaded = sem("x_loaded")
        x_taken = sem("x_taken")
        xn_ready = sem("xn_ready")
        xT_ps = sem("xT_ps")
        xT_hi = sem("xT_hi")
        xT_lo = sem("xT_lo")
        router_ps = sem("router_ps")
        logits_ready = sem("logits_ready")
        odds_ready = sem("odds_ready")
        gu_ps = sem("gu_ps")
        silu_ready = sem("silu_ready")
        hid_ready = sem("hid_ready")
        hT_ps = sem("hT_ps")
        hT_hi = sem("hT_hi")
        hT_lo = sem("hT_lo")
        y_ps = sem("y_ps")
        y_ready = sem("y_ready")
        x_out_free = sem("x_out_free")
        stored = sem("stored")
        dve_steps = sem("dve_steps")

        order = [E] + list(range(E))
        n_groups = -(-FCH // GROUP)
        groups = [range(g * GROUP, min(FCH, (g + 1) * GROUP)) for g in range(n_groups)]
        block = ctx.enter_context(nc.Block())

        @block.sync
        def _(sp):
            with sp.Fori(0, B) as b:
                sp.wait_ge(x_taken, b + 1)
                sp.dma_start(x_in[:], token_tiles(x, b)).then_inc(x_loaded, 16)

        @block.gpsimd
        def _(pool):
            pool.sem_inc(x_out_free, 1)
            with pool.Fori(0, B) as b:
                pool.wait_ge(y_ready, NT * b + NT)
                pool.dma_start(token_tiles(out, b), x_out[:]).then_inc(stored, 16)
                pool.wait_ge(stored, 16 * (b + 1))
                pool.sem_inc(x_out_free, 1)

        @block.scalar
        def _(act):
            def high_hT(b, t, g):
                act.wait_ge(hT_ps, n_groups * (NT * b + t) + g + 1)
                k = groups[g]
                act.activation(hT[0][:, k.start:k.stop, :], ps_t[g % 2][:, 0:len(k), :], ACT.Copy).then_inc(hT_hi, 1)

            with act.Fori(0, B) as b:
                for c in range(NC):
                    act.wait_ge(xT_ps, NC * b + c + 1)
                    act.activation(xT[0][:, c, :], ps_xT[c][:], ACT.Copy).then_inc(xT_hi, 1)
                act.wait_ge(logits_ready, b + 1)
                act.activation(r["e"][:], r["logits"][:], ACT.Exp, scale=-1.0).then_inc(odds_ready, 1)
                for t in range(NT + 1):
                    for n in range(NE0):
                        if t < NT:
                            step = NE0 * t + n
                            act.wait_ge(gu_ps, NE0 * NT * b + step + 1)
                            if step >= 2:
                                act.wait_ge(hid_ready, NE0 * NT * b + step - 1)
                            act.activation(act_g[:, step % 2, :], ps_gu[step % 4][:, 0:HF], ACT.Silu).then_inc(silu_ready, 1)
                        if t >= 1 and n < n_groups:
                            high_hT(b, t - 1, n)

        @block.vector
        def _(dve):
            chain = Chain(dve, dve_steps)
            dve.sem_inc(x_taken, 1)
            chain.step(dve.memset(hid[:], 0.0))
            chain.restart()

            def low_hT(b, t, g):
                dve.wait_ge(hT_hi, n_groups * (NT * b + t) + g + 1)
                k = groups[g]
                dve.tensor_tensor(hT[1][:, k.start:k.stop, :], ps_t[g % 2][:, 0:len(k), :],
                                  hT[0][:, k.start:k.stop, :].bitcast(F32), ALU.subtract).then_inc(hT_lo, 1)

            with dve.Fori(0, B) as b:
                dve.wait_ge(x_loaded, 16 * (b + 1))
                layernorm_stats(dve, chain, x_in, ln)
                for t in range(NT):
                    dve.tensor_scalar(xn[:, t, :], x_in[:, t, :], ln["mv"][:, t, 0:1], ln["rstd"][:, t:t + 1],
                                      ALU.subtract, ALU.mult).then_inc(xn_ready, 1)
                for c in range(NC):
                    dve.wait_ge(xT_hi, NC * b + c + 1)
                    dve.tensor_tensor(xT[1][:, c, :], ps_xT[c][:], xT[0][:, c, :].bitcast(F32),
                                      ALU.subtract).then_inc(xT_lo, 1)
                dve.tensor_copy(x_res[:], x_in[:]).then_inc(x_taken, 1)
                dve.wait_ge(router_ps, b + 1)
                dve.tensor_tensor(r["logits"][:], ps_r[:, 0:NT * E].rearrange("p (t e) -> p t e", e=E),
                                  rbias[:, 0, :].unsqueeze(1).to_broadcast([P, NT, E]), ALU.add).then_inc(logits_ready, 1)
                dve.wait_ge(odds_ready, b + 1)
                chain.step(dve.tensor_scalar(r["e"][:], r["e"][:], 1.0, None, ALU.add))
                chain.done()
                chain.step(dve.reciprocal(r["p"][:], r["e"][:]))
                chain.done()
                top_k_mask(dve, chain, r, before)
                chain.step(dve.tensor_tensor(r["e"][:], r["p"][:], r["mask"][:], ALU.mult))
                chain.done()
                chain.step(normalized(dve, chain, r, r["w"][:], r["e"][:]))
                chain.done()
                for t in range(NT + 1):
                    for n, e in enumerate(order):
                        if t < NT:
                            step = NE0 * t + n
                            dve.wait_ge(silu_ready, NE0 * NT * b + step + 1)
                            dst = hid[:, t % 2, e * HF:(e + 1) * HF]
                            if n == 0 and t >= 2:
                                dve.wait_ge(hT_ps, n_groups * (NT * b + t - 1))
                            up = ps_gu[step % 4][:, HF:2 * HF]
                            if e == E:
                                dve.tensor_tensor(dst, act_g[:, step % 2, :], up, ALU.mult).then_inc(hid_ready, 1)
                            else:
                                dve.scalar_tensor_tensor(out=dst, in0=act_g[:, step % 2, :], scalar=r["w"][:, t, e:e + 1],
                                                         in1=up, op0=ALU.mult, op1=ALU.mult).then_inc(hid_ready, 1)
                        if t >= 1 and n < n_groups:
                            low_hT(b, t - 1, n)
                        if t >= 1 and n == n_groups + 1:
                            if t == 1:
                                dve.wait_ge(x_out_free, b + 1)
                            dve.wait_ge(y_ps, NT * b + t)
                            dve.tensor_tensor(x_out[:, t - 1, :], ps_y[(t - 1) % 2][:, 0:D], x_res[:, t - 1, :],
                                              ALU.add).then_inc(y_ready, 1)
                chain.restart()

        @block.tensor
        def _(pe):
            def gate_up(b, step):
                t, n = step // NE0, step % NE0
                if step >= 4:
                    pe.wait_ge(hid_ready, NE0 * NT * b + step - 3)
                elif step == 2:
                    pe.wait_ge(logits_ready, b + 1)
                k = 0
                for c in range(NC):
                    for a, m in PASSES:
                        last = pe.matmul(ps_gu[step % 4][:, 0:2 * HF], xT[a][:, c, t * P:(t + 1) * P],
                                         wgu[m][:, c, order[n], :], start=(k == 0), stop=(k == 3 * NC - 1))
                        k += 1
                last.then_inc(gu_ps, 1)

            def transposes(b, t, g):
                if g == 0:
                    pe.wait_ge(hid_ready, NE0 * (NT * b + t + 1))
                if g >= 2 or t >= 1:
                    pe.wait_ge(hT_lo, n_groups * (NT * b + t) + g - 1)
                for k in groups[g]:
                    last = pe.transpose(ps_t[g % 2][:, k - groups[g].start, :], hid[:, t % 2, k * P:(k + 1) * P], ident[:])
                last.then_inc(hT_ps, 1)

            def down(b, t, g):
                pe.wait_ge(hT_lo, n_groups * (NT * b + t) + g + 1)
                if g == 0 and t >= 2:
                    pe.wait_ge(y_ready, NT * b + t - 1)
                for k in groups[g]:
                    for j, (a, m) in enumerate(PASSES):
                        last = pe.matmul(ps_y[t % 2][:, 0:D], hT[a][:, k, :], wdn[m][:, k, :],
                                         start=(k == 0 and j == 0), stop=(k == FCH - 1 and j == 2))
                if g == n_groups - 1:
                    last.then_inc(y_ps, 1)

            with pe.Fori(0, B) as b:
                for c in range(NC):
                    for t in range(NT):
                        pe.wait_ge(xn_ready, NT * b + t + 1)
                        last = pe.transpose(ps_xT[c][:, t * P:(t + 1) * P], xn[:, t, c * P:(c + 1) * P], ident[:])
                    last.then_inc(xT_ps, 1)
                pe.wait_ge(xT_lo, NC * (b + 1))
                for t in range(NT):
                    k = 0
                    for c in range(NC):
                        for a, m in PASSES:
                            last = pe.matmul(ps_r[:, t * E:(t + 1) * E], xT[a][:, c, t * P:(t + 1) * P], wrt[m][:, c, :],
                                             start=(k == 0), stop=(k == 3 * NC - 1))
                            k += 1
                last.then_inc(router_ps, 1)
                for t in range(NT + 1):
                    for n in range(NE0):
                        if t < NT:
                            gate_up(b, NE0 * t + n)
                        if t >= 1 and n < n_groups:
                            transposes(b, t - 1, n)
                        if t >= 1 and 1 <= n <= n_groups:
                            down(b, t - 1, n - 1)


FW = 128


def experts1(nc, x, wr, w1, b1, w2, b2, out):
    ctx = ExitStack()
    with ctx:
        def sb(name, shape, dt, stack=ctx):
            return stack.enter_context(nc.sbuf_tensor(f"d_{name}", shape, dt))

        def pb(name, shape, dt):
            return ctx.enter_context(nc.psum_tensor(f"d_{name}", shape, dt))

        def sem(name):
            return ctx.enter_context(nc.semaphore(f"d_{name}"))

        wup = [sb(f"wup{k}", [P, NC, E, FW], F32R) for k in range(2)]
        wdn = [sb(f"wdn{k}", [P, E, D], F32R) for k in range(2)]
        wrt = [sb(f"wrt{k}", [P, NC, E], F32R) for k in range(2)]
        b2p = [sb(f"b2p{k}", [P, D], F32R) for k in range(2)]
        sel = sb("sel", [P, E, P], F32R)
        b1_sb = sb("b1", [P, E], F32)
        ident = sb("ident", [P, P], F32)
        before = sb("before", [P, E, E], F32)

        loaded = [sem(f"loaded{i}") for i in range(5)]
        setup_hi = sem("setup_hi")
        setup_lo = sem("setup_lo")
        setup_pool = sem("setup_pool")
        cleared = sem("cleared")

        with ExitStack() as setup:
            wup_in = sb("wup_in", [P, NC, E, FW], F32, setup)
            wdn_in = sb("wdn_in", [P, E, D], F32, setup)
            wrt_in = sb("wrt_in", [P, NC, E], F32, setup)
            b2_in = sb("b2_in", [P, D], F32, setup)
            sel_in = sb("sel_in", [P, E, P], F32, setup)
            block = setup.enter_context(nc.Block())

            @block.sync
            def _(sp):
                for c in range(NC):
                    sp.dma_start(wup_in[:, c, :, :], w1[:, c * P:(c + 1) * P, :].rearrange("e p f -> p e f")).then_inc(loaded[0], 16)
                sp.dma_start(wdn_in[:], w2.rearrange("e f d -> f e d")).then_inc(loaded[1], 16)
                sp.dma_start(wrt_in[:], wr.rearrange("(c p) e -> p c e", p=P)).then_inc(loaded[2], 16)
                sp.dma_start(b1_sb[:], b1).then_inc(loaded[4], 16)
                sp.wait_ge(cleared, 1)
                sp.dma_start(b2_in[0:E, :], b2).then_inc(loaded[3], 16)
                sp.wait_ge(loaded[4], 16)

            @block.gpsimd
            def _(pool):
                chain = Chain(pool, setup_pool)
                make_identity(pool, chain, ident[:])
                make_before(pool, chain, before[:])
                chain.step(pool.memset(sel_in[:], 0.0))
                chain.done()
                chain.step(pool.affine_select(out=sel_in[:], in_=sel_in[:], compare_op=ALU.not_equal, fill=1.0, base=0,
                                              pattern=[[-1, E], [0, P]], channel_multiplier=1))
                chain.done()

            parts = ((wup, wup_in, 0, 16 * NC), (wdn, wdn_in, 1, 16), (wrt, wrt_in, 2, 16), (b2p, b2_in, 3, 16))

            @block.scalar
            def _(act):
                for w, w_in, k, n in parts:
                    act.wait_ge(loaded[k], n)
                    act.activation(w[0][:], w_in[:], ACT.Copy).then_inc(setup_hi, 1)
                act.wait_ge(setup_pool, 6)
                act.activation(sel[:], sel_in[:], ACT.Copy).then_inc(setup_hi, 1)

            @block.vector
            def _(dve):
                dve.memset(b2_in[:], 0.0).then_inc(cleared, 1)
                for i, (w, w_in, k, n) in enumerate(parts):
                    dve.wait_ge(setup_hi, i + 1)
                    dve.tensor_tensor(w[1][:], w_in[:], w[0][:].bitcast(F32), ALU.subtract).then_inc(setup_lo, 1)

        x_in = sb("x_in", [P, NT, D], F32)
        x_res = sb("x_res", [P, NT, D], F32)
        x_out = sb("x_out", [P, NT, D], F32)
        xn = sb("xn", [P, NT, D], F32)
        ln = layernorm_buffers(sb, "d")
        r = router_buffers(sb)
        shares = sb("shares", [P, NT, P], F32)
        shT = [sb(f"shT{k}", [P, S], F32R) for k in range(2)]
        xT = [sb(f"xT{k}", [P, NC, S], F32R) for k in range(2)]
        gel = sb("gel", [P, 2, S], F32)
        hid = sb("hid", [P, 2, S], F32)
        hid_parts = [sb(f"hid{k}", [P, 2, S], F32R) for k in range(2)]

        ps_u = [pb(f"ps_u{i}", [P, S], F32) for i in range(2)]
        ps_c = [pb(f"ps_c{i}", [P, S], F32) for i in range(2)]
        ps_y = [pb(f"ps_y{i}", [P, 2, D], F32) for i in range(2)]
        ps_m = [pb(f"ps_m{i}", [P, S], F32) for i in range(2)]

        x_loaded = sem("x_loaded")
        x_taken = sem("x_taken")
        xn_ready = sem("xn_ready")
        xT_ps = sem("xT_ps")
        xT_hi = sem("xT_hi")
        xT_lo = sem("xT_lo")
        router_ps = sem("router_ps")
        shifted_ready = sem("shifted_ready")
        exp_ready = sem("exp_ready")
        shares_ready = sem("shares_ready")
        shT_ps = sem("shT_ps")
        shT_hi = sem("shT_hi")
        shT_lo = sem("shT_lo")
        u_ps = sem("u_ps")
        gelu_ready = sem("gelu_ready")
        c_ps = sem("c_ps")
        hid_ready = sem("hid_ready")
        hid_hi = sem("hid_hi")
        hid_lo = sem("hid_lo")
        down_done = sem("down_done")
        y_ready = sem("y_ready")
        x_out_free = sem("x_out_free")
        stored = sem("stored")
        dve_steps = sem("dve_steps")

        block = ctx.enter_context(nc.Block())

        @block.sync
        def _(sp):
            with sp.Fori(0, B) as b:
                sp.wait_ge(x_taken, b + 1)
                sp.dma_start(x_in[:], token_tiles(x, b)).then_inc(x_loaded, 16)

        @block.gpsimd
        def _(pool):
            pool.sem_inc(x_out_free, 1)
            with pool.Fori(0, B) as b:
                pool.wait_ge(y_ready, 2 * b + 2)
                pool.dma_start(token_tiles(out, b), x_out[:]).then_inc(stored, 16)
                pool.wait_ge(stored, 16 * (b + 1))
                pool.sem_inc(x_out_free, 1)

        @block.scalar
        def _(act):
            with act.Fori(0, B) as b:
                for c in range(NC):
                    act.wait_ge(xT_ps, NC * b + c + 1)
                    act.activation(xT[0][:, c, :], ps_m[c][:], ACT.Copy).then_inc(xT_hi, 1)
                for k in range(2):
                    act.wait_ge(shifted_ready, 2 * b + k + 1)
                    act.activation(r["e"][:], r["logits"][:], ACT.Exp).then_inc(exp_ready, 1)
                act.wait_ge(shT_ps, b + 1)
                act.activation(shT[0][:], ps_m[1][:], ACT.Copy).then_inc(shT_hi, 1)
                for e in range(E + 1):
                    if e < E:
                        act.wait_ge(u_ps, E * b + e + 1)
                        if e >= 2:
                            act.wait_ge(hid_ready, E * b + e - 1)
                        act.activation(gel[:, e % 2, :], ps_u[e % 2][:], ACT.Gelu, bias=b1_sb[:, e:e + 1]).then_inc(gelu_ready, 1)
                    if e >= 1:
                        act.wait_ge(hid_ready, E * b + e)
                        if e >= 3:
                            act.wait_ge(down_done, E * b + e - 2)
                        act.activation(hid_parts[0][:, (e - 1) % 2, :], hid[:, (e - 1) % 2, :], ACT.Copy).then_inc(hid_hi, 1)

        @block.vector
        def _(dve):
            chain = Chain(dve, dve_steps)
            dve.sem_inc(x_taken, 1)
            chain.step(dve.memset(shares[:], 0.0))
            chain.restart()

            with dve.Fori(0, B) as b:
                dve.wait_ge(x_loaded, 16 * (b + 1))
                layernorm_stats(dve, chain, x_in, ln)
                for t in range(NT):
                    dve.tensor_scalar(xn[:, t, :], x_in[:, t, :], ln["mv"][:, t, 0:1], ln["rstd"][:, t:t + 1],
                                      ALU.subtract, ALU.mult).then_inc(xn_ready, 1)
                for c in range(NC):
                    dve.wait_ge(xT_hi, NC * b + c + 1)
                    dve.tensor_tensor(xT[1][:, c, :], ps_m[c][:], xT[0][:, c, :].bitcast(F32),
                                      ALU.subtract).then_inc(xT_lo, 1)
                dve.tensor_copy(x_res[:], x_in[:]).then_inc(x_taken, 1)
                dve.wait_ge(router_ps, b + 1)
                lg = ps_m[0][:, 0:NT * E].rearrange("p (t e) -> p t e", e=E)
                chain.step(dve.tensor_reduce(r["max"][:], lg, AX.X, ALU.max))
                chain.done()
                dve.tensor_tensor(r["logits"][:], lg, over_experts(r["max"][:]), ALU.subtract).then_inc(shifted_ready, 1)
                dve.wait_ge(exp_ready, 2 * b + 1)
                chain.step(normalized(dve, chain, r, r["p"][:], r["e"][:]))
                chain.done()
                top_k_mask(dve, chain, r, before)
                chain.step(dve.tensor_reduce(r["max"][:], r["p"][:], AX.X, ALU.max))
                chain.done()
                dve.tensor_tensor(r["logits"][:], r["p"][:], over_experts(r["max"][:]), ALU.subtract).then_inc(shifted_ready, 1)
                dve.wait_ge(exp_ready, 2 * b + 2)
                chain.step(dve.tensor_tensor(r["w"][:], r["e"][:], r["mask"][:], ALU.mult))
                chain.done()
                normalized(dve, chain, r, shares[:, :, 0:E], r["w"][:]).then_inc(shares_ready, 1)
                dve.wait_ge(shT_hi, b + 1)
                dve.tensor_tensor(shT[1][:], ps_m[1][:], shT[0][:].bitcast(F32), ALU.subtract).then_inc(shT_lo, 1)
                for e in range(E + 1):
                    if e < E:
                        dve.wait_ge(gelu_ready, E * b + e + 1)
                        dve.wait_ge(c_ps, E * b + e + 1)
                        if e >= 2:
                            dve.wait_ge(hid_hi, E * b + e - 1)
                        dve.tensor_tensor(hid[:, e % 2, :], gel[:, e % 2, :], ps_c[e % 2][:], ALU.mult).then_inc(hid_ready, 1)
                    if e >= 1:
                        dve.wait_ge(hid_hi, E * b + e)
                        dve.tensor_tensor(hid_parts[1][:, (e - 1) % 2, :], hid[:, (e - 1) % 2, :],
                                          hid_parts[0][:, (e - 1) % 2, :].bitcast(F32), ALU.subtract).then_inc(hid_lo, 1)
                dve.wait_ge(x_out_free, b + 1)
                dve.wait_ge(down_done, E * (b + 1))
                for u in range(2):
                    dve.tensor_tensor(x_out[:, 2 * u:2 * u + 2, :], ps_y[u][:], x_res[:, 2 * u:2 * u + 2, :],
                                      ALU.add).then_inc(y_ready, 1)
                chain.restart()

        @block.tensor
        def _(pe):
            def up(b, e):
                if e >= 2:
                    pe.wait_ge(gelu_ready, E * b + e - 1)
                k = 0
                for c in range(NC):
                    for a, m in PASSES:
                        last = pe.matmul(ps_u[e % 2][:], wup[a][:, c, e, :], xT[m][:, c, :], start=(k == 0), stop=(k == 3 * NC - 1))
                        k += 1
                last.then_inc(u_ps, 1)

            def spread(b, e):
                if e >= 2:
                    pe.wait_ge(hid_ready, E * b + e - 1)
                for m in range(2):
                    last = pe.matmul(ps_c[e % 2][:], sel[:, e, :], shT[m][:], start=(m == 0), stop=(m == 1))
                last.then_inc(c_ps, 1)

            def down(b, e):
                pe.wait_ge(hid_lo, E * b + e + 1)
                for t in range(NT):
                    for k, (a, m) in enumerate(PASSES):
                        last = pe.matmul(ps_y[t // 2][:, t % 2, :], hid_parts[a][:, e % 2, t * P:(t + 1) * P], wdn[m][:, e, :],
                                         start=False, stop=(e == E - 1 and k == 2), skip_group_check=True)
                last.then_inc(down_done, 1)

            with pe.Fori(0, B) as b:
                for c in range(NC):
                    for t in range(NT):
                        pe.wait_ge(xn_ready, NT * b + t + 1)
                        last = pe.transpose(ps_m[c][:, t * P:(t + 1) * P], xn[:, t, c * P:(c + 1) * P], ident[:])
                    last.then_inc(xT_ps, 1)
                pe.wait_ge(xT_lo, NC * (b + 1))
                for t in range(NT):
                    k = 0
                    for c in range(NC):
                        for a, m in PASSES:
                            last = pe.matmul(ps_m[0][:, t * E:(t + 1) * E], xT[a][:, c, t * P:(t + 1) * P], wrt[m][:, c, :],
                                             start=(k == 0), stop=(k == 3 * NC - 1))
                            k += 1
                last.then_inc(router_ps, 1)
                up(b, 0)
                up(b, 1)
                pe.wait_ge(shares_ready, b + 1)
                for t in range(NT):
                    last = pe.transpose(ps_m[1][:, t * P:(t + 1) * P], shares[:, t, :], ident[:])
                last.then_inc(shT_ps, 1)
                pe.wait_ge(shT_lo, b + 1)
                for t in range(NT):
                    for k, (a, m) in enumerate(PASSES):
                        pe.matmul(ps_y[t // 2][:, t % 2, :], shT[a][:, t * P:(t + 1) * P], b2p[m][:],
                                  start=(k == 0 and t % 2 == 0), stop=False, skip_group_check=True)
                for e in range(E):
                    spread(b, e)
                    if e + 2 < E:
                        up(b, e + 2)
                    if e >= 1:
                        down(b, e - 1)
                down(b, E - 1)


def preln_stack(nc, x, out, a, f, g, e, cs0, sn0, cs1, sn1):
    mid = [nc.dram_tensor(f"x_after_{n}", (B, S, D), F32, kind="Internal").ap() for n in ("attention0", "experts0", "attention1")]
    attention0(nc, x, *a, cs0, sn0, mid[0])
    experts0(nc, mid[0], *f, mid[1])
    attention1(nc, mid[1], *g, cs1, sn1, mid[2])
    experts1(nc, mid[2], *e, out)


def rope_tables(n, width):
    import numpy as np

    inv = (1.0 / 10000.0 ** (np.arange(0, width, 2, dtype=np.float32) / width)).astype(np.float32)
    freqs = np.outer(np.arange(n, dtype=np.float32), inv)
    return np.cos(freqs).astype(np.float32), np.sin(freqs).astype(np.float32)


def kernel(**inputs):
    import numpy as np
    import concourse.bacc as bacc
    from concourse.bass_utils import run_bass_kernel_spmd

    i = {k: np.asarray(v) for k, v in inputs.items()}
    cs0, sn0 = rope_tables(S, HD0)
    cs1, sn1 = rope_tables(S, HD1)

    def heads(w):
        return w.reshape(H1, D, ROT, 2).transpose(1, 0, 3, 2).reshape(D, H1 * HD1)

    def head_bias(v):
        return v.reshape(H1, ROT, 2).transpose(2, 1, 0).reshape(HD1, H1)

    groups = {
        "x": [i["L0_attn_x"]],
        "a": [i["L0_attn_" + n] for n in ("wq", "bq", "wk", "bk", "wv", "bv", "wo", "bo", "q_norm_scale", "k_norm_scale")],
        "f": [i["L0_ffn_" + n] for n in ("Wg", "Wu", "Wd", "Wg_s", "Wu_s", "Wd_s", "Wr", "br", "rb")],
        "g": [heads(i["L1_attn_W_Q"]), head_bias(i["L1_attn_b_Q"]), heads(i["L1_attn_W_K"]), head_bias(i["L1_attn_b_K"]),
              i["L1_attn_W_V"].transpose(1, 0, 2).reshape(D, H1 * HD1), i["L1_attn_b_V"].T, i["L1_attn_W_O"], i["L1_attn_b_O"]],
        "e": [i["L1_ffn_w_gate"], i["L1_ffn_W1"], i["L1_ffn_b1"].T, i["L1_ffn_W2"], i["L1_ffn_b2"]],
        "t": [cs0, sn0, cs1.T, sn1.T],
    }
    nc = bacc.Bacc("TRN2", target_bir_lowering=False, num_devices=1)
    arrays, args = {}, {}
    for name, group in groups.items():
        args[name] = []
        for n, v in enumerate(group):
            v = np.ascontiguousarray(v)
            arrays[f"in_{name}{n}"] = v
            args[name].append(nc.dram_tensor(f"in_{name}{n}", v.shape, mybir.dt.from_np(v.dtype), kind="ExternalInput").ap())
    out = nc.dram_tensor("out", (B, S, D), F32, kind="ExternalOutput").ap()
    preln_stack(nc, args["x"][0], out, args["a"], args["f"], args["g"], args["e"], *args["t"])
    r = run_bass_kernel_spmd(nc, [arrays], core_ids=[0])
    return r.results[0]["out"]
```

```python
from contextlib import ExitStack

import concourse.bass as bass
from concourse import mybir
from concourse.alu_op_type import AluOpType as ALU

F32 = mybir.dt.float32
F32R = mybir.dt.float32r
F16 = mybir.dt.float16
BF16 = mybir.dt.bfloat16
I32 = mybir.dt.int32
ACT = mybir.ActivationFunctionType
AX = mybir.AxisListType

P = 128
B, S, D = 8, 512, 256
NT = S // P
NC = D // P
LN_EPS = 1e-5
MASKED = -1e38
RSQRT_MAGIC = 1597463007.0


class Chain:

    def __init__(self, eng, sem):
        self.eng, self.sem, self.n = eng, sem, 0

    def step(self, ins):
        ins.then_inc(self.sem, 1)
        self.n += 1
        return self.n

    def done(self, n=None):
        self.eng.wait_ge(self.sem, self.n if n is None else n)

    def restart(self):
        self.done()
        self.eng.sem_clear(self.sem)
        self.n = 0


def rsqrt_seed(dve, chain, y, x, sq):
    chain.step(dve.tensor_scalar(sq.bitcast(I32), x.bitcast(I32), 1, None, ALU.logical_shift_right))
    chain.done()
    chain.step(dve.tensor_scalar(y.bitcast(I32), sq.bitcast(I32), -1.0, RSQRT_MAGIC, ALU.mult, ALU.add))
    chain.done()


def rsqrt_newton(dve, chain, y, x, sq):
    chain.step(dve.tensor_tensor(sq, y, y, ALU.mult))
    chain.done()
    chain.step(dve.scalar_tensor_tensor(out=sq, in0=sq, scalar=-0.5, in1=x, op0=ALU.mult, op1=ALU.mult))
    chain.done()
    chain.step(dve.scalar_tensor_tensor(out=y, in0=sq, scalar=1.5, in1=y, op0=ALU.add, op1=ALU.mult))
    chain.done()


def rsqrt(dve, chain, y, x, sq):
    rsqrt_seed(dve, chain, y, x, sq)
    for _ in range(3):
        rsqrt_newton(dve, chain, y, x, sq)


def layernorm_sums(dve, chain, x, ln):
    for t in range(NT):
        chain.step(dve.bn_stats(ln["stats"][:, t, :], x[:, t, :]))
    chain.done()
    for t in range(NT):
        chain.step(dve.bn_aggr(ln["mv"][:, t, :], ln["stats"][:, t, :]))
    chain.done()
    chain.step(dve.tensor_scalar(ln["var"][:, :], ln["mv"][:, :, 1], LN_EPS, None, ALU.add))
    chain.done()


def layernorm_apply(dve, x, ln, xn, t):
    return dve.tensor_scalar(xn[:, t, :], x[:, t, :], ln["mv"][:, t, 0:1], ln["rstd"][:, t:t + 1],
                             ALU.subtract, ALU.mult)


def layernorm_stats(dve, chain, x, ln):
    layernorm_sums(dve, chain, x, ln)
    rsqrt(dve, chain, ln["rstd"][:, :], ln["var"][:, :], ln["sq"][:, :])


LN_PIECES = 5


def layernorm_piece(dve, chain, x, ln, xn, xn_ready, piece):
    rstd, var, sq = ln["rstd"][:, :], ln["var"][:, :], ln["sq"][:, :]
    if piece == 0:
        layernorm_sums(dve, chain, x, ln)
    elif piece == 1:
        rsqrt_seed(dve, chain, rstd, var, sq)
        rsqrt_newton(dve, chain, rstd, var, sq)
    elif piece == 2:
        rsqrt_newton(dve, chain, rstd, var, sq)
        rsqrt_newton(dve, chain, rstd, var, sq)
    else:
        for t in (0, 1) if piece == 3 else (2, 3):
            layernorm_apply(dve, x, ln, xn, t).then_inc(xn_ready, 1)


def layernorm_buffers(sb, tag):
    return {
        "stats": sb(f"{tag}_ln_stats", [P, NT, 6], F32),
        "mv": sb(f"{tag}_ln_mv", [P, NT, 2], F32),
        "var": sb(f"{tag}_ln_var", [P, NT], F32),
        "rstd": sb(f"{tag}_ln_rstd", [P, NT], F32),
        "sq": sb(f"{tag}_ln_sq", [P, NT], F32),
    }


def token_tiles(x, b):
    return x[b, :, :].rearrange("(t p) d -> p t d", p=P)


def row_to_all(v):
    return v.rearrange("(o n) -> o n", o=1).partition_broadcast(P)


def make_identity(pool, chain, m):
    chain.step(pool.memset(m, 0.0))
    chain.done()
    chain.step(pool.affine_select(out=m, in_=m, compare_op=ALU.not_equal, fill=1.0, base=0,
                                  pattern=[[-1, P]], channel_multiplier=1))


def make_causal(pool, chain, m):
    chain.step(pool.memset(m, 0.0))
    chain.done()
    chain.step(pool.affine_select(out=m, in_=m, compare_op=ALU.is_ge, fill=MASKED, base=0,
                                  pattern=[[-1, P]], channel_multiplier=1))


HD0, H0, G0 = 16, 16, 4
REP0 = H0 // G0
HALF0 = HD0 // 2
QK0 = (H0 + G0) * HD0
QKV0 = (H0 + 2 * G0) * HD0
GW = 32
RMS_EPS = 1e-6
TRI = [P * (i + 1) for i in range(NT)]
P_AT = [sum(TRI[:i]) for i in range(NT + 1)]
T_AT = [sum(S - P * k for k in range(j)) for j in range(NT + 1)]


def attention0(nc, x, wq, bq, wk, bk, wv, bv, wo, bo, q_scale, k_scale, cos, sin, out):
    ctx = ExitStack()
    with ctx:
        def sb(name, shape, dt):
            return ctx.enter_context(nc.sbuf_tensor(f"a_{name}", shape, dt))

        def pb(name, shape, dt):
            return ctx.enter_context(nc.psum_tensor(f"a_{name}", shape, dt))

        def sem(name):
            return ctx.enter_context(nc.semaphore(f"a_{name}"))

        w_in = sb("w_in", [P, NC, QKV0], F32)
        wo_in = sb("wo_in", [P, NC, D], F32)
        w16 = sb("w16", [P, NC, QKV0], F16)
        wo16 = sb("wo16", [P, NC, D], F16)
        b_in = sb("b_in", [P, QKV0], F32)
        b16 = sb("b16", [P, QKV0], F16)
        bo_in = sb("bo_in", [P, D], F32)
        bo16 = sb("bo16", [P, D], F16)
        cs_in = sb("cs_in", [P, NT, HD0 // 2], F32)
        sn_in = sb("sn_in", [P, NT, HD0 // 2], F32)
        scales = sb("scales", [P, 2, HD0], F32)
        tab_c = sb("tab_c", [P, NT, 2, HD0], F32)
        tab_s = sb("tab_s", [P, NT, 2, HD0], F32)
        ident = sb("ident", [P, P], F16)
        ident_b = sb("ident_b", [P, P], BF16)
        causal = sb("causal", [P, P], BF16)
        x_in = sb("x_in", [P, NT, D], F32)
        x_res = sb("x_res", [P, NT, D], F32)
        x_out = sb("x_out", [P, NT, D], F32)
        xn = sb("xn", [P, NT, D], F16)
        ln = layernorm_buffers(sb, "x")
        xT = sb("xT", [P, NC, S], F16)
        qkv = sb("qkv", [P, NT, QKV0], F16)
        sq = sb("sq", [P, NT, QK0], F32)
        ra = sb("ra", [P, NT, QK0], F32)
        rb = sb("rb", [P, NT, QK0], F32)
        ms = sb("ms", [P, NT * (H0 + G0)], F32)
        rs = sb("rs", [P, NT * (H0 + G0)], F32)
        rs_sq = sb("rs_sq", [P, NT * (H0 + G0)], F32)
        q_pad = sb("q_pad", [P, NT, REP0, G0, GW], F16)
        k_pad = sb("k_pad", [P, NT, G0, GW], F16)
        qT = sb("qT", [P, REP0, S], F16)
        kT = sb("kT", [P, G0, S], F16)
        nmax = sb("nmax", [P, 2, NT], F32)
        sums = sb("sums", [P, NT, H0], F32)
        rsum = sb("rsum", [P, NT, H0], F32)
        probs = sb("probs", [P, 2, P_AT[NT]], F16)
        pT = sb("pT", [P, 2, T_AT[NT]], F16)
        z16 = sb("z16", [P, NT, D], F16)
        zT = sb("zT", [P, NC, S], F16)

        ps_s = [pb(f"ps_s{i}", [P, S], F32) for i in range(4)]
        ps_t = [pb(f"ps_t{i}", [P, 2 * S], F16) for i in range(2)]
        ps_z = [pb(f"ps_z{i}", [P, 2, D], F32) for i in range(2)]
        ps_xT = ps_t
        ps_qkv = ps_s[0:2]
        ps_qT = ps_t
        ps_kT = ps_z[0][:, 0, :].bitcast(F16)
        ps_zT = ps_t

        loaded = [sem(f"loaded{i}") for i in range(3)]
        setup_pool = sem("setup_pool")
        setup_dve = sem("setup_dve")
        consts_ready = sem("consts_ready")
        x_loaded = sem("x_loaded")
        x_taken = sem("x_taken")
        xn_ready = sem("xn_ready")
        xT_ps = sem("xT_ps")
        xT_ready = sem("xT_ready")
        qkv_ps = sem("qkv_ps")
        qkv_ready = sem("qkv_ready")
        sq_ready = sem("sq_ready")
        rot_ready = sem("rot_ready")
        qk_ready = sem("qk_ready")
        qkT_ps = sem("qkT_ps")
        kT_ready = sem("kT_ready")
        qT_ready = sem("qT_ready")
        scores_ps = sem("scores_ps")
        max_ready = sem("max_ready")
        probs_ready = sem("probs_ready")
        pT_ps = sem("pT_ps")
        pT_ready = sem("pT_ready")
        z_ps = sem("z_ps")
        z_ready = sem("z_ready")
        zT_ps = sem("zT_ps")
        zT_ready = sem("zT_ready")
        y_ps = sem("y_ps")
        y_ready = sem("y_ready")
        stored = sem("stored")
        x_out_free = sem("x_out_free")
        dve_steps = sem("dve_steps")

        block = ctx.enter_context(nc.Block())

        def real(h):
            return 0 <= h < H0

        def tile_at(b, h, i):
            return NT * (H0 * b + h) + i + 1

        def half_at(b, h, k):
            return 2 * (H0 * b + h) + k + 1

        @block.sync
        def _(sp):
            sp.dma_start(x_in[:], token_tiles(x, 0)).then_inc(x_loaded, 16)
            sp.sem_inc(x_out_free, 1)
            sp.dma_start(w_in[:, :, 0:D], wq.rearrange("(c p) n -> p c n", p=P)).then_inc(loaded[1], 16)
            sp.dma_start(w_in[:, :, D:QK0], wk.rearrange("(c p) n -> p c n", p=P)).then_inc(loaded[1], 16)
            sp.dma_start(w_in[:, :, QK0:QKV0], wv.rearrange("(c p) n -> p c n", p=P)).then_inc(loaded[1], 16)
            sp.dma_start(b_in[:, 0:D], row_to_all(bq)).then_inc(loaded[1], 16)
            sp.dma_start(b_in[:, D:QK0], row_to_all(bk)).then_inc(loaded[1], 16)
            sp.dma_start(b_in[:, QK0:QKV0], row_to_all(bv)).then_inc(loaded[1], 16)
            sp.dma_start(cs_in[:], cos.rearrange("(t p) n -> p t n", p=P)).then_inc(loaded[0], 16)
            sp.dma_start(sn_in[:], sin.rearrange("(t p) n -> p t n", p=P)).then_inc(loaded[0], 16)
            sp.dma_start(scales[:, 0, :], row_to_all(q_scale)).then_inc(loaded[0], 16)
            sp.dma_start(scales[:, 1, :], row_to_all(k_scale)).then_inc(loaded[0], 16)
            sp.dma_start(wo_in[:], wo.rearrange("(c p) n -> p c n", p=P)).then_inc(loaded[2], 16)
            sp.dma_start(bo_in[:], row_to_all(bo)).then_inc(loaded[2], 16)

            def store(b):
                sp.wait_ge(y_ready, 2 * b + 2)
                sp.dma_start(token_tiles(out, b), x_out[:]).then_inc(stored, 16)
                sp.wait_ge(stored, 16 * b + 16)

            with sp.Fori(0, B - 1) as b:
                sp.wait_ge(x_taken, b + 1)
                sp.dma_start(x_in[:], token_tiles(x, b + 1)).then_inc(x_loaded, 16)
                store(b)
                sp.sem_inc(x_out_free, 1)
            store(B - 1)

        @block.gpsimd
        def _(pool):
            chain = Chain(pool, setup_pool)
            make_identity(pool, chain, ident[:])
            make_identity(pool, chain, ident_b[:])
            make_causal(pool, chain, causal[:])
            pool.wait_ge(consts_ready, 1)
            with pool.Fori(0, B) as b:
                for t in range(NT):
                    pool.wait_ge(qkv_ready, NT * b + t + 1)
                    for j, (c0, nh) in enumerate(((0, H0), (D, G0))):
                        src = qkv[:, t, c0:c0 + nh * HD0].rearrange("p (h d) -> p h d", d=HD0)
                        r = rb[:, t, c0:c0 + nh * HD0].rearrange("p (h d) -> p h d", d=HD0)
                        for to, frm in ((slice(0, HALF0), slice(HALF0, HD0)), (slice(HALF0, HD0), slice(0, HALF0))):
                            pool.tensor_tensor(r[:, :, to], src[:, :, frm],
                                               tab_s[:, t, j, to].unsqueeze(1).to_broadcast([P, nh, HALF0]),
                                               ALU.mult).then_inc(rot_ready, 1)
                pool.wait_ge(x_out_free, b + 1)
                pool.tensor_tensor(x_res[:], x_in[:], bo16[:].unsqueeze(1).to_broadcast([P, NT, D]),
                                   ALU.add).then_inc(x_taken, 1)

        @block.scalar
        def _(act):
            def copy_xT(b, c):
                act.wait_ge(xT_ps, NC * b + c + 1)
                act.activation(xT[:, c, :], ps_xT[c][:, 0:S], ACT.Copy).then_inc(xT_ready, 1)

            def copy_kT(g):
                rows = slice(GW * g, GW * (g + 1))
                act.activation(kT[rows, g, :], ps_kT[rows, :], ACT.Copy).then_inc(kT_ready, 1)

            def one_batch(b, more):
                for t in range(NT):
                    act.wait_ge(qkv_ready, NT * b + t + 1)
                    act.activation(sq[:, t, :], qkv[:, t, 0:QK0], ACT.Square).then_inc(sq_ready, 1)
                act.wait_ge(qkT_ps, 3 * b + 1)
                copy_kT(0)
                for h in range(H0):
                    for i in range(NT):
                        act.wait_ge(max_ready, tile_at(b, h, i))
                        if i == 0 and h >= 2:
                            act.wait_ge(pT_ps, half_at(b, h - 2, 1))
                        act.activation(probs[:, h % 2, P_AT[i]:P_AT[i + 1]], ps_s[i][:, 0:TRI[i]], ACT.Exp,
                                       bias=nmax[:, h % 2, i:i + 1],
                                       accum_out=sums[:, i, h:h + 1]).then_inc(probs_ready, 1)
                    if h == 0:
                        for g in range(1, G0):
                            copy_kT(g)
                for c in range(NC):
                    act.wait_ge(zT_ps, NC * b + c + 1)
                    act.activation(zT[:, c, :], ps_zT[c][:, 0:S], ACT.Copy).then_inc(zT_ready, 1)
                for c in range(NC if more else 0):
                    copy_xT(b + 1, c)

            for c in range(NC):
                copy_xT(0, c)
            with act.Fori(0, B - 1) as b:
                one_batch(b, True)
            one_batch(B - 1, False)

        @block.vector
        def _(dve):
            chain = Chain(dve, setup_dve)
            dve.wait_ge(loaded[0], 16 * 4)
            for j in range(2):
                by = float(HD0) ** -1 if j == 0 else 1.0
                lo = scales[:, j, 0:HALF0].unsqueeze(1).to_broadcast([P, NT, HALF0])
                hi = scales[:, j, HALF0:HD0].unsqueeze(1).to_broadcast([P, NT, HALF0])
                for dst, table, scale, sign in ((tab_c[:, :, j, 0:HALF0], cs_in, lo, 1.0), (tab_c[:, :, j, HALF0:HD0], cs_in, hi, 1.0),
                                                (tab_s[:, :, j, 0:HALF0], sn_in, hi, -1.0), (tab_s[:, :, j, HALF0:HD0], sn_in, lo, 1.0)):
                    chain.step(dve.scalar_tensor_tensor(out=dst, in0=table[:], scalar=sign * by, in1=scale,
                                                        op0=ALU.mult, op1=ALU.mult))
            dve.wait_ge(loaded[1], 16 * 6)
            chain.step(dve.tensor_copy(w16[:], w_in[:]))
            chain.step(dve.tensor_copy(b16[:], b_in[:]))
            dve.wait_ge(loaded[2], 16 * 2)
            chain.step(dve.tensor_copy(wo16[:], wo_in[:]))
            chain.step(dve.tensor_copy(bo16[:], bo_in[:]))
            chain.step(dve.memset(q_pad[:].rearrange("p a b c d -> p (a b c d)"), 0.0))
            chain.step(dve.memset(k_pad[:].rearrange("p a b c -> p (a b c)"), 0.0))
            chain.step(dve.memset(kT[:].rearrange("p a b -> p (a b)"), 0.0))
            chain.done()
            dve.sem_inc(consts_ready, 1)

            chain = Chain(dve, dve_steps)
            def layernorm(b):
                dve.wait_ge(x_loaded, 16 * b + 16)
                for piece in range(LN_PIECES):
                    layernorm_piece(dve, chain, x_in, ln, xn, xn_ready, piece)

            def one_batch(b, more):
                for t in range(NT):
                    dve.wait_ge(qkv_ps, NT * b + t + 1)
                    dve.tensor_tensor(qkv[:, t, :], ps_qkv[t % 2][:, 0:QKV0], b16[:], ALU.add).then_inc(qkv_ready, 1)
                dve.wait_ge(qkv_ready, NT * b + NT)
                for t in range(NT):
                    for j, (c0, nh) in enumerate(((0, H0), (D, G0))):
                        src = qkv[:, t, c0:c0 + nh * HD0].rearrange("p (h d) -> p h d", d=HD0)
                        a = ra[:, t, c0:c0 + nh * HD0].rearrange("p (h d) -> p h d", d=HD0)
                        chain.step(dve.tensor_tensor(a, src, tab_c[:, t, j, :].unsqueeze(1).to_broadcast([P, nh, HD0]), ALU.mult))
                dve.wait_ge(sq_ready, NT * b + NT)
                chain.step(dve.tensor_reduce(ms[:], sq[:].rearrange("p t (h d) -> p (t h) d", d=HD0), AX.X, ALU.add))
                chain.done()
                chain.step(dve.tensor_scalar(ms[:], ms[:], 1.0 / HD0, RMS_EPS, ALU.mult, ALU.add))
                chain.done()
                rsqrt(dve, chain, rs[:], ms[:], rs_sq[:])
                dve.wait_ge(rot_ready, 4 * NT * b + 4 * NT)
                chain.step(dve.tensor_tensor(ra[:], ra[:], rb[:], ALU.add))
                chain.done()
                for t in range(NT):
                    r4 = rs[:, t * (H0 + G0):(t + 1) * (H0 + G0)]
                    for g in range(G0):
                        h0 = g * REP0
                        dve.tensor_tensor(
                            q_pad[:, t, :, g, 0:HD0],
                            ra[:, t, h0 * HD0:(h0 + REP0) * HD0].rearrange("p (r d) -> p r d", d=HD0),
                            r4[:, h0:h0 + REP0].unsqueeze(2).to_broadcast([P, REP0, HD0]), ALU.mult).then_inc(qk_ready, 1)
                    dve.tensor_tensor(
                        k_pad[:, t, :, 0:HD0], ra[:, t, D:QK0].rearrange("p (g d) -> p g d", d=HD0),
                        r4[:, H0:H0 + G0].unsqueeze(2).to_broadcast([P, G0, HD0]), ALU.mult).then_inc(qk_ready, 1)

                for u in range(2):
                    dve.wait_ge(qkT_ps, 3 * b + u + 2)
                    dve.tensor_copy(qT[:, 2 * u:2 * u + 2, :].rearrange("p r s -> p (r s)"), ps_qT[u][:]).then_inc(qT_ready, 1)

                def maxima(h, i):
                    if real(h):
                        dve.wait_ge(scores_ps, tile_at(b, h, i))
                        dve.tensor_reduce(nmax[:, h % 2, i:i + 1], ps_s[i][:, 0:TRI[i]], AX.X, ALU.max,
                                          negate=True).then_inc(max_ready, 1)

                def copy_pT(h, k):
                    if real(h):
                        dve.wait_ge(pT_ps, half_at(b, h, k))
                        if h >= 2:
                            dve.wait_ge(z_ps, H0 * b + h - 1)
                        dve.tensor_copy(pT[:, h % 2, T_AT[2 * k]:T_AT[2 * k + 2]],
                                        ps_t[k][:, 0:T_AT[2 * k + 2] - T_AT[2 * k]]).then_inc(pT_ready, 1)

                for s in range(-1, H0 + 3):
                    maxima(s, 0)
                    copy_pT(s - 2, 1)
                    maxima(s, 1)
                    maxima(s, 2)
                    maxima(s, 3)
                    copy_pT(s - 1, 0)
                dve.wait_ge(probs_ready, H0 * NT * (b + 1))
                chain.step(dve.reciprocal(rsum[:], sums[:]))
                chain.done()
                dve.wait_ge(z_ps, H0 * (b + 1))
                for t in range(NT):
                    dve.tensor_tensor(z16[:, t, :].rearrange("p (h d) -> p h d", d=HD0),
                                      ps_z[t // 2][:, t % 2, :].rearrange("p (h d) -> p h d", d=HD0),
                                      rsum[:, t, :].unsqueeze(2).to_broadcast([P, H0, HD0]), ALU.mult).then_inc(z_ready, 1)
                if more:
                    layernorm(b + 1)
                dve.wait_ge(x_taken, b + 1)
                for u in range(2):
                    dve.wait_ge(y_ps, 2 * b + u + 1)
                    if u == 0:
                        dve.wait_ge(x_out_free, b + 1)
                    dve.tensor_tensor(x_out[:, 2 * u:2 * u + 2, :], ps_z[u][:], x_res[:, 2 * u:2 * u + 2, :],
                                      ALU.add).then_inc(y_ready, 1)
                chain.restart()

            layernorm(0)
            chain.restart()
            with dve.Fori(0, B - 1) as b:
                one_batch(b, True)
            one_batch(B - 1, False)

        @block.tensor
        def _(pe):
            pe.wait_ge(setup_pool, 6)
            pe.wait_ge(consts_ready, 1)
            def transpose_x(b):
                for c in range(NC):
                    for t in range(NT):
                        pe.wait_ge(xn_ready, NT * b + t + 1)
                        last = pe.transpose(ps_xT[c][:, t * P:(t + 1) * P],
                                            xn[:, t, c * P:(c + 1) * P], ident[:])
                    last.then_inc(xT_ps, 1)

            def one_batch(b, more):
                pe.wait_ge(xT_ready, NC * b + NC)
                for t in range(NT):
                    if t >= 2:
                        pe.wait_ge(qkv_ready, NT * b + t - 1)
                    for c in range(NC):
                        last = pe.matmul(ps_qkv[t % 2][:, 0:QKV0], xT[:, c, t * P:(t + 1) * P], w16[:, c, :],
                                         start=(c == 0), stop=(c == NC - 1))
                    last.then_inc(qkv_ps, 1)
                pe.wait_ge(qk_ready, NT * (G0 + 1) * (b + 1))
                for t in range(NT):
                    last = pe.transpose(ps_kT[:, t * P:(t + 1) * P],
                                        k_pad[:, t, :, :].rearrange("p g d -> p (g d)"), ident[:])
                last.then_inc(qkT_ps, 1)
                for r in range(REP0):
                    for t in range(NT):
                        last = pe.transpose(ps_qT[r // 2][:, (r % 2) * S + t * P:(r % 2) * S + (t + 1) * P],
                                            q_pad[:, t, r, :, :].rearrange("p g d -> p (g d)"), ident[:])
                    if r % 2 == 1:
                        last.then_inc(qkT_ps, 1)

                def scores(h, i):
                    if real(h):
                        g, r = h // REP0, h % REP0
                        if i == 0 and r == 0:
                            pe.wait_ge(kT_ready, G0 * b + g + 1)
                        if i == 0 and h in (0, 2):
                            pe.wait_ge(qT_ready, 2 * b + h // 2 + 1)
                        if h >= 1:
                            pe.wait_ge(probs_ready, tile_at(b, h - 1, i))
                        pe.matmul(ps_s[i][:, 0:TRI[i]], qT[:, r, i * P:(i + 1) * P], kT[:, g, 0:TRI[i]],
                                  start=True, stop=False)
                        pe.matmul(ps_s[i][:, i * P:TRI[i]], ident_b[:], causal[:],
                                  start=False, stop=True).then_inc(scores_ps, 1)

                def transposes(h, k):
                    if real(h):
                        pe.wait_ge(probs_ready, tile_at(b, h, NT - 1))
                        if h >= 1:
                            pe.wait_ge(pT_ready, half_at(b, h - 1, k))
                        for j in (2 * k, 2 * k + 1):
                            for i in range(j, NT):
                                at = T_AT[j] - T_AT[2 * k] + (i - j) * P
                                last = pe.transpose(ps_t[k][:, at:at + P],
                                                    probs[:, h % 2, P_AT[i] + j * P:P_AT[i] + (j + 1) * P], ident[:])
                        last.then_inc(pT_ps, 1)

                def values(h):
                    if real(h):
                        v0 = QK0 + (h // REP0) * HD0
                        pe.wait_ge(pT_ready, half_at(b, h, 1))
                        if h == 0:
                            pe.wait_ge(kT_ready, G0 * b + G0)
                        for i in range(NT):
                            for j in range(i + 1):
                                at = T_AT[j] + (i - j) * P
                                last = pe.matmul(ps_z[i // 2][:, i % 2, h * HD0:(h + 1) * HD0], pT[:, h % 2, at:at + P],
                                                 qkv[:, j, v0:v0 + HD0], start=(j == 0), stop=(j == i))
                        last.then_inc(z_ps, 1)

                for s in range(-1, H0 + 3):
                    scores(s, 1)
                    scores(s, 2)
                    values(s - 3)
                    scores(s, 3)
                    transposes(s - 1, 0)
                    transposes(s - 1, 1)
                    scores(s + 1, 0)
                for c in range(NC):
                    for t in range(NT):
                        pe.wait_ge(z_ready, NT * b + t + 1)
                        last = pe.transpose(ps_zT[c][:, t * P:(t + 1) * P],
                                            z16[:, t, c * P:(c + 1) * P], ident[:])
                    last.then_inc(zT_ps, 1)
                pe.wait_ge(zT_ready, NC * b + NC)
                for t in range(NT):
                    for c in range(NC):
                        last = pe.matmul(ps_z[t // 2][:, t % 2, :], zT[:, c, t * P:(t + 1) * P], wo16[:, c, :],
                                         start=(c == 0), stop=(c == NC - 1))
                    if t % 2 == 1:
                        last.then_inc(y_ps, 1)
                if more:
                    transpose_x(b + 1)

            transpose_x(0)
            with pe.Fori(0, B - 1) as b:
                one_batch(b, True)
            one_batch(B - 1, False)

H1, HD1 = 16, 128
ROT = HD1 // 2
SCALE1 = float(HD1) ** -0.5
PASSES = ((0, 0), (0, 1), (1, 0))


def attention1(nc, x, wq, bq, wk, bk, wv, bv, wo, bo, cos, sin, out):
    ctx = ExitStack()
    with ctx:
        def sb(name, shape, dt, stack=ctx):
            return stack.enter_context(nc.sbuf_tensor(f"c_{name}", shape, dt))

        def pb(name, shape, dt):
            return ctx.enter_context(nc.psum_tensor(f"c_{name}", shape, dt))

        def sem(name):
            return ctx.enter_context(nc.semaphore(f"c_{name}"))

        DM = H1 * HD1
        w_hi = sb("w_hi", [P, 3, NC, DM], F32R)
        w_lo = sb("w_lo", [P, 3, NC, DM], F32R)
        w_parts = (w_hi, w_lo)
        wo_sb = sb("wo", [P, H1, D], F32)
        ident = sb("ident", [P, P], F32)
        ident_b = sb("ident_b", [P, P], BF16)
        causal = sb("causal", [P, P], BF16)
        cosT = sb("cosT", [P, S], F32)
        sinT = sb("sinT", [P, S], F32)
        bias = sb("bias", [P, 3, H1], F32)
        bo_sb = sb("bo", [P, D], F32)

        loaded = [sem(f"loaded{i}") for i in range(5)]
        setup_hi = sem("setup_hi")
        setup_lo = sem("setup_lo")
        setup_pool = sem("setup_pool")

        x_in = sb("x_in", [P, NT, D], F32)
        ln = layernorm_buffers(sb, "c")
        x_loaded = sem("x_loaded")
        xn_ready = sem("xn_ready")
        dve_steps = sem("dve_steps")

        with ExitStack() as setup:
            w_in = sb("w_in", [P, 3, NC * DM], F32, setup)
            block = setup.enter_context(nc.Block())

            @block.sync
            def _(sp):
                sp.dma_start(x_in[:], token_tiles(x, 0)).then_inc(x_loaded, 16)
                for i, w in enumerate((wq, wk, wv)):
                    for c in range(NC):
                        sp.dma_start(w_in[:, i, c * DM:(c + 1) * DM], w[c * P:(c + 1) * P, :]).then_inc(loaded[i], 16)
                for i, v in enumerate((bq, bk, bv)):
                    sp.dma_start(bias[:, i, :], v).then_inc(loaded[4], 16)
                sp.dma_start(bo_sb[:], row_to_all(bo)).then_inc(loaded[4], 16)
                for k in range(2):
                    sp.dma_start(cosT[k * ROT:(k + 1) * ROT, :], cos).then_inc(loaded[4], 16)
                    sp.dma_start(sinT[k * ROT:(k + 1) * ROT, :], sin).then_inc(loaded[4], 16)
                sp.dma_start(wo_sb[:], wo.rearrange("n d m -> d n m")).then_inc(loaded[3], 16)

            @block.gpsimd
            def _(pool):
                chain = Chain(pool, setup_pool)
                make_identity(pool, chain, ident[:])
                make_identity(pool, chain, ident_b[:])
                make_causal(pool, chain, causal[:])
                chain.done()

            @block.scalar
            def _(act):
                for i in range(3):
                    act.wait_ge(loaded[i], 16 * NC)
                    act.activation(w_hi[:, i, :, :].rearrange("p c n -> p (c n)"), w_in[:, i, :],
                                   ACT.Copy).then_inc(setup_hi, 1)

            @block.vector
            def _(dve):
                chain = Chain(dve, dve_steps)
                dve.wait_ge(x_loaded, 16)
                for piece in range(LN_PIECES):
                    layernorm_piece(dve, chain, x_in, ln, x_in, xn_ready, piece)
                chain.restart()
                for i in range(3):
                    dve.wait_ge(setup_hi, i + 1)
                    dve.tensor_tensor(w_lo[:, i, :, :].rearrange("p c n -> p (c n)"), w_in[:, i, :],
                                      w_hi[:, i, :, :].rearrange("p c n -> p (c n)").bitcast(F32),
                                      ALU.subtract).then_inc(setup_lo, 1)
                dve.wait_ge(loaded[4], 16 * 8)
                dve.tensor_scalar(bias[:, 0, :], bias[:, 0, :], SCALE1, None, ALU.mult).then_inc(setup_lo, 1)
                dve.tensor_scalar(sinT[0:ROT, :], sinT[0:ROT, :], 1.0, None, ALU.mult).then_inc(setup_lo, 1)
                dve.tensor_scalar(sinT[ROT:P, :], sinT[ROT:P, :], -1.0, None, ALU.mult).then_inc(setup_lo, 1)

        x_res = sb("x_res", [P, NT, D], F32)
        xT = [sb(f"xT{k}", [P, NC, S], F32R) for k in range(2)]
        raw = sb("raw", [P, 2, S], F32)
        turn = sb("turn", [P, 2, S], F32)
        cross = sb("cross", [P, 2, S], F32)
        qkT = [sb(f"qkT{k}", [P, 2, 2, S], F32R) for k in range(2)]
        v = [sb(f"v{k}", [P, 2, NT, 2 * HD1], F32R) for k in range(2)]
        probs = sb("probs", [P, 2, P_AT[NT]], F32)
        pT = [sb(f"pT{k}", [P, T_AT[NT]], F32R) for k in range(2)]
        zT = [sb(f"zT{k}", [P, S], F32R) for k in range(2)]
        wo_parts = [sb(f"wo{k}", [P, 2, D], F32R) for k in range(2)]
        nmax = sb("nmax", [P, 2, NT], F32)
        sums = sb("sums", [P, 2, NT], F32)
        rsum = sb("rsum", [P, 2, NT], F32)

        ps_s = [pb(f"ps_s{i}", [P, S], F32) for i in range(2)]
        ps_t = [pb(f"ps_t{i}", [P, S], F32) for i in range(2)]
        ps_proj = pb("ps_proj", [P, S], F32)
        ps_z = pb("ps_z", [P, S], F32)
        ps_o = [pb(f"ps_o{i}", [P, 2, D], F32) for i in range(2)]

        res_loaded = sem("res_loaded")
        res_ready = sem("res_ready")
        xT_ps = sem("xT_ps")
        xT_hi = sem("xT_hi")
        xT_lo = sem("xT_lo")
        qk_ps = [sem(f"qk_ps{j}") for j in range(2)]
        qk_raw = [sem(f"qk_raw{j}") for j in range(2)]
        qk_cos = [sem(f"qk_cos{j}") for j in range(2)]
        qk_turned = [sem(f"qk_turned{j}") for j in range(2)]
        qk_hi = [sem(f"qk_hi{j}") for j in range(2)]
        qk_lo = [sem(f"qk_lo{j}") for j in range(2)]
        v_ps = sem("v_ps")
        v_hi = sem("v_hi")
        v_lo = sem("v_lo")
        scores_ps = [sem(f"scores_ps{i}") for i in range(NT)]
        max_ready = [sem(f"max_ready{i}") for i in range(NT)]
        exp_ready = [sem(f"exp_ready{i}") for i in range(NT)]
        probs_ready = [sem(f"probs_ready{i}") for i in range(NT)]
        pT_ps = sem("pT_ps")
        pT_hi = sem("pT_hi")
        pT_lo = sem("pT_lo")
        pv_done = sem("pv_done")
        o_done = sem("o_done")
        z_hi = sem("z_hi")
        z_lo = sem("z_lo")
        wo_hi = sem("wo_hi")
        wo_lo = sem("wo_lo")
        y_ready = sem("y_ready")
        stored = sem("stored")

        block = ctx.enter_context(nc.Block())

        @block.sync
        def _(sp):
            sp.dma_start(x_res[:], token_tiles(x, 0)).then_inc(res_loaded, 16)
            with sp.Fori(0, B - 1) as b:
                sp.wait_ge(xT_ps, NC * b + NC)
                sp.dma_start(x_in[:], token_tiles(x, b + 1)).then_inc(x_loaded, 16)
                sp.wait_ge(y_ready, 2 * b + 2)
                sp.dma_start(token_tiles(out, b), x_res[:]).then_inc(stored, 16)
                sp.wait_ge(stored, 16 * b + 16)
                sp.dma_start(x_res[:], token_tiles(x, b + 1)).then_inc(res_loaded, 16)
            sp.wait_ge(y_ready, 2 * B)
            sp.dma_start(token_tiles(out, B - 1), x_res[:]).then_inc(stored, 16)
            sp.wait_ge(stored, 16 * B)

        def at(b, h):
            return H1 * b + h + 1

        def row_at(b, h, j):
            return NT * (H1 * b + h) + j + 1

        def heads_of(first, last):
            return range(0 if first else -H1, H1 if last else 2 * H1)

        def slots_of(first, last):
            return range(-2 if first else 0, H1 + 2 if last else H1)

        @block.gpsimd
        def _(pool):
            def cos_part(heads, b, h, j):
                if h in heads:
                    pool.wait_ge(qk_raw[j], at(b, h))
                    if h - 1 in heads:
                        pool.wait_ge(qk_lo[j], at(b, h - 1))
                    pool.tensor_tensor(turn[:, j, :], raw[:, j, :], cosT[:], ALU.mult).then_inc(qk_cos[j], 1)

            def low_head(heads, b, h, j):
                if h in heads:
                    pool.wait_ge(qk_hi[j], at(b, h))
                    pool.tensor_tensor(qkT[1][:, h % 2, j, :], turn[:, j, :], qkT[0][:, h % 2, j, :].bitcast(F32),
                                       ALU.subtract).then_inc(qk_lo[j], 1)

            def low_wo(heads, b, h):
                if h in heads:
                    pool.wait_ge(wo_hi, at(b, h))
                    pool.tensor_tensor(wo_parts[1][:, h % 2, :], wo_sb[:, h % H1, :],
                                       wo_parts[0][:, h % 2, :].bitcast(F32), ALU.subtract).then_inc(wo_lo, 1)

            def one_batch(b, first, last):
                heads = heads_of(first, last)
                for s in slots_of(first, last):
                    low_head(heads, b, s + 1, 1)
                    cos_part(heads, b, s + 2, 0)
                    cos_part(heads, b, s + 2, 1)
                    low_head(heads, b, s + 2, 0)
                    low_wo(heads, b, s)
                    if s == H1 // 2:
                        pool.wait_ge(res_loaded, 16 * b + 16)
                        pool.tensor_tensor(x_res[:], x_res[:], bo_sb[:].unsqueeze(1).to_broadcast([P, NT, D]),
                                           ALU.add).then_inc(res_ready, 1)

            pool.wait_ge(loaded[3], 16)
            one_batch(0, True, False)
            with pool.Fori(1, B - 1) as b:
                one_batch(b, False, False)
            one_batch(B - 1, False, True)

        @block.scalar
        def _(act):
            def raw_head(heads, b, h, j):
                if h in heads:
                    act.wait_ge(qk_ps[j], at(b, h))
                    act.activation(raw[:, j, :], ps_proj[:], ACT.Identity, bias=bias[:, 1 - j, h % H1:h % H1 + 1],
                                   scale=SCALE1 if j == 1 else 1.0).then_inc(qk_raw[j], 1)

            def high_head(heads, b, h, j):
                if h in heads:
                    act.wait_ge(qk_turned[j], at(b, h))
                    if h - 2 in heads:
                        act.wait_ge(scores_ps[NT - 1], at(b, h - 2))
                    act.activation(qkT[0][:, h % 2, j, :], turn[:, j, :], ACT.Copy).then_inc(qk_hi[j], 1)

            def high_v(heads, b, part):
                if part in heads:
                    act.wait_ge(v_ps, at(b, part))
                    if 2 * (part // 2) - 3 in heads:
                        act.wait_ge(pv_done, row_at(b, 2 * (part // 2) - 3, NT - 1))
                    t0 = 2 * (part % 2)
                    act.activation(v[0][:, (part // 2) % 2, t0:t0 + 2, :], ps_proj[:].rearrange("p (t n) -> p t n", t=2),
                                   ACT.Copy).then_inc(v_hi, 1)

            def exps(heads, b, h, i):
                if h in heads:
                    act.wait_ge(max_ready[i], at(b, h))
                    if h - 2 in heads:
                        act.wait_ge(pT_ps, row_at(b, h - 2, i))
                    act.activation(probs[:, h % 2, P_AT[i]:P_AT[i + 1]], ps_s[i % 2][:, 0:TRI[i]], ACT.Exp,
                                   bias=nmax[:, h % 2, i:i + 1], accum_out=sums[:, h % 2, i:i + 1]).then_inc(exp_ready[i], 1)

            def high_pT(heads, b, h, j):
                if h in heads:
                    act.wait_ge(pT_ps, row_at(b, h, j))
                    if h - 1 in heads:
                        act.wait_ge(pv_done, row_at(b, h - 1, j))
                    act.activation(pT[0][:, T_AT[j]:T_AT[j + 1]], ps_t[j % 2][:, 0:S - j * P], ACT.Copy).then_inc(pT_hi, 1)

            def high_z(heads, b, h):
                if h in heads:
                    act.wait_ge(pv_done, row_at(b, h, NT - 1))
                    if h - 1 in heads:
                        act.wait_ge(o_done, at(b, h - 1))
                    act.activation(zT[0][:], ps_z[:], ACT.Identity, bias=bias[:, 2, h % H1:h % H1 + 1]).then_inc(z_hi, 1)

            def high_wo(heads, b, h):
                if h in heads:
                    if h - 2 in heads:
                        act.wait_ge(o_done, at(b, h - 2))
                    act.activation(wo_parts[0][:, h % 2, :], wo_sb[:, h % H1, :], ACT.Copy).then_inc(wo_hi, 1)

            def high_xT(b, c):
                act.wait_ge(xT_ps, NC * b + c + 1)
                act.activation(xT[0][:, c, :], ps_proj[:], ACT.Copy).then_inc(xT_hi, 1)

            def one_batch(b, first, last):
                heads = heads_of(first, last)
                for s in slots_of(first, last):
                    if s == H1 - 1 and not last:
                        high_head(heads, b, s, 1)
                        exps(heads, b, s - 1, 2)
                        high_pT(heads, b, s - 2, 2)
                        high_xT(b + 1, 0)
                        high_pT(heads, b, s - 2, 3)
                        exps(heads, b, s - 1, 3)
                        high_wo(heads, b, s - 1)
                        high_xT(b + 1, 1)
                        high_z(heads, b, s - 2)
                        exps(heads, b, s, 0)
                        high_pT(heads, b, s - 1, 0)
                        raw_head(heads, b, s + 1, 0)
                        high_pT(heads, b, s - 1, 1)
                        exps(heads, b, s, 1)
                        raw_head(heads, b, s + 1, 1)
                        high_head(heads, b, s + 1, 0)
                        high_v(heads, b, s + 1)
                        continue
                    high_head(heads, b, s, 1)
                    exps(heads, b, s - 1, 2)
                    high_pT(heads, b, s - 2, 2)
                    high_pT(heads, b, s - 2, 3)
                    exps(heads, b, s - 1, 3)
                    high_wo(heads, b, s - 1)
                    raw_head(heads, b, s + 1, 0)
                    high_z(heads, b, s - 2)
                    raw_head(heads, b, s + 1, 1)
                    exps(heads, b, s, 0)
                    high_pT(heads, b, s - 1, 0)
                    high_head(heads, b, s + 1, 0)
                    high_pT(heads, b, s - 1, 1)
                    exps(heads, b, s, 1)
                    high_v(heads, b, s + 1)

            for c in range(NC):
                high_xT(0, c)
            act.wait_ge(loaded[3], 16)
            one_batch(0, True, False)
            with act.Fori(1, B - 1) as b:
                one_batch(b, False, False)
            one_batch(B - 1, False, True)

        @block.vector
        def _(dve):
            chain = Chain(dve, dve_steps)
            crossed, inverted = {}, {}

            def cross_part(heads, b, h, j):
                if h in heads:
                    dve.wait_ge(qk_raw[j], at(b, h))
                    for to, frm in ((slice(0, ROT), slice(ROT, P)), (slice(ROT, P), slice(0, ROT))):
                        crossed[j] = chain.step(dve.tensor_tensor(cross[to, j, :], raw[frm, j, :], sinT[frm, :], ALU.mult))

            def turn_head(heads, b, h, j):
                if h in heads:
                    chain.done(crossed[j])
                    dve.wait_ge(qk_cos[j], at(b, h))
                    dve.tensor_tensor(turn[:, j, :], turn[:, j, :], cross[:, j, :], ALU.add).then_inc(qk_turned[j], 1)

            def low_v(heads, b, part):
                if part in heads:
                    dve.wait_ge(v_hi, at(b, part))
                    t0 = 2 * (part % 2)
                    dve.tensor_tensor(v[1][:, (part // 2) % 2, t0:t0 + 2, :], ps_proj[:].rearrange("p (t n) -> p t n", t=2),
                                      v[0][:, (part // 2) % 2, t0:t0 + 2, :].bitcast(F32), ALU.subtract).then_inc(v_lo, 1)

            def maxima(heads, b, h, i):
                if h in heads:
                    dve.wait_ge(scores_ps[i], at(b, h))
                    dve.tensor_reduce(nmax[:, h % 2, i:i + 1], ps_s[i % 2][:, 0:TRI[i]], AX.X, ALU.max,
                                      negate=True).then_inc(max_ready[i], 1)

            def invert(heads, b, h, i):
                if h in heads:
                    dve.wait_ge(exp_ready[i], at(b, h))
                    inverted[i] = chain.step(dve.reciprocal(rsum[:, h % 2, i:i + 1], sums[:, h % 2, i:i + 1]))

            def normalize(heads, b, h, i):
                if h in heads:
                    if i in inverted:
                        chain.done(inverted[i])
                    pr = probs[:, h % 2, P_AT[i]:P_AT[i + 1]]
                    dve.tensor_scalar(pr, pr, rsum[:, h % 2, i:i + 1], None, ALU.mult).then_inc(probs_ready[i], 1)

            def low_pT(heads, b, h, j):
                if h in heads:
                    dve.wait_ge(pT_hi, row_at(b, h, j))
                    dve.tensor_tensor(pT[1][:, T_AT[j]:T_AT[j + 1]], ps_t[j % 2][:, 0:S - j * P],
                                      pT[0][:, T_AT[j]:T_AT[j + 1]].bitcast(F32), ALU.subtract).then_inc(pT_lo, 1)

            def low_z(heads, b, h):
                if h in heads:
                    dve.wait_ge(z_hi, at(b, h))
                    dve.scalar_tensor_tensor(out=zT[1][:], in0=ps_z[:], scalar=bias[:, 2, h % H1:h % H1 + 1],
                                             in1=zT[0][:].bitcast(F32), op0=ALU.add, op1=ALU.subtract).then_inc(z_lo, 1)

            def layernorm(b, piece):
                if piece == 0:
                    dve.wait_ge(x_loaded, 16 * b + 16)
                layernorm_piece(dve, chain, x_in, ln, x_in, xn_ready, piece)

            def low_xT(b, c):
                dve.wait_ge(xT_hi, NC * b + c + 1)
                dve.tensor_tensor(xT[1][:, c, :], ps_proj[:], xT[0][:, c, :].bitcast(F32), ALU.subtract).then_inc(xT_lo, 1)

            def add_residual(b):
                dve.wait_ge(res_ready, b + 1)
                dve.wait_ge(o_done, at(b, H1 - 1))
                for u in range(2):
                    dve.tensor_tensor(x_res[:, 2 * u:2 * u + 2, :], ps_o[u][:], x_res[:, 2 * u:2 * u + 2, :],
                                      ALU.add).then_inc(y_ready, 1)

            def one_batch(b, first, last):
                heads = heads_of(first, last)
                for s in slots_of(first, last):
                    if s == 2 and not first:
                        add_residual(b - 1)
                    if H1 // 2 <= s < H1 // 2 + LN_PIECES and not last:
                        layernorm(b + 1, s - H1 // 2)
                    if s == H1 - 1 and not last:
                        low_v(heads, b, s)
                        maxima(heads, b, s - 1, 3)
                        invert(heads, b, s - 1, 1)
                        normalize(heads, b, s - 1, 0)
                        invert(heads, b, s - 1, 2)
                        low_pT(heads, b, s - 2, 2)
                        low_xT(b + 1, 0)
                        low_pT(heads, b, s - 2, 3)
                        normalize(heads, b, s - 1, 2)
                        normalize(heads, b, s - 1, 1)
                        invert(heads, b, s - 1, 3)
                        normalize(heads, b, s - 1, 3)
                        low_xT(b + 1, 1)
                        maxima(heads, b, s, 0)
                        maxima(heads, b, s, 1)
                        low_z(heads, b, s - 2)
                        invert(heads, b, s, 0)
                        low_pT(heads, b, s - 1, 0)
                        cross_part(heads, b, s + 1, 0)
                        turn_head(heads, b, s + 1, 0)
                        low_pT(heads, b, s - 1, 1)
                        maxima(heads, b, s, 2)
                        cross_part(heads, b, s + 1, 1)
                        turn_head(heads, b, s + 1, 1)
                        continue
                    low_v(heads, b, s)
                    maxima(heads, b, s - 1, 3)
                    invert(heads, b, s - 1, 1)
                    normalize(heads, b, s - 1, 0)
                    invert(heads, b, s - 1, 2)
                    low_pT(heads, b, s - 2, 2)
                    low_pT(heads, b, s - 2, 3)
                    normalize(heads, b, s - 1, 2)
                    normalize(heads, b, s - 1, 1)
                    invert(heads, b, s - 1, 3)
                    normalize(heads, b, s - 1, 3)
                    maxima(heads, b, s, 0)
                    cross_part(heads, b, s + 1, 0)
                    maxima(heads, b, s, 1)
                    low_z(heads, b, s - 2)
                    turn_head(heads, b, s + 1, 0)
                    cross_part(heads, b, s + 1, 1)
                    invert(heads, b, s, 0)
                    low_pT(heads, b, s - 1, 0)
                    turn_head(heads, b, s + 1, 1)
                    low_pT(heads, b, s - 1, 1)
                    maxima(heads, b, s, 2)
                chain.restart()
                inverted.clear()

            for c in range(NC):
                low_xT(0, c)
            one_batch(0, True, False)
            with dve.Fori(1, B - 1) as b:
                one_batch(b, False, False)
            one_batch(B - 1, False, True)
            add_residual(B - 1)

        @block.tensor
        def _(pe):
            def project(heads, b, h, j):
                if h not in heads:
                    return
                if j == 1:
                    pe.wait_ge(qk_raw[0], at(b, h))
                elif h % H1 == 0:
                    pe.wait_ge(xT_lo, NC * (b + h // H1) + NC)
                else:
                    pe.wait_ge(v_lo, at(b, h - 1))
                n0 = h % H1 * HD1
                k = 0
                for c in range(NC):
                    for a, m in PASSES:
                        last = pe.matmul(ps_proj[:], w_parts[a][:, 1 - j, c, n0:n0 + HD1], xT[m][:, c, :],
                                         start=(k == 0), stop=(k == 3 * NC - 1))
                        k += 1
                last.then_inc(qk_ps[j], 1)

            def project_v(heads, b, part):
                if part not in heads:
                    return
                pe.wait_ge(qk_raw[1], at(b, part))
                n0 = part % H1 // 2 * 2 * HD1
                for u in range(2):
                    t = 2 * (part % 2) + u
                    k = 0
                    for c in range(NC):
                        for a, m in PASSES:
                            last = pe.matmul(ps_proj[:, u * 2 * HD1:(u + 1) * 2 * HD1], xT[a][:, c, t * P:(t + 1) * P],
                                             w_parts[m][:, 2, c, n0:n0 + 2 * HD1], start=(k == 0), stop=(k == 3 * NC - 1))
                            k += 1
                last.then_inc(v_ps, 1)

            def scores(heads, b, h, i):
                if h not in heads:
                    return
                for j in range(2):
                    pe.wait_ge(qk_lo[j], at(b, h))
                if i >= 2:
                    pe.wait_ge(exp_ready[i - 2], at(b, h))
                elif h - 1 in heads:
                    pe.wait_ge(exp_ready[i + 2], at(b, h - 1))
                for k, (a, m) in enumerate(PASSES):
                    pe.matmul(ps_s[i % 2][:, 0:TRI[i]], qkT[a][:, h % 2, 1, i * P:(i + 1) * P],
                              qkT[m][:, h % 2, 0, 0:TRI[i]], start=(k == 0), stop=False)
                pe.matmul(ps_s[i % 2][:, i * P:TRI[i]], ident_b[:], causal[:], start=False,
                          stop=True).then_inc(scores_ps[i], 1)

            def transposes(heads, b, h, j):
                if h not in heads:
                    return
                for i in range(j, NT):
                    pe.wait_ge(probs_ready[i], at(b, h))
                if j >= 2:
                    pe.wait_ge(pT_lo, row_at(b, h, j - 2))
                elif h - 1 in heads:
                    pe.wait_ge(pT_lo, row_at(b, h - 1, j + 2))
                for i in range(j, NT):
                    last = pe.transpose(ps_t[j % 2][:, (i - j) * P:(i - j + 1) * P],
                                        probs[:, h % 2, P_AT[i] + j * P:P_AT[i] + (j + 1) * P], ident[:])
                last.then_inc(pT_ps, 1)

            def values(heads, b, h, j):
                if h not in heads:
                    return
                pe.wait_ge(pT_lo, row_at(b, h, j))
                if j == 0:
                    pe.wait_ge(v_lo, at(b, 2 * (h // 2) + 1))
                    if h - 1 in heads:
                        pe.wait_ge(z_lo, at(b, h - 1))
                for k, (a, m) in enumerate(PASSES):
                    last = pe.matmul(ps_z[:, j * P:S], v[a][:, (h // 2) % 2, j, (h % 2) * HD1:(h % 2 + 1) * HD1],
                                     pT[m][:, T_AT[j]:T_AT[j + 1]], start=(j == 0 and k == 0),
                                     stop=(j == NT - 1 and k == 2), skip_group_check=True)
                last.then_inc(pv_done, 1)

            def outputs(heads, b, h):
                if h not in heads:
                    return
                pe.wait_ge(z_lo, at(b, h))
                pe.wait_ge(wo_lo, at(b, h))
                if h == 0 and h - 1 in heads:
                    pe.wait_ge(y_ready, 2 * b)
                for t in range(NT):
                    for k, (a, m) in enumerate(PASSES):
                        last = pe.matmul(ps_o[t // 2][:, t % 2, :], zT[a][:, t * P:(t + 1) * P],
                                         wo_parts[m][:, h % 2, :], start=(h % H1 == 0 and k == 0 and t % 2 == 0),
                                         stop=(h % H1 == H1 - 1 and k == 2), skip_group_check=True)
                last.then_inc(o_done, 1)

            def transpose_x(b, c, first=False):
                for t in range(NT):
                    pe.wait_ge(xn_ready, NT * b + t + 1)
                    if t == 0 and c >= 1:
                        pe.wait_ge(xT_lo, NC * b + c)
                    elif t == 0 and not first:
                        pe.wait_ge(v_lo, at(b, -1))
                    last = pe.transpose(ps_proj[:, t * P:(t + 1) * P], x_in[:, t, c * P:(c + 1) * P], ident[:])
                last.then_inc(xT_ps, 1)

            def one_batch(b, first, last):
                heads = heads_of(first, last)
                for s in slots_of(first, last):
                    if s == H1 - 1 and not last:
                        scores(heads, b, s, 0)
                        values(heads, b, s - 2, 2)
                        values(heads, b, s - 2, 3)
                        transpose_x(b + 1, 1)
                        transposes(heads, b, s - 1, 0)
                        transposes(heads, b, s - 1, 1)
                        outputs(heads, b, s - 2)
                        project(heads, b, s + 1, 0)
                        scores(heads, b, s, 2)
                        project(heads, b, s + 1, 1)
                        scores(heads, b, s, 3)
                        transposes(heads, b, s - 1, 2)
                        transposes(heads, b, s - 1, 3)
                        project_v(heads, b, s + 1)
                        values(heads, b, s - 1, 0)
                        values(heads, b, s - 1, 1)
                        project(heads, b, s + 2, 0)
                        scores(heads, b, s + 1, 1)
                        continue
                    scores(heads, b, s, 0)
                    values(heads, b, s - 2, 2)
                    values(heads, b, s - 2, 3)
                    project(heads, b, s + 1, 1)
                    transposes(heads, b, s - 1, 0)
                    transposes(heads, b, s - 1, 1)
                    project_v(heads, b, s + 1)
                    scores(heads, b, s, 2)
                    outputs(heads, b, s - 2)
                    scores(heads, b, s, 3)
                    transposes(heads, b, s - 1, 2)
                    transposes(heads, b, s - 1, 3)
                    values(heads, b, s - 1, 0)
                    values(heads, b, s - 1, 1)
                    if s == H1 - 2 and not last:
                        transpose_x(b + 1, 0)
                    else:
                        project(heads, b, s + 2, 0)
                    scores(heads, b, s + 1, 1)

            for c in range(NC):
                transpose_x(0, c, first=True)
            one_batch(0, True, False)
            with pe.Fori(1, B - 1) as b:
                one_batch(b, False, False)
            one_batch(B - 1, False, True)

E, TOP_K = 8, 2


def router_buffers(sb):
    names = {n: sb(f"r_{n}", [P, NT, E], F32) for n in ("logits", "e", "p", "rank", "mask", "w")}
    names.update({n: sb(f"r_{n}", [P, NT], F32) for n in ("max", "sum", "rsum")})
    names.update({n: sb(f"r_{n}", [P, NT, E, E], F32) for n in ("gt", "ge")})
    return names


def over_experts(v):
    return v.unsqueeze(2).to_broadcast([P, NT, E])


def top_k_mask(dve, chain, r, before):
    mine = r["p"][:].unsqueeze(3).to_broadcast([P, NT, E, E])
    other = r["p"][:].unsqueeze(2).to_broadcast([P, NT, E, E])
    chain.step(dve.tensor_tensor(r["gt"][:], other, mine, ALU.is_gt))
    chain.step(dve.tensor_tensor(r["ge"][:], other, mine, ALU.is_ge))
    chain.done()
    for t in range(NT):
        chain.step(dve.tensor_tensor(r["ge"][:, t, :, :], r["ge"][:, t, :, :], before[:], ALU.mult))
    chain.done()
    chain.step(dve.tensor_tensor(r["gt"][:], r["gt"][:], r["ge"][:], ALU.max))
    chain.done()
    chain.step(dve.tensor_reduce(r["rank"][:], r["gt"][:], AX.X, ALU.add))
    chain.done()
    chain.step(dve.tensor_scalar(r["mask"][:], r["rank"][:], TOP_K - 0.5, None, ALU.is_lt))
    chain.done()


def normalized(dve, chain, r, dst, v):
    chain.step(dve.tensor_reduce(r["sum"][:], v, AX.X, ALU.add))
    chain.done()
    chain.step(dve.reciprocal(r["rsum"][:], r["sum"][:]))
    chain.done()
    return dve.tensor_tensor(dst, v, over_experts(r["rsum"][:]), ALU.mult)


def make_before(pool, chain, m):
    chain.step(pool.memset(m, 1.0))
    chain.done()
    chain.step(pool.affine_select(out=m, in_=m, compare_op=ALU.is_gt, fill=0.0, base=0,
                                  pattern=[[1, E], [-1, E]], channel_multiplier=0))


HF = 176
NE0 = E + 1
FCH = -(-NE0 * HF // P)
FPAD = FCH * P
GROUP = S // P


def experts0(nc, x, wg, wu, wd, wgs, wus, wds, wr, br, rb, out):
    ctx = ExitStack()
    with ctx:
        def sb(name, shape, dt, stack=ctx):
            return stack.enter_context(nc.sbuf_tensor(f"b_{name}", shape, dt))

        def pb(name, shape, dt):
            return ctx.enter_context(nc.psum_tensor(f"b_{name}", shape, dt))

        def sem(name):
            return ctx.enter_context(nc.semaphore(f"b_{name}"))

        wgu = [sb(f"wgu{k}", [P, NC, NE0, 2 * HF], F32R) for k in range(2)]
        wdn = [sb(f"wdn{k}", [P, FCH, D], F32R) for k in range(2)]
        wrt = [sb(f"wrt{k}", [P, NC, E], F32R) for k in range(2)]
        ident = sb("ident", [P, P], F32)
        before = sb("before", [P, E, E], F32)
        rbias = sb("rbias", [P, 2, E], F32)

        loaded = [sem(f"loaded{i}") for i in range(4)]
        setup_hi = sem("setup_hi")
        setup_lo = sem("setup_lo")
        setup_pool = sem("setup_pool")
        cleared = sem("cleared")

        x_in = sb("x_in", [P, NT, D], F32)
        xn = sb("xn", [P, NT, D], F32)
        ln = layernorm_buffers(sb, "b")
        x_loaded = sem("x_loaded")
        xn_ready = sem("xn_ready")
        dve_steps = sem("dve_steps")

        with ExitStack() as setup:
            wgu_in = sb("wgu_in", [P, NC, NE0, 2 * HF], F32, setup)
            wdn_in = sb("wdn_in", [P, FCH, D], F32, setup)
            wrt_in = sb("wrt_in", [P, NC, E], F32, setup)
            block = setup.enter_context(nc.Block())
            full = E * HF // P
            rest = NE0 * HF - full * P

            @block.sync
            def _(sp):
                sp.dma_start(x_in[:], token_tiles(x, 0)).then_inc(x_loaded, 16)
                for c in range(NC):
                    rows = slice(c * P, (c + 1) * P)
                    sp.dma_start(wgu_in[:, c, 0:E, 0:HF], wg[:, rows, :].rearrange("e p h -> p e h")).then_inc(loaded[0], 16)
                    sp.dma_start(wgu_in[:, c, 0:E, HF:2 * HF], wu[:, rows, :].rearrange("e p h -> p e h")).then_inc(loaded[0], 16)
                    sp.dma_start(wgu_in[:, c, E, 0:HF], wgs[rows, :]).then_inc(loaded[0], 16)
                    sp.dma_start(wgu_in[:, c, E, HF:2 * HF], wus[rows, :]).then_inc(loaded[0], 16)
                sp.wait_ge(cleared, 1)
                sp.dma_start(wdn_in[:, 0:full, :], wd.rearrange("e h d -> (e h) d").rearrange("(k p) d -> p k d", p=P)).then_inc(loaded[1], 16)
                sp.dma_start(wdn_in[:, full, :], wds[0:P, :]).then_inc(loaded[1], 16)
                sp.dma_start(wdn_in[0:rest - P, full + 1, :], wds[P:HF, :]).then_inc(loaded[1], 16)
                sp.dma_start(wrt_in[:], wr.rearrange("(c p) e -> p c e", p=P)).then_inc(loaded[2], 16)
                sp.dma_start(rbias[:, 0, :], row_to_all(br)).then_inc(loaded[3], 16)
                sp.dma_start(rbias[:, 1, :], row_to_all(rb)).then_inc(loaded[3], 16)

            @block.gpsimd
            def _(pool):
                chain = Chain(pool, setup_pool)
                make_identity(pool, chain, ident[:])
                make_before(pool, chain, before[:])
                chain.done()

            parts = ((wgu, wgu_in, 0, 16 * 4 * NC), (wdn, wdn_in, 1, 16 * 3), (wrt, wrt_in, 2, 16))

            @block.scalar
            def _(act):
                for w, w_in, k, n in parts:
                    act.wait_ge(loaded[k], n)
                    act.activation(w[0][:], w_in[:], ACT.Copy).then_inc(setup_hi, 1)

            @block.vector
            def _(dve):
                dve.memset(wdn_in[:, full + 1, :], 0.0).then_inc(cleared, 1)
                chain = Chain(dve, dve_steps)
                dve.wait_ge(x_loaded, 16)
                for piece in range(LN_PIECES):
                    layernorm_piece(dve, chain, x_in, ln, xn, xn_ready, piece)
                chain.restart()
                for i, (w, w_in, k, n) in enumerate(parts):
                    dve.wait_ge(setup_hi, i + 1)
                    dve.tensor_tensor(w[1][:], w_in[:], w[0][:].bitcast(F32), ALU.subtract).then_inc(setup_lo, 1)
                dve.wait_ge(loaded[3], 32)
                dve.tensor_tensor(rbias[:, 0, :], rbias[:, 0, :], rbias[:, 1, :], ALU.add).then_inc(setup_lo, 1)

        x_res = sb("x_res", [P, NT, D], F32)
        x_out = sb("x_out", [P, NT, D], F32)
        r = router_buffers(sb)
        xT = [sb(f"xT{k}", [P, NC, S], F32R) for k in range(2)]
        act_g = sb("act_g", [P, 4, HF], F32)
        hid = sb("hid", [P, NT, FPAD], F32)
        hT = [sb(f"hT{k}", [P, FCH, P], F32R) for k in range(2)]

        ps_gu = [pb(f"ps_gu{i}", [P, S], F32) for i in range(4)]
        ps_t = [pb(f"ps_t{i}", [P, GROUP, P], F32) for i in range(2)]
        ps_y = [pb(f"ps_y{i}", [P, S], F32) for i in range(2)]
        ps_xT = ps_gu[0:2]
        ps_r = ps_t[0][:, 0, 0:NT * E]

        x_taken = sem("x_taken")
        xT_ps = sem("xT_ps")
        xT_hi = sem("xT_hi")
        xT_lo = sem("xT_lo")
        router_ps = sem("router_ps")
        logits_ready = sem("logits_ready")
        odds_ready = sem("odds_ready")
        gu_ps = sem("gu_ps")
        silu_ready = sem("silu_ready")
        hid_ready = sem("hid_ready")
        hT_ps = sem("hT_ps")
        hT_hi = sem("hT_hi")
        hT_lo = sem("hT_lo")
        y_ps = sem("y_ps")
        y_ready = sem("y_ready")
        x_out_free = sem("x_out_free")
        stored = sem("stored")

        STEPS = NE0 * NT

        def step_of(t, e):
            return t if e == E else NT + E * t + e

        n_groups = -(-FCH // GROUP)
        groups = [range(g * GROUP, min(FCH, (g + 1) * GROUP)) for g in range(n_groups)]
        block = ctx.enter_context(nc.Block())

        @block.sync
        def _(sp):
            with sp.Fori(0, B - 1) as b:
                sp.wait_ge(x_taken, b + 1)
                sp.dma_start(x_in[:], token_tiles(x, b + 1)).then_inc(x_loaded, 16)

        @block.gpsimd
        def _(pool):
            pool.sem_inc(x_out_free, 1)
            with pool.Fori(0, B) as b:
                pool.wait_ge(y_ready, NT * b + NT)
                pool.dma_start(token_tiles(out, b), x_out[:]).then_inc(stored, 16)
                pool.wait_ge(stored, 16 * (b + 1))
                pool.sem_inc(x_out_free, 1)

        @block.scalar
        def _(act):
            def high_xT(b, c):
                act.wait_ge(xT_ps, NC * b + c + 1)
                act.activation(xT[0][:, c, :], ps_xT[c][:], ACT.Copy).then_inc(xT_hi, 1)

            def silu(b, step):
                act.wait_ge(gu_ps, STEPS * b + step + 1)
                if step >= 4:
                    act.wait_ge(hid_ready, STEPS * b + step - 3)
                act.activation(act_g[:, step % 4, :], ps_gu[step % 4][:, 0:HF], ACT.Silu).then_inc(silu_ready, 1)

            def high_hT(b, t, g):
                act.wait_ge(hT_ps, n_groups * (NT * b + t) + g + 1)
                k = groups[g]
                act.activation(hT[0][:, k.start:k.stop, :], ps_t[g % 2][:, 0:len(k), :], ACT.Copy).then_inc(hT_hi, 1)

            def turn(b, more):
                act.wait_ge(logits_ready, b + 1)
                act.activation(r["e"][:], r["logits"][:], ACT.Exp, scale=-1.0).then_inc(odds_ready, 1)
                for t in range(NT):
                    silu(b, step_of(t, E))
                for t in range(NT):
                    for e in range(E):
                        silu(b, step_of(t, e))
                        if t >= 1 and e < n_groups:
                            high_hT(b, t - 1, e)
                for g in range(n_groups):
                    high_hT(b, NT - 1, g)
                    if g == 1:
                        for c in range(NC if more else 0):
                            high_xT(b + 1, c)

            for c in range(NC):
                high_xT(0, c)
            with act.Fori(0, B - 1) as b:
                turn(b, True)
            turn(B - 1, False)

        @block.vector
        def _(dve):
            chain = Chain(dve, dve_steps)
            chain.step(dve.memset(hid[:], 0.0))

            def normalize(b, piece):
                if piece == 0:
                    dve.wait_ge(x_loaded, 16 * b + 16)
                layernorm_piece(dve, chain, x_in, ln, xn, xn_ready, piece)

            def low_xT(b, c):
                dve.wait_ge(xT_hi, NC * b + c + 1)
                dve.tensor_tensor(xT[1][:, c, :], ps_xT[c][:], xT[0][:, c, :].bitcast(F32),
                                  ALU.subtract).then_inc(xT_lo, 1)

            def low_hT(b, t, g):
                dve.wait_ge(hT_hi, n_groups * (NT * b + t) + g + 1)
                k = groups[g]
                dve.tensor_tensor(hT[1][:, k.start:k.stop, :], ps_t[g % 2][:, 0:len(k), :],
                                  hT[0][:, k.start:k.stop, :].bitcast(F32), ALU.subtract).then_inc(hT_lo, 1)

            def hidden(b, t, e):
                step = step_of(t, e)
                dve.wait_ge(silu_ready, STEPS * b + step + 1)
                dst, up = hid[:, t, e * HF:(e + 1) * HF], ps_gu[step % 4][:, HF:2 * HF]
                if e == E:
                    dve.tensor_tensor(dst, act_g[:, step % 4, :], up, ALU.mult).then_inc(hid_ready, 1)
                else:
                    dve.scalar_tensor_tensor(out=dst, in0=act_g[:, step % 4, :], scalar=r["w"][:, t, e:e + 1],
                                             in1=up, op0=ALU.mult, op1=ALU.mult).then_inc(hid_ready, 1)

            def add_residual(b, t):
                if t == 0:
                    dve.wait_ge(x_out_free, b + 1)
                    dve.wait_ge(x_taken, b + 1)
                dve.wait_ge(y_ps, NT * b + t + 1)
                dve.tensor_tensor(x_out[:, t, :], ps_y[t % 2][:, 0:D], x_res[:, t, :],
                                  ALU.add).then_inc(y_ready, 1)

            def turn(b, more):
                dve.wait_ge(router_ps, b + 1)
                dve.tensor_tensor(r["logits"][:], ps_r.rearrange("p (t e) -> p t e", e=E),
                                  rbias[:, 0, :].unsqueeze(1).to_broadcast([P, NT, E]), ALU.add).then_inc(logits_ready, 1)
                dve.wait_ge(odds_ready, b + 1)
                chain.step(dve.tensor_scalar(r["e"][:], r["e"][:], 1.0, None, ALU.add))
                chain.done()
                chain.step(dve.reciprocal(r["p"][:], r["e"][:]))
                chain.done()
                top_k_mask(dve, chain, r, before)
                chain.step(dve.tensor_tensor(r["e"][:], r["p"][:], r["mask"][:], ALU.mult))
                chain.done()
                chain.step(normalized(dve, chain, r, r["w"][:], r["e"][:]))
                chain.done()
                for t in range(NT):
                    hidden(b, t, E)
                for t in range(NT):
                    for e in range(E):
                        hidden(b, t, e)
                        if t >= 1 and e < n_groups:
                            low_hT(b, t - 1, e)
                        if t >= 1 and e == n_groups + 1:
                            add_residual(b, t - 1)
                        if more and t == 0 and e < LN_PIECES:
                            normalize(b + 1, e)
                for g in range(n_groups):
                    low_hT(b, NT - 1, g)
                    if g == 1:
                        for c in range(NC if more else 0):
                            low_xT(b + 1, c)
                add_residual(b, NT - 1)
                if more:
                    dve.wait_ge(y_ready, NT * b + NT)
                    dve.tensor_copy(x_res[:], x_in[:]).then_inc(x_taken, 1)
                chain.restart()

            for c in range(NC):
                low_xT(0, c)
            dve.tensor_copy(x_res[:], x_in[:]).then_inc(x_taken, 1)
            chain.restart()
            with dve.Fori(0, B - 1) as b:
                turn(b, True)
            turn(B - 1, False)

        @block.tensor
        def _(pe):
            def transpose_x(b, c):
                for t in range(NT):
                    pe.wait_ge(xn_ready, NT * b + t + 1)
                    last = pe.transpose(ps_xT[c][:, t * P:(t + 1) * P], xn[:, t, c * P:(c + 1) * P], ident[:])
                last.then_inc(xT_ps, 1)

            def gate_up(b, t, e):
                step = step_of(t, e)
                if step >= 4:
                    pe.wait_ge(hid_ready, STEPS * b + step - 3)
                k = 0
                for c in range(NC):
                    for a, m in PASSES:
                        last = pe.matmul(ps_gu[step % 4][:, 0:2 * HF], xT[a][:, c, t * P:(t + 1) * P],
                                         wgu[m][:, c, e, :], start=(k == 0), stop=(k == 3 * NC - 1))
                        k += 1
                last.then_inc(gu_ps, 1)

            def transposes(b, t, g):
                if g == 0:
                    pe.wait_ge(hid_ready, STEPS * b + step_of(t, E - 1) + 1)
                if g >= 2 or t >= 1:
                    pe.wait_ge(hT_lo, n_groups * (NT * b + t) + g - 1)
                for k in groups[g]:
                    last = pe.transpose(ps_t[g % 2][:, k - groups[g].start, :], hid[:, t, k * P:(k + 1) * P], ident[:])
                last.then_inc(hT_ps, 1)

            def down(b, t, g):
                pe.wait_ge(hT_lo, n_groups * (NT * b + t) + g + 1)
                if g == 0 and t >= 2:
                    pe.wait_ge(y_ready, NT * b + t - 1)
                for k in groups[g]:
                    for i, (a, m) in enumerate(PASSES):
                        last = pe.matmul(ps_y[t % 2][:, 0:D], hT[a][:, k, :], wdn[m][:, k, :],
                                         start=(k == 0 and i == 0), stop=(k == FCH - 1 and i == 2))
                if g == n_groups - 1:
                    last.then_inc(y_ps, 1)

            def turn(b, more):
                pe.wait_ge(xT_lo, NC * b + NC)
                for t in range(NT):
                    k = 0
                    for c in range(NC):
                        for a, m in PASSES:
                            last = pe.matmul(ps_r[:, t * E:(t + 1) * E], xT[a][:, c, t * P:(t + 1) * P], wrt[m][:, c, :],
                                             start=(k == 0), stop=(k == 3 * NC - 1))
                            k += 1
                last.then_inc(router_ps, 1)
                for t in range(NT):
                    gate_up(b, t, E)
                for t in range(NT):
                    for e in range(E):
                        gate_up(b, t, e)
                        if t >= 1 and e < n_groups:
                            transposes(b, t - 1, e)
                        if t >= 1 and 1 <= e <= n_groups:
                            down(b, t - 1, e - 1)
                transposes(b, NT - 1, 0)
                transposes(b, NT - 1, 1)
                for c in range(NC if more else 0):
                    transpose_x(b + 1, c)
                for g in range(n_groups):
                    down(b, NT - 1, g)
                    if g + 2 < n_groups:
                        transposes(b, NT - 1, g + 2)

            for c in range(NC):
                transpose_x(0, c)
            with pe.Fori(0, B - 1) as b:
                turn(b, True)
            turn(B - 1, False)


FW = 128
DEPTH = 4


def experts1(nc, x, wr, w1, b1, w2, b2, out):
    ctx = ExitStack()
    with ctx:
        def sb(name, shape, dt, stack=ctx):
            return stack.enter_context(nc.sbuf_tensor(f"d_{name}", shape, dt))

        def pb(name, shape, dt):
            return ctx.enter_context(nc.psum_tensor(f"d_{name}", shape, dt))

        def sem(name):
            return ctx.enter_context(nc.semaphore(f"d_{name}"))

        wup = [sb(f"wup{k}", [P, NC, E, FW], F32R) for k in range(2)]
        wdn = [sb(f"wdn{k}", [P, E, D], F32R) for k in range(2)]
        wrt = [sb(f"wrt{k}", [P, NC, E], F32R) for k in range(2)]
        b2p = [sb(f"b2p{k}", [P, D], F32R) for k in range(2)]
        sel = sb("sel", [P, E, P], F32R)
        b1_sb = sb("b1", [P, E], F32)
        ident = sb("ident", [P, P], F32)
        before = sb("before", [P, E, E], F32)

        loaded = [sem(f"loaded{i}") for i in range(5)]
        setup_hi = sem("setup_hi")
        setup_lo = sem("setup_lo")
        setup_pool = sem("setup_pool")
        cleared = sem("cleared")

        x_in = sb("x_in", [P, NT, D], F32)
        xn = sb("xn", [P, NT, D], F32)
        ln = layernorm_buffers(sb, "d")
        x_loaded = sem("x_loaded")
        xn_ready = sem("xn_ready")
        dve_steps = sem("dve_steps")

        with ExitStack() as setup:
            wup_in = sb("wup_in", [P, NC, E, FW], F32, setup)
            wdn_in = sb("wdn_in", [P, E, D], F32, setup)
            wrt_in = sb("wrt_in", [P, NC, E], F32, setup)
            b2_in = sb("b2_in", [P, D], F32, setup)
            sel_in = sb("sel_in", [P, E, P], F32, setup)
            block = setup.enter_context(nc.Block())

            @block.sync
            def _(sp):
                sp.dma_start(x_in[:], token_tiles(x, 0)).then_inc(x_loaded, 16)
                for c in range(NC):
                    sp.dma_start(wup_in[:, c, :, :], w1[:, c * P:(c + 1) * P, :].rearrange("e p f -> p e f")).then_inc(loaded[0], 16)
                sp.dma_start(wdn_in[:], w2.rearrange("e f d -> f e d")).then_inc(loaded[1], 16)
                sp.dma_start(wrt_in[:], wr.rearrange("(c p) e -> p c e", p=P)).then_inc(loaded[2], 16)
                sp.dma_start(b1_sb[:], b1).then_inc(loaded[4], 16)
                sp.wait_ge(cleared, 1)
                sp.dma_start(b2_in[0:E, :], b2).then_inc(loaded[3], 16)
                sp.wait_ge(loaded[4], 16)

            @block.gpsimd
            def _(pool):
                chain = Chain(pool, setup_pool)
                make_identity(pool, chain, ident[:])
                make_before(pool, chain, before[:])
                chain.step(pool.memset(sel_in[:], 0.0))
                chain.done()
                chain.step(pool.affine_select(out=sel_in[:], in_=sel_in[:], compare_op=ALU.not_equal, fill=1.0, base=0,
                                              pattern=[[-1, E], [0, P]], channel_multiplier=1))
                chain.done()

            parts = ((wup, wup_in, 0, 16 * NC), (wdn, wdn_in, 1, 16), (wrt, wrt_in, 2, 16), (b2p, b2_in, 3, 16))

            @block.scalar
            def _(act):
                for w, w_in, k, n in parts:
                    act.wait_ge(loaded[k], n)
                    act.activation(w[0][:], w_in[:], ACT.Copy).then_inc(setup_hi, 1)
                act.wait_ge(setup_pool, 6)
                act.activation(sel[:], sel_in[:], ACT.Copy).then_inc(setup_hi, 1)

            @block.vector
            def _(dve):
                dve.memset(b2_in[:], 0.0).then_inc(cleared, 1)
                chain = Chain(dve, dve_steps)
                dve.wait_ge(x_loaded, 16)
                for piece in range(LN_PIECES):
                    layernorm_piece(dve, chain, x_in, ln, xn, xn_ready, piece)
                chain.restart()
                for i, (w, w_in, k, n) in enumerate(parts):
                    dve.wait_ge(setup_hi, i + 1)
                    dve.tensor_tensor(w[1][:], w_in[:], w[0][:].bitcast(F32), ALU.subtract).then_inc(setup_lo, 1)

        x_res = sb("x_res", [P, NT, D], F32)
        x_out = sb("x_out", [P, NT, D], F32)
        r = router_buffers(sb)
        logitsT = sb("logitsT", [P, S], F32)
        shares = sb("shares", [P, NT, P], F32)
        shT = [sb(f"shT{k}", [P, S], F32R) for k in range(2)]
        xT = [sb(f"xT{k}", [P, NC, S], F32R) for k in range(2)]
        gel = sb("gel", [P, E, S], F32)
        hid = sb("hid", [P, DEPTH, S], F32)
        hid_parts = [sb(f"hid{k}", [P, DEPTH, S], F32R) for k in range(2)]

        ps_u = [pb(f"ps_u{i}", [P, S], F32) for i in range(4)]
        ps_c = ps_u[2:4]
        ps_y = [pb(f"ps_y{i}", [P, 2, D], F32) for i in range(2)]
        ps_m = [pb(f"ps_m{i}", [P, S], F32) for i in range(2)]

        x_taken = sem("x_taken")
        xT_ps = sem("xT_ps")
        xT_hi = sem("xT_hi")
        xT_lo = sem("xT_lo")
        rows_cleared = sem("rows_cleared")
        routerT_ps = sem("routerT_ps")
        routerT_sb = sem("routerT_sb")
        router_ps = sem("router_ps")
        shifted_ready = sem("shifted_ready")
        exp_ready = sem("exp_ready")
        shares_ready = sem("shares_ready")
        shT_ps = sem("shT_ps")
        shT_hi = sem("shT_hi")
        shT_lo = sem("shT_lo")
        u_ps = sem("u_ps")
        gelu_ready = sem("gelu_ready")
        c_ps = sem("c_ps")
        hid_ready = sem("hid_ready")
        hid_hi = sem("hid_hi")
        hid_lo = sem("hid_lo")
        down_done = sem("down_done")
        y_ready = sem("y_ready")
        x_out_free = sem("x_out_free")
        stored = sem("stored")

        block = ctx.enter_context(nc.Block())

        @block.sync
        def _(sp):
            with sp.Fori(0, B - 1) as b:
                sp.wait_ge(x_taken, b + 1)
                sp.dma_start(x_in[:], token_tiles(x, b + 1)).then_inc(x_loaded, 16)

        @block.gpsimd
        def _(pool):
            pool.sem_inc(x_out_free, 1)
            with pool.Fori(0, B) as b:
                for e in range(E):
                    pool.wait_ge(hid_hi, E * b + e + 1)
                    pool.tensor_tensor(hid_parts[1][:, e % DEPTH, :], hid[:, e % DEPTH, :],
                                       hid_parts[0][:, e % DEPTH, :].bitcast(F32), ALU.subtract).then_inc(hid_lo, 1)
                pool.wait_ge(y_ready, 2 * b + 2)
                pool.dma_start(token_tiles(out, b), x_out[:]).then_inc(stored, 16)
                pool.wait_ge(stored, 16 * (b + 1))
                pool.sem_inc(x_out_free, 1)

        @block.scalar
        def _(act):
            def high_xT(b, c):
                act.wait_ge(xT_ps, NC * b + c + 1)
                act.activation(xT[0][:, c, :], ps_m[c][:], ACT.Copy).then_inc(xT_hi, 1)

            def exp(b, k):
                act.wait_ge(shifted_ready, 2 * b + k + 1)
                act.activation(r["e"][:], r["logits"][:], ACT.Exp).then_inc(exp_ready, 1)

            def gelu(b, e):
                act.wait_ge(u_ps, E * b + e + 1)
                act.activation(gel[:, e, :], ps_u[e % 4][:], ACT.Gelu, bias=b1_sb[:, e:e + 1]).then_inc(gelu_ready, 1)

            def high_hid(b, e):
                act.wait_ge(hid_ready, E * b + e + 1)
                if e >= DEPTH:
                    act.wait_ge(down_done, E * b + e - DEPTH + 1)
                act.activation(hid_parts[0][:, e % DEPTH, :], hid[:, e % DEPTH, :], ACT.Copy).then_inc(hid_hi, 1)

            def turn(b, more):
                act.wait_ge(routerT_ps, b + 1)
                act.activation(logitsT[0:E, :], ps_m[0][0:E, :], ACT.Copy).then_inc(routerT_sb, 1)
                exp(b, 0)
                for e in range(E // 2):
                    gelu(b, e)
                exp(b, 1)
                for e in range(E // 2, E):
                    gelu(b, e)
                act.wait_ge(shT_ps, b + 1)
                act.activation(shT[0][:], ps_m[1][:], ACT.Copy).then_inc(shT_hi, 1)
                for e in range(E):
                    high_hid(b, e)
                for c in range(NC if more else 0):
                    high_xT(b + 1, c)

            for c in range(NC):
                high_xT(0, c)
            act.wait_ge(rows_cleared, 1)
            with act.Fori(0, B - 1) as b:
                turn(b, True)
            turn(B - 1, False)

        @block.vector
        def _(dve):
            chain = Chain(dve, dve_steps)
            chain.step(dve.memset(shares[:], 0.0))
            chain.step(dve.memset(logitsT[:], 0.0))
            chain.done()
            dve.sem_inc(rows_cleared, 1)

            def low_xT(b, c):
                dve.wait_ge(xT_hi, NC * b + c + 1)
                dve.tensor_tensor(xT[1][:, c, :], ps_m[c][:], xT[0][:, c, :].bitcast(F32),
                                  ALU.subtract).then_inc(xT_lo, 1)

            def normalize(b, piece):
                if piece == 0:
                    dve.wait_ge(x_loaded, 16 * b + 16)
                layernorm_piece(dve, chain, x_in, ln, xn, xn_ready, piece)

            def turn(b, more):
                dve.wait_ge(router_ps, b + 1)
                lg = ps_m[0][:].rearrange("p (t e) -> p t e", e=P)[:, :, 0:E]
                chain.step(dve.tensor_reduce(r["max"][:], lg, AX.X, ALU.max))
                chain.done()
                dve.tensor_tensor(r["logits"][:], lg, over_experts(r["max"][:]), ALU.subtract).then_inc(shifted_ready, 1)
                dve.wait_ge(exp_ready, 2 * b + 1)
                chain.step(normalized(dve, chain, r, r["p"][:], r["e"][:]))
                chain.done()
                top_k_mask(dve, chain, r, before)
                chain.step(dve.tensor_reduce(r["max"][:], r["p"][:], AX.X, ALU.max))
                chain.done()
                dve.tensor_tensor(r["logits"][:], r["p"][:], over_experts(r["max"][:]), ALU.subtract).then_inc(shifted_ready, 1)
                dve.wait_ge(exp_ready, 2 * b + 2)
                chain.step(dve.tensor_tensor(r["w"][:], r["e"][:], r["mask"][:], ALU.mult))
                chain.done()
                normalized(dve, chain, r, shares[:, :, 0:E], r["w"][:]).then_inc(shares_ready, 1)
                dve.wait_ge(shT_hi, b + 1)
                dve.tensor_tensor(shT[1][:], ps_m[1][:], shT[0][:].bitcast(F32), ALU.subtract).then_inc(shT_lo, 1)
                for e in range(E):
                    dve.wait_ge(gelu_ready, E * b + e + 1)
                    dve.wait_ge(c_ps, E * b + e + 1)
                    if e >= DEPTH:
                        dve.wait_ge(hid_lo, E * b + e - DEPTH + 1)
                    dve.tensor_tensor(hid[:, e % DEPTH, :], gel[:, e, :], ps_c[e % 2][:], ALU.mult).then_inc(hid_ready, 1)
                    if more and e < LN_PIECES:
                        normalize(b + 1, e)
                for c in range(NC if more else 0):
                    low_xT(b + 1, c)
                dve.wait_ge(x_out_free, b + 1)
                dve.wait_ge(x_taken, b + 1)
                dve.wait_ge(down_done, E * b + E)
                for u in range(2):
                    dve.tensor_tensor(x_out[:, 2 * u:2 * u + 2, :], ps_y[u][:], x_res[:, 2 * u:2 * u + 2, :],
                                      ALU.add).then_inc(y_ready, 1)
                if more:
                    dve.wait_ge(y_ready, 2 * b + 2)
                    dve.tensor_copy(x_res[:], x_in[:]).then_inc(x_taken, 1)
                chain.restart()

            for c in range(NC):
                low_xT(0, c)
            dve.tensor_copy(x_res[:], x_in[:]).then_inc(x_taken, 1)
            chain.restart()
            with dve.Fori(0, B - 1) as b:
                turn(b, True)
            turn(B - 1, False)

        @block.tensor
        def _(pe):
            def transpose_x(b, c):
                for t in range(NT):
                    pe.wait_ge(xn_ready, NT * b + t + 1)
                    last = pe.transpose(ps_m[c][:, t * P:(t + 1) * P], xn[:, t, c * P:(c + 1) * P], ident[:])
                last.then_inc(xT_ps, 1)

            def up(b, e):
                if e >= 4:
                    pe.wait_ge(gelu_ready, E * b + e - 3)
                k = 0
                for c in range(NC):
                    for a, m in PASSES:
                        last = pe.matmul(ps_u[e % 4][:], wup[a][:, c, e, :], xT[m][:, c, :], start=(k == 0), stop=(k == 3 * NC - 1))
                        k += 1
                last.then_inc(u_ps, 1)

            def spread(b, e):
                if e < 2:
                    pe.wait_ge(gelu_ready, E * b + E - 1 + e)
                else:
                    pe.wait_ge(hid_ready, E * b + e - 1)
                for m in range(2):
                    last = pe.matmul(ps_c[e % 2][:], sel[:, e, :], shT[m][:], start=(m == 0), stop=(m == 1))
                last.then_inc(c_ps, 1)

            def down(b, e):
                pe.wait_ge(hid_lo, E * b + e + 1)
                for t in range(NT):
                    for k, (a, m) in enumerate(PASSES):
                        last = pe.matmul(ps_y[t // 2][:, t % 2, :], hid_parts[a][:, e % DEPTH, t * P:(t + 1) * P], wdn[m][:, e, :],
                                         start=False, stop=(e == E - 1 and k == 2), skip_group_check=True)
                last.then_inc(down_done, 1)

            def turn(b, more):
                pe.wait_ge(xT_lo, NC * b + NC)
                k = 0
                for c in range(NC):
                    for a, m in PASSES:
                        last = pe.matmul(ps_m[0][0:E, :], wrt[a][:, c, :], xT[m][:, c, :], start=(k == 0), stop=(k == 3 * NC - 1))
                        k += 1
                last.then_inc(routerT_ps, 1)
                up(b, 0)
                pe.wait_ge(routerT_sb, b + 1)
                for t in range(NT):
                    last = pe.transpose(ps_m[0][:, t * P:(t + 1) * P], logitsT[:, t * P:(t + 1) * P], ident[:])
                last.then_inc(router_ps, 1)
                for e in range(1, E):
                    up(b, e)
                pe.wait_ge(shares_ready, b + 1)
                for t in range(NT):
                    last = pe.transpose(ps_m[1][:, t * P:(t + 1) * P], shares[:, t, :], ident[:])
                last.then_inc(shT_ps, 1)
                pe.wait_ge(shT_lo, b + 1)
                spread(b, 0)
                spread(b, 1)
                for t in range(NT):
                    for k, (a, m) in enumerate(PASSES):
                        pe.matmul(ps_y[t // 2][:, t % 2, :], shT[a][:, t * P:(t + 1) * P], b2p[m][:],
                                  start=(k == 0 and t % 2 == 0), stop=False, skip_group_check=True)
                for e in range(E):
                    if e + 2 < E:
                        spread(b, e + 2)
                    if more and e == E - 2:
                        for c in range(NC):
                            transpose_x(b + 1, c)
                    down(b, e)

            for c in range(NC):
                transpose_x(0, c)
            with pe.Fori(0, B - 1) as b:
                turn(b, True)
            turn(B - 1, False)


def preln_stack(nc, x, out, a, f, g, e, cs0, sn0, cs1, sn1):
    mid = [nc.dram_tensor(f"x_after_{n}", (B, S, D), F32, kind="Internal").ap() for n in ("attention0", "experts0", "attention1")]
    attention0(nc, x, *a, cs0, sn0, mid[0])
    experts0(nc, mid[0], *f, mid[1])
    attention1(nc, mid[1], *g, cs1, sn1, mid[2])
    experts1(nc, mid[2], *e, out)


def rope_tables(n, width):
    import numpy as np

    inv = (1.0 / 10000.0 ** (np.arange(0, width, 2, dtype=np.float32) / width)).astype(np.float32)
    freqs = np.outer(np.arange(n, dtype=np.float32), inv)
    return np.cos(freqs).astype(np.float32), np.sin(freqs).astype(np.float32)


def kernel(**inputs):
    import numpy as np
    import concourse.bacc as bacc
    from concourse.bass_utils import run_bass_kernel_spmd

    i = {k: np.asarray(v) for k, v in inputs.items()}
    cs0, sn0 = rope_tables(S, HD0)
    cs1, sn1 = rope_tables(S, HD1)

    def heads(w):
        return w.reshape(H1, D, ROT, 2).transpose(1, 0, 3, 2).reshape(D, H1 * HD1)

    def head_bias(v):
        return v.reshape(H1, ROT, 2).transpose(2, 1, 0).reshape(HD1, H1)

    groups = {
        "x": [i["L0_attn_x"]],
        "a": [i["L0_attn_" + n] for n in ("wq", "bq", "wk", "bk", "wv", "bv", "wo", "bo", "q_norm_scale", "k_norm_scale")],
        "f": [i["L0_ffn_" + n] for n in ("Wg", "Wu", "Wd", "Wg_s", "Wu_s", "Wd_s", "Wr", "br", "rb")],
        "g": [heads(i["L1_attn_W_Q"]), head_bias(i["L1_attn_b_Q"]), heads(i["L1_attn_W_K"]), head_bias(i["L1_attn_b_K"]),
              i["L1_attn_W_V"].transpose(1, 0, 2).reshape(D, H1 * HD1), i["L1_attn_b_V"].T, i["L1_attn_W_O"], i["L1_attn_b_O"]],
        "e": [i["L1_ffn_w_gate"], i["L1_ffn_W1"], i["L1_ffn_b1"].T, i["L1_ffn_W2"], i["L1_ffn_b2"]],
        "t": [cs0, sn0, cs1.T, sn1.T],
    }
    nc = bacc.Bacc("TRN2", target_bir_lowering=False, num_devices=1)
    arrays, args = {}, {}
    for name, group in groups.items():
        args[name] = []
        for n, v in enumerate(group):
            v = np.ascontiguousarray(v)
            arrays[f"in_{name}{n}"] = v
            args[name].append(nc.dram_tensor(f"in_{name}{n}", v.shape, mybir.dt.from_np(v.dtype), kind="ExternalInput").ap())
    out = nc.dram_tensor("out", (B, S, D), F32, kind="ExternalOutput").ap()
    preln_stack(nc, args["x"][0], out, args["a"], args["f"], args["g"], args["e"], *args["t"])
    r = run_bass_kernel_spmd(nc, [arrays], core_ids=[0])
    return r.results[0]["out"]
```
